# Optimizing a Trainium2 kernel written in Bass

```python
import numpy as np
import jax
import jax.numpy as jnp

def _softmax(x, axis=-1):
    return jax.nn.softmax(x, axis=axis)

def _gelu(x):
    return jax.nn.gelu(x, approximate=True)

def _silu(x):
    return jax.nn.silu(x)

def _sigmoid(x):
    return jax.nn.sigmoid(x)

def _layernorm(x, axis=-1, eps=1e-05):
    m = jnp.mean(x, axis=axis, keepdims=True)
    v = jnp.var(x, axis=axis, keepdims=True)
    return (x - m) / jnp.sqrt(v + eps)

def _scatter_add(tgt, idx, src, axis=0):
    return tgt.at[idx].add(src)

def _segment_sum(src, seg, n):
    return jax.ops.segment_sum(src, seg, n)
kernel_name = 'mk_audio_tower_d4_tok_audfeat512_r4_8f405a'

def setup_inputs(seed: int=0):
    np.random.seed(seed)
    _w = jnp.asarray

    def _rec_inputs():
        import jax
        import jax.numpy as jnp
        _rk = jax.random.key(seed)
        x = -0.000153849 + 1.00027 * jax.random.normal(jax.random.fold_in(_rk, 1), (64, 250, 24), jnp.float32)
        return x
    x = _rec_inputs()

    def _L0_tok_setup():
        import jax, jax.numpy as jnp
        import numpy as np
        CONTEXT = 5
        DILATION = 1
        BN_EPS = 1e-05
        key = jax.random.key(seed)
        k1, k2 = jax.random.split(key)
        B, T, D = (64, 1024, 24)
        OUT = 128
        x = jax.random.normal(k1, (B, T, D), dtype=jnp.float32)
        W = jax.random.normal(k2, (OUT, CONTEXT * D), dtype=jnp.float32) * 0.05
        b = jnp.zeros((OUT,), dtype=jnp.float32)
        gamma = jnp.ones((OUT,), dtype=jnp.float32)
        beta = jnp.zeros((OUT,), dtype=jnp.float32)
        return {'x': x, 'W': W, 'b': b, 'gamma': gamma, 'beta': beta}
    _L0_tok_all = _L0_tok_setup()
    _L0_tok_in = {k: v for k, v in _L0_tok_all.items() if k in ('W', 'b', 'gamma', 'beta')}
    del _L0_tok_all

    def _L0_attn_setup():
        import math
        import jax, jax.numpy as jnp
        import numpy as np
        H, N, L_MAX = (128, 64, 512)
        BATCH = 8

        def _s4_forward(u, Lambda_re, Lambda_im, P, B, C, D, log_step):
            L = u.shape[1]
            Lam = jnp.minimum(Lambda_re, -0.0001) + 1j * Lambda_im
            Pc = P[..., 0] + 1j * P[..., 1]
            Bc = B[..., 0] + 1j * B[..., 1]
            Cc = C[..., 0] + 1j * C[..., 1]
            step = jnp.exp(log_step)[:, None]
            Omega = jnp.exp(jnp.arange(L) * (-2j * jnp.pi / L)).astype(jnp.complex64)
            g = 2.0 / step * ((1.0 - Omega) / (1.0 + Omega))
            c_scale = 2.0 / (1.0 + Omega)
            rec = 1.0 / (g[:, :, None] - Lam[:, None, :])

            def cau(v):
                return jnp.einsum('hn,hln->hl', v, rec)
            a0, a1 = (jnp.conj(Cc), jnp.conj(Pc))
            b0, b1 = (Bc, Pc)
            k00 = cau(a0 * b0)
            k01 = cau(a0 * b1)
            k10 = cau(a1 * b0)
            k11 = cau(a1 * b1)
            at_roots = c_scale[None, :] * (k00 - k01 * k10 / (1.0 + k11))
            K = jnp.fft.ifft(at_roots, n=L, axis=1).real.astype(u.dtype)
            fft_size = 2 * L
            U = jnp.fft.rfft(u, n=fft_size, axis=1)
            Kf = jnp.fft.rfft(K, n=fft_size, axis=1)
            Y = jnp.fft.irfft(U * Kf.T[None, :, :], n=fft_size, axis=1)[:, :L, :]
            return Y.astype(u.dtype) + u * D[None, None, :]
        key = jax.random.key(seed)
        ks = jax.random.split(key, 8)
        u = jax.random.normal(ks[0], (BATCH, L_MAX, H), dtype=jnp.float32)
        Lambda_re = -(jax.random.uniform(ks[1], (H, N), dtype=jnp.float32) * 0.5 + 0.05)
        Lambda_im = jax.random.normal(ks[2], (H, N), dtype=jnp.float32) * 3.0
        P = jax.random.normal(ks[3], (H, N, 2), dtype=jnp.float32)
        B = jax.random.normal(ks[4], (H, N, 2), dtype=jnp.float32)
        C = jax.random.normal(ks[5], (H, N, 2), dtype=jnp.float32) * 0.5 ** 0.5
        D = jnp.ones((H,), dtype=jnp.float32)
        log_step = jax.random.uniform(ks[6], (H,), dtype=jnp.float32) * (math.log(0.1) - math.log(0.001)) + math.log(0.001)
        return {'u': u, 'Lambda_re': Lambda_re, 'Lambda_im': Lambda_im, 'P': P, 'B': B, 'C': C, 'D': D, 'log_step': log_step}
    _L0_attn_all = _L0_attn_setup()
    _L0_attn_in = {k: v for k, v in _L0_attn_all.items() if k in ('Lambda_re', 'Lambda_im', 'P', 'B', 'C', 'D', 'log_step')}
    del _L0_attn_all

    def _L0_ffn_setup():
        import jax, jax.numpy as jnp
        import numpy as np
        NUM_EXPERTS = 32
        GROUP_SIZE = 4
        NUM_GROUPS = NUM_EXPERTS // GROUP_SIZE
        C_CAP = 1.0
        key = jax.random.key(seed)
        ks = jax.random.split(key, 5)
        B, S, H = (16, 512, 128)
        D_FF = int(H * 4 * (2.0 / 3.0))
        x = jax.random.normal(ks[0], (B, S, H), dtype=jnp.float32)
        W_router = jax.random.normal(ks[1], (H, NUM_EXPERTS), dtype=jnp.float32) * (1.0 / np.sqrt(H))
        b_router = jnp.zeros((NUM_EXPERTS,), dtype=jnp.float32)
        W_up = jax.random.normal(ks[2], (NUM_GROUPS, H, D_FF), dtype=jnp.float32) * (1.0 / np.sqrt(H))
        b_up = jnp.zeros((NUM_GROUPS, D_FF), dtype=jnp.float32)
        W_down = jax.random.normal(ks[3], (NUM_EXPERTS, D_FF, H), dtype=jnp.float32) * (1.0 / np.sqrt(D_FF))
        b_down = jnp.zeros((NUM_EXPERTS, H), dtype=jnp.float32)
        return {'x': x, 'W_router': W_router, 'b_router': b_router, 'W_up': W_up, 'b_up': b_up, 'W_down': W_down, 'b_down': b_down}
    _L0_ffn_all = _L0_ffn_setup()
    _L0_ffn_in = {k: v for k, v in _L0_ffn_all.items() if k in ('W_router', 'b_router', 'W_up', 'b_up', 'W_down', 'b_down')}
    del _L0_ffn_all

    def _L1_attn_setup():
        import jax, jax.numpy as jnp
        import numpy as np
        B, T, D, H = (4, 256, 128, 8)
        HD = D // H
        key = jax.random.key(seed)
        ks = jax.random.split(key, 32)
        sc = 0.02
        w = lambda k, s: jax.random.normal(k, s, jnp.float32) * sc
        theta = 1.0 / 10000.0 ** (2.0 * jnp.arange(H, dtype=jnp.float32) / H)
        return {'x': jax.random.normal(ks[0], (B, T, D), jnp.float32), 'li_Win': w(ks[1], (D, D)), 'li_Wrec': w(ks[2], (D, D)), 'li_tau': jnp.full((D,), 1.1, jnp.float32), 'li_b': jnp.zeros((D,), jnp.float32), 'li_Wout': w(ks[3], (D, D)), 're_Wq': w(ks[4], (D, D)), 're_Wk': w(ks[5], (D, D)), 're_Wv': w(ks[6], (D, D)), 're_Wo': w(ks[7], (D, D)), 're_bo': jnp.zeros((D,), jnp.float32), 're_theta': theta, 're_gnw': jnp.ones((D,), jnp.float32), 're_gnb': jnp.zeros((D,), jnp.float32), 'la_Wq': w(ks[8], (D, D)), 'la_bq': jnp.zeros((D,), jnp.float32), 'la_Wk': w(ks[9], (D, D)), 'la_bk': jnp.zeros((D,), jnp.float32), 'la_Wv': w(ks[10], (D, D)), 'la_bv': jnp.zeros((D,), jnp.float32), 'la_Wo': w(ks[11], (D, D)), 'la_bo': jnp.zeros((D,), jnp.float32), 'rt_W1': w(ks[12], (D // 4, D)), 'rt_b1': jnp.zeros((D // 4,), jnp.float32), 'rt_W2': w(ks[13], (3, D // 4)), 'rt_b2': jnp.zeros((3,), jnp.float32), 'fusion_w': jnp.ones((3,), jnp.float32), 'ln_w': jnp.ones((D,), jnp.float32), 'ln_b': jnp.zeros((D,), jnp.float32)}
    _L1_attn_all = _L1_attn_setup()
    _L1_attn_in = {k: v for k, v in _L1_attn_all.items() if k in ('li_Win', 'li_Wrec', 'li_tau', 'li_b', 'li_Wout', 're_Wq', 're_Wk', 're_Wv', 're_Wo', 're_bo', 're_theta', 're_gnw', 're_gnb', 'la_Wq', 'la_bq', 'la_Wk', 'la_bk', 'la_Wv', 'la_bv', 'la_Wo', 'la_bo', 'rt_W1', 'rt_b1', 'rt_W2', 'rt_b2', 'fusion_w', 'ln_w', 'ln_b')}
    del _L1_attn_all

    def _L1_ffn_setup():
        import jax, jax.numpy as jnp
        import numpy as np
        D, H, E, B, S = (128, 512, 16, 8, 2048)
        MAX_GROUP_SIZE = 1024
        MIN_CAPACITY = 8
        CAPACITY_FACTOR = 1.0

        def _group_dims(num_tokens, num_experts):
            num_groups = -(-num_tokens // MAX_GROUP_SIZE)
            while num_tokens % num_groups != 0 or num_groups % num_experts != 0:
                num_groups += 1
            return (num_tokens // num_groups, num_groups)
        key = jax.random.key(seed)
        ks = jax.random.split(key, 6)
        s = 0.02
        return {'x': jax.random.normal(ks[0], (B, S, D), jnp.float32), 'gate_w': jax.random.normal(ks[1], (D, E), jnp.float32) * s, 'w1': jax.random.normal(ks[2], (E, D, H), jnp.float32) * s, 'b1': jnp.zeros((E, H), jnp.float32), 'w2': jax.random.normal(ks[3], (E, H, D), jnp.float32) * s, 'b2': jnp.zeros((E, D), jnp.float32), 'sw1': jax.random.normal(ks[4], (D, H), jnp.float32) * s, 'sb1': jnp.zeros((H,), jnp.float32), 'sw2': jax.random.normal(ks[5], (H, D), jnp.float32) * s, 'sb2': jnp.zeros((D,), jnp.float32)}
    _L1_ffn_all = _L1_ffn_setup()
    _L1_ffn_in = {k: v for k, v in _L1_ffn_all.items() if k in ('gate_w', 'w1', 'b1', 'w2', 'b2', 'sw1', 'sb1', 'sw2', 'sb2')}
    del _L1_ffn_all

    def _L2_attn_setup():
        import jax, jax.numpy as jnp
        import numpy as np
        S, B, H, D, IN = (128, 8, 8, 64, 128)
        PROJ = H * (5 * D + 2)
        key = jax.random.key(seed)
        k0, k1, k2 = jax.random.split(key, 3)
        x = jax.random.normal(k0, (S, B, IN), jnp.float32)
        W_slow = jax.random.normal(k1, (PROJ, IN), jnp.float32) / np.sqrt(IN).astype(np.float32)
        W_out = jax.random.normal(k2, (IN, H * D), jnp.float32) / np.sqrt(H * D).astype(np.float32)
        ln_gamma = jnp.ones((IN,), jnp.float32)
        ln_beta = jnp.zeros((IN,), jnp.float32)
        return dict(x=x, W_slow=W_slow, W_out=W_out, ln_gamma=ln_gamma, ln_beta=ln_beta)
    _L2_attn_all = _L2_attn_setup()
    _L2_attn_in = {k: v for k, v in _L2_attn_all.items() if k in ('W_slow', 'W_out', 'ln_gamma', 'ln_beta')}
    del _L2_attn_all

    def _L2_ffn_setup():
        import jax, jax.numpy as jnp
        import numpy as np
        B, L, H, E, F, C = (8, 2048, 128, 8, 256, 2)
        key = jax.random.key(seed)
        ks = jax.random.split(key, 4)
        x = jax.random.normal(ks[0], (B, L, H), jnp.float32)
        Wg = jax.random.normal(ks[1], (H, E), jnp.float32) * H ** (-0.5)
        W1 = jax.random.normal(ks[2], (E, H, F), jnp.float32) * H ** (-0.5)
        b1 = jnp.zeros((E, F), jnp.float32)
        W2 = jax.random.normal(ks[3], (E, F, H), jnp.float32) * F ** (-0.5)
        b2 = jnp.zeros((E, H), jnp.float32)
        return {'x': x, 'Wg': Wg, 'W1': W1, 'b1': b1, 'W2': W2, 'b2': b2}
    _L2_ffn_all = _L2_ffn_setup()
    _L2_ffn_in = {k: v for k, v in _L2_ffn_all.items() if k in ('Wg', 'W1', 'b1', 'W2', 'b2')}
    del _L2_ffn_all

    def _L3_attn_setup():
        import jax, jax.numpy as jnp
        import numpy as np
        H_HEADS = 8
        HIDDEN = 128
        D_K = HIDDEN // H_HEADS

        def rel_shift(x):
            B, H, T, P = x.shape
            x = jnp.pad(x, ((0, 0), (0, 0), (0, 0), (1, 0)))
            x = x.reshape(B, H, P + 1, T)[:, :, 1:, :]
            return x.reshape(B, H, T, P)
        key = jax.random.key(seed)
        ks = jax.random.split(key, 16)
        B, T = (4, 256)
        P = 2 * T - 1
        s = 0.02
        inp = {'x': jax.random.normal(ks[0], (B, T, HIDDEN), dtype=jnp.float32), 'pos_emb': jax.random.normal(ks[1], (1, P, HIDDEN), dtype=jnp.float32), 'Wq': jax.random.normal(ks[2], (HIDDEN, HIDDEN), dtype=jnp.float32) * s, 'bq': jnp.zeros((HIDDEN,), dtype=jnp.float32), 'Wk': jax.random.normal(ks[3], (HIDDEN, HIDDEN), dtype=jnp.float32) * s, 'bk': jnp.zeros((HIDDEN,), dtype=jnp.float32), 'Wv': jax.random.normal(ks[4], (HIDDEN, HIDDEN), dtype=jnp.float32) * s, 'bv': jnp.zeros((HIDDEN,), dtype=jnp.float32), 'Wp': jax.random.normal(ks[5], (HIDDEN, HIDDEN), dtype=jnp.float32) * s, 'bp': jnp.zeros((HIDDEN,), dtype=jnp.float32), 'Wo': jax.random.normal(ks[6], (HIDDEN, HIDDEN), dtype=jnp.float32) * s, 'bo': jnp.zeros((HIDDEN,), dtype=jnp.float32), 'pos_bias_u': jax.random.normal(ks[7], (H_HEADS, D_K), dtype=jnp.float32) * s, 'pos_bias_v': jax.random.normal(ks[8], (H_HEADS, D_K), dtype=jnp.float32) * s}
        return inp
    _L3_attn_all = _L3_attn_setup()
    _L3_attn_in = {k: v for k, v in _L3_attn_all.items() if k in ('pos_emb', 'Wq', 'bq', 'Wk', 'bk', 'Wv', 'bv', 'Wp', 'bp', 'Wo', 'bo', 'pos_bias_u', 'pos_bias_v')}
    del _L3_attn_all

    def _L3_ffn_setup():
        import jax, jax.numpy as jnp
        import numpy as np
        B, S, D, E, O = (256, 64, 128, 16, 128)
        key = jax.random.key(seed)
        k_x, k_wg, k_bg, k_we, k_be = jax.random.split(key, 5)
        scale_g = 1.0 / np.sqrt(D)
        scale_e = 1.0 / np.sqrt(D)
        return {'x': jax.random.normal(k_x, (B, S, D), dtype=jnp.float32), 'Wg': jax.random.uniform(k_wg, (D, E), jnp.float32, -scale_g, scale_g), 'bg': jax.random.uniform(k_bg, (E,), jnp.float32, -scale_g, scale_g), 'We': jax.random.uniform(k_we, (E, D, O), jnp.float32, -scale_e, scale_e), 'be': jax.random.uniform(k_be, (E, O), jnp.float32, -scale_e, scale_e)}
    _L3_ffn_all = _L3_ffn_setup()
    _L3_ffn_in = {k: v for k, v in _L3_ffn_all.items() if k in ('Wg', 'bg', 'We', 'be')}
    del _L3_ffn_all
    return {'x': x, 'L0_tok_W': _L0_tok_in['W'], 'L0_tok_b': _L0_tok_in['b'], 'L0_tok_gamma': _L0_tok_in['gamma'], 'L0_tok_beta': _L0_tok_in['beta'], 'L0_attn_Lambda_re': _L0_attn_in['Lambda_re'], 'L0_attn_Lambda_im': _L0_attn_in['Lambda_im'], 'L0_attn_P': _L0_attn_in['P'], 'L0_attn_B': _L0_attn_in['B'], 'L0_attn_C': _L0_attn_in['C'], 'L0_attn_D': _L0_attn_in['D'], 'L0_attn_log_step': _L0_attn_in['log_step'], 'L0_ffn_W_router': _L0_ffn_in['W_router'], 'L0_ffn_b_router': _L0_ffn_in['b_router'], 'L0_ffn_W_up': _L0_ffn_in['W_up'], 'L0_ffn_b_up': _L0_ffn_in['b_up'], 'L0_ffn_W_down': _L0_ffn_in['W_down'], 'L0_ffn_b_down': _L0_ffn_in['b_down'], 'L1_attn_li_Win': _L1_attn_in['li_Win'], 'L1_attn_li_Wrec': _L1_attn_in['li_Wrec'], 'L1_attn_li_tau': _L1_attn_in['li_tau'], 'L1_attn_li_b': _L1_attn_in['li_b'], 'L1_attn_li_Wout': _L1_attn_in['li_Wout'], 'L1_attn_re_Wq': _L1_attn_in['re_Wq'], 'L1_attn_re_Wk': _L1_attn_in['re_Wk'], 'L1_attn_re_Wv': _L1_attn_in['re_Wv'], 'L1_attn_re_Wo': _L1_attn_in['re_Wo'], 'L1_attn_re_bo': _L1_attn_in['re_bo'], 'L1_attn_re_theta': _L1_attn_in['re_theta'], 'L1_attn_re_gnw': _L1_attn_in['re_gnw'], 'L1_attn_re_gnb': _L1_attn_in['re_gnb'], 'L1_attn_la_Wq': _L1_attn_in['la_Wq'], 'L1_attn_la_bq': _L1_attn_in['la_bq'], 'L1_attn_la_Wk': _L1_attn_in['la_Wk'], 'L1_attn_la_bk': _L1_attn_in['la_bk'], 'L1_attn_la_Wv': _L1_attn_in['la_Wv'], 'L1_attn_la_bv': _L1_attn_in['la_bv'], 'L1_attn_la_Wo': _L1_attn_in['la_Wo'], 'L1_attn_la_bo': _L1_attn_in['la_bo'], 'L1_attn_rt_W1': _L1_attn_in['rt_W1'], 'L1_attn_rt_b1': _L1_attn_in['rt_b1'], 'L1_attn_rt_W2': _L1_attn_in['rt_W2'], 'L1_attn_rt_b2': _L1_attn_in['rt_b2'], 'L1_attn_fusion_w': _L1_attn_in['fusion_w'], 'L1_attn_ln_w': _L1_attn_in['ln_w'], 'L1_attn_ln_b': _L1_attn_in['ln_b'], 'L1_ffn_gate_w': _L1_ffn_in['gate_w'], 'L1_ffn_w1': _L1_ffn_in['w1'], 'L1_ffn_b1': _L1_ffn_in['b1'], 'L1_ffn_w2': _L1_ffn_in['w2'], 'L1_ffn_b2': _L1_ffn_in['b2'], 'L1_ffn_sw1': _L1_ffn_in['sw1'], 'L1_ffn_sb1': _L1_ffn_in['sb1'], 'L1_ffn_sw2': _L1_ffn_in['sw2'], 'L1_ffn_sb2': _L1_ffn_in['sb2'], 'L2_attn_W_slow': _L2_attn_in['W_slow'], 'L2_attn_W_out': _L2_attn_in['W_out'], 'L2_attn_ln_gamma': _L2_attn_in['ln_gamma'], 'L2_attn_ln_beta': _L2_attn_in['ln_beta'], 'L2_ffn_Wg': _L2_ffn_in['Wg'], 'L2_ffn_W1': _L2_ffn_in['W1'], 'L2_ffn_b1': _L2_ffn_in['b1'], 'L2_ffn_W2': _L2_ffn_in['W2'], 'L2_ffn_b2': _L2_ffn_in['b2'], 'L3_attn_pos_emb': _L3_attn_in['pos_emb'], 'L3_attn_Wq': _L3_attn_in['Wq'], 'L3_attn_bq': _L3_attn_in['bq'], 'L3_attn_Wk': _L3_attn_in['Wk'], 'L3_attn_bk': _L3_attn_in['bk'], 'L3_attn_Wv': _L3_attn_in['Wv'], 'L3_attn_bv': _L3_attn_in['bv'], 'L3_attn_Wp': _L3_attn_in['Wp'], 'L3_attn_bp': _L3_attn_in['bp'], 'L3_attn_Wo': _L3_attn_in['Wo'], 'L3_attn_bo': _L3_attn_in['bo'], 'L3_attn_pos_bias_u': _L3_attn_in['pos_bias_u'], 'L3_attn_pos_bias_v': _L3_attn_in['pos_bias_v'], 'L3_ffn_Wg': _L3_ffn_in['Wg'], 'L3_ffn_bg': _L3_ffn_in['bg'], 'L3_ffn_We': _L3_ffn_in['We'], 'L3_ffn_be': _L3_ffn_in['be']}

def reference(x, L0_tok_W, L0_tok_b, L0_tok_gamma, L0_tok_beta, L0_attn_Lambda_re, L0_attn_Lambda_im, L0_attn_P, L0_attn_B, L0_attn_C, L0_attn_D, L0_attn_log_step, L0_ffn_W_router, L0_ffn_b_router, L0_ffn_W_up, L0_ffn_b_up, L0_ffn_W_down, L0_ffn_b_down, L1_attn_li_Win, L1_attn_li_Wrec, L1_attn_li_tau, L1_attn_li_b, L1_attn_li_Wout, L1_attn_re_Wq, L1_attn_re_Wk, L1_attn_re_Wv, L1_attn_re_Wo, L1_attn_re_bo, L1_attn_re_theta, L1_attn_re_gnw, L1_attn_re_gnb, L1_attn_la_Wq, L1_attn_la_bq, L1_attn_la_Wk, L1_attn_la_bk, L1_attn_la_Wv, L1_attn_la_bv, L1_attn_la_Wo, L1_attn_la_bo, L1_attn_rt_W1, L1_attn_rt_b1, L1_attn_rt_W2, L1_attn_rt_b2, L1_attn_fusion_w, L1_attn_ln_w, L1_attn_ln_b, L1_ffn_gate_w, L1_ffn_w1, L1_ffn_b1, L1_ffn_w2, L1_ffn_b2, L1_ffn_sw1, L1_ffn_sb1, L1_ffn_sw2, L1_ffn_sb2, L2_attn_W_slow, L2_attn_W_out, L2_attn_ln_gamma, L2_attn_ln_beta, L2_ffn_Wg, L2_ffn_W1, L2_ffn_b1, L2_ffn_W2, L2_ffn_b2, L3_attn_pos_emb, L3_attn_Wq, L3_attn_bq, L3_attn_Wk, L3_attn_bk, L3_attn_Wv, L3_attn_bv, L3_attn_Wp, L3_attn_bp, L3_attn_Wo, L3_attn_bo, L3_attn_pos_bias_u, L3_attn_pos_bias_v, L3_ffn_Wg, L3_ffn_bg, L3_ffn_We, L3_ffn_be):
    import jax
    import jax.numpy as jnp

    def _L0_tok_ref(x, W, b, gamma, beta):
        import jax, jax.numpy as jnp
        import numpy as np
        CONTEXT = 5
        DILATION = 1
        BN_EPS = 1e-05
        B, T, D = x.shape
        Tp = T - DILATION * (CONTEXT - 1)
        frames = jnp.concatenate([x[:, i * DILATION:i * DILATION + Tp, :] for i in range(CONTEXT)], axis=-1)
        h = jax.nn.relu(jnp.einsum('btf,of->bto', frames, W) + b)
        mean = jnp.mean(h, axis=(0, 1))
        var = jnp.mean(jnp.square(h - mean), axis=(0, 1))
        y = gamma * (h - mean) * jax.lax.rsqrt(var + BN_EPS) + beta
        return y

    def _L0_attn_ref(u, Lambda_re, Lambda_im, P, B, C, D, log_step):
        import math
        import jax, jax.numpy as jnp
        import numpy as np
        H, N, L_MAX = (128, 64, 512)
        BATCH = 8

        def _s4_forward(u, Lambda_re, Lambda_im, P, B, C, D, log_step):
            L = u.shape[1]
            Lam = jnp.minimum(Lambda_re, -0.0001) + 1j * Lambda_im
            Pc = P[..., 0] + 1j * P[..., 1]
            Bc = B[..., 0] + 1j * B[..., 1]
            Cc = C[..., 0] + 1j * C[..., 1]
            step = jnp.exp(log_step)[:, None]
            Omega = jnp.exp(jnp.arange(L) * (-2j * jnp.pi / L)).astype(jnp.complex64)
            g = 2.0 / step * ((1.0 - Omega) / (1.0 + Omega))
            c_scale = 2.0 / (1.0 + Omega)
            rec = 1.0 / (g[:, :, None] - Lam[:, None, :])

            def cau(v):
                return jnp.einsum('hn,hln->hl', v, rec)
            a0, a1 = (jnp.conj(Cc), jnp.conj(Pc))
            b0, b1 = (Bc, Pc)
            k00 = cau(a0 * b0)
            k01 = cau(a0 * b1)
            k10 = cau(a1 * b0)
            k11 = cau(a1 * b1)
            at_roots = c_scale[None, :] * (k00 - k01 * k10 / (1.0 + k11))
            K = jnp.fft.ifft(at_roots, n=L, axis=1).real.astype(u.dtype)
            fft_size = 2 * L
            U = jnp.fft.rfft(u, n=fft_size, axis=1)
            Kf = jnp.fft.rfft(K, n=fft_size, axis=1)
            Y = jnp.fft.irfft(U * Kf.T[None, :, :], n=fft_size, axis=1)[:, :L, :]
            return Y.astype(u.dtype) + u * D[None, None, :]
        return _s4_forward(u, Lambda_re, Lambda_im, P, B, C, D, log_step)

    def _L0_ffn_ref(x, W_router, b_router, W_up, b_up, W_down, b_down):
        import jax, jax.numpy as jnp
        import numpy as np
        NUM_EXPERTS = 32
        GROUP_SIZE = 4
        NUM_GROUPS = NUM_EXPERTS // GROUP_SIZE
        C_CAP = 1.0
        B, S, H = x.shape
        bs = B * S
        E = NUM_EXPERTS
        k = min(int(bs * C_CAP) // E, bs)
        xf = x.reshape(bs, H)
        h = xf @ W_router + b_router
        Sm = jax.nn.softmax(h, axis=-1)
        G_ek, idx_ek = jax.lax.top_k(Sm.T, k)
        tokens = xf[idx_ek]
        D_FF = W_up.shape[-1]
        tok_g = tokens.reshape(NUM_GROUPS, GROUP_SIZE, k, H)
        up = jnp.einsum('gjkh,ghf->gjkf', tok_g, W_up) + b_up[:, None, None, :]
        act = jax.nn.silu(up).reshape(E, k, D_FF)
        Eout = jnp.einsum('ekf,efh->ekh', act, W_down) + b_down[:, None, :]
        weighted = G_ek[..., None] * Eout
        y = jnp.zeros((bs, H), dtype=x.dtype).at[idx_ek.reshape(-1)].add(weighted.reshape(-1, H))
        return y.reshape(B, S, H)

    def _L1_attn_ref(x, li_Win, li_Wrec, li_tau, li_b, li_Wout, re_Wq, re_Wk, re_Wv, re_Wo, re_bo, re_theta, re_gnw, re_gnb, la_Wq, la_bq, la_Wk, la_bk, la_Wv, la_bv, la_Wo, la_bo, rt_W1, rt_b1, rt_W2, rt_b2, fusion_w, ln_w, ln_b):
        import jax, jax.numpy as jnp
        import numpy as np
        B, T, D, H = (4, 256, 128, 8)
        HD = D // H
        Bn, Tn, Dm = x.shape
        Hn = H
        hd = Dm // Hn
        dt = 0.1
        eps = 1e-05

        def lstep(h, xt):
            s = xt @ li_Win.T
            r = h @ li_Wrec.T
            tau = jax.nn.softplus(li_tau + 0.1 * jnp.mean(jnp.abs(s), axis=0))
            a = jnp.tanh(s + r + li_b)
            h = h + dt * (-h / tau[None, :] + a)
            return (h, h @ li_Wout.T)
        h0 = jnp.zeros((Bn, Dm), x.dtype)
        _, liq = jax.lax.scan(lstep, h0, jnp.swapaxes(x, 0, 1))
        liquid_out = jnp.swapaxes(liq, 0, 1)
        q = (x @ re_Wq.T).reshape(Bn, Tn, Hn, hd)
        k = (x @ re_Wk.T).reshape(Bn, Tn, Hn, hd)
        v = (x @ re_Wv.T).reshape(Bn, Tn, Hn, hd)
        idx = jnp.arange(Tn)
        diff = (idx[:, None] - idx[None, :]).astype(x.dtype)
        causal = idx[:, None] >= idx[None, :]
        dm = jnp.mean(jnp.exp(-re_theta[:, None, None] * diff), axis=0)
        dm = jnp.where(causal, dm, 0.0)
        scores = jnp.einsum('bthd,bshd->bths', q, k) / jnp.sqrt(jnp.asarray(hd, x.dtype))
        scores = scores * dm[None, :, None, :]
        scores = jnp.where(causal[None, :, None, :], scores, -jnp.inf)
        ret = jax.nn.softmax(scores, axis=-1)
        r_out = jnp.einsum('bths,bshd->bthd', ret, v)
        mu = r_out.mean(-1, keepdims=True)
        var = r_out.var(-1, keepdims=True)
        g = (r_out - mu) / jnp.sqrt(var + eps)
        r_out = g.reshape(Bn, Tn, Dm) * re_gnw + re_gnb
        retentive_out = r_out @ re_Wo.T + re_bo
        fm = lambda z: jax.nn.elu(z) + 1.0
        q2 = fm((x @ la_Wq.T + la_bq).reshape(Bn, Tn, Hn, hd))
        k2 = fm((x @ la_Wk.T + la_bk).reshape(Bn, Tn, Hn, hd))
        v2 = (x @ la_Wv.T + la_bv).reshape(Bn, Tn, Hn, hd)
        kv = jnp.einsum('bthd,bthe->bhde', k2, v2)
        ksum = k2.sum(axis=1)
        num = jnp.einsum('bthd,bhde->bthe', q2, kv)
        den = jnp.einsum('bthd,bhd->bth', q2, ksum)[..., None] + 1e-08
        linear_out = (num / den).reshape(Bn, Tn, Dm) @ la_Wo.T + la_bo
        stats = x.mean(axis=1)
        rw = jax.nn.softmax(jax.nn.relu(stats @ rt_W1.T + rt_b1) @ rt_W2.T + rt_b2, axis=-1)
        fw = jax.nn.softmax(fusion_w)
        wgt = rw * fw[None, :]
        fused = wgt[:, 0, None, None] * liquid_out + wgt[:, 1, None, None] * retentive_out + wgt[:, 2, None, None] * linear_out
        mu = fused.mean(-1, keepdims=True)
        var = fused.var(-1, keepdims=True)
        out = (fused - mu) / jnp.sqrt(var + eps) * ln_w + ln_b
        return out

    def _L1_ffn_ref(x, gate_w, w1, b1, w2, b2, sw1, sb1, sw2, sb2):
        import jax, jax.numpy as jnp
        import numpy as np
        D, H, E, B, S = (128, 512, 16, 8, 2048)
        MAX_GROUP_SIZE = 1024
        MIN_CAPACITY = 8
        CAPACITY_FACTOR = 1.0

        def _group_dims(num_tokens, num_experts):
            num_groups = -(-num_tokens // MAX_GROUP_SIZE)
            while num_tokens % num_groups != 0 or num_groups % num_experts != 0:
                num_groups += 1
            return (num_tokens // num_groups, num_groups)
        Bn, Sn, Dn = x.shape
        En = gate_w.shape[1]
        T = Bn * Sn
        group_size, num_groups = _group_dims(T, En)
        cap = max(int(round(CAPACITY_FACTOR * group_size * num_groups / En)), MIN_CAPACITY)
        xg = x.reshape(num_groups, group_size, Dn)
        logits = jnp.einsum('gsd,de->gse', xg, gate_w)
        probs = jax.nn.softmax(logits, axis=-1)
        flat_probs = probs.transpose(2, 0, 1).reshape(En, T)
        scores, tok_idx = jax.lax.top_k(flat_probs, cap)
        xf = x.reshape(T, Dn)
        toks = xf[tok_idx]
        h = jax.nn.gelu(jnp.einsum('ecd,edh->ech', toks, w1) + b1[:, None, :])
        y = jnp.einsum('ech,ehd->ecd', h, w2) + b2[:, None, :]
        y = y * scores[..., None]
        routed = jnp.zeros_like(xf).at[tok_idx.reshape(-1)].add(y.reshape(-1, Dn))
        shared = jax.nn.gelu(xf @ sw1 + sb1) @ sw2 + sb2
        out = (routed + shared).reshape(Bn, Sn, Dn)
        return out

    def _L2_attn_ref(x, W_slow, W_out, ln_gamma, ln_beta):
        import jax, jax.numpy as jnp
        import numpy as np
        S, B, H, D, IN = (128, 8, 8, 64, 128)
        PROJ = H * (5 * D + 2)
        slen, bsz, in_dim = x.shape
        mu = x.mean(-1, keepdims=True)
        var = x.var(-1, keepdims=True)
        normed = (x - mu) / jnp.sqrt(var + 1e-05) * ln_gamma + ln_beta
        qkvb = (normed @ W_slow.T).reshape(slen, bsz, H, 5 * D + 2)
        q, k, v, rk, rv, beta, rbeta = jnp.split(qkvb, [D, 2 * D, 3 * D, 4 * D, 5 * D, 5 * D + 1], axis=-1)
        q = jax.nn.softmax(q, axis=-1)
        k = jax.nn.softmax(k, axis=-1)
        rk = jax.nn.softmax(rk, axis=-1)
        beta = jax.nn.sigmoid(beta)
        rbeta = jax.nn.sigmoid(rbeta)
        W0 = jnp.zeros((bsz, H, D, D), x.dtype)

        def fw_step(W, inp):
            qt, kt, vt, bt = inp
            v_old = jnp.einsum('bhij,bhj->bhi', W, kt)
            W = W + (bt * (vt - v_old))[..., :, None] * kt[..., None, :]
            z = jnp.einsum('bhij,bhj->bhi', W, qt)
            return (W, z)
        _, z = jax.lax.scan(fw_step, W0, (q, k, v, beta))
        R0 = jnp.zeros((bsz, H, D, D), x.dtype)
        h0 = jnp.zeros((bsz, H, D), x.dtype)

        def rec_step(carry, inp):
            R, h = carry
            zt, kt, vt, bt = inp
            qh = jax.nn.softmax(h, axis=-1)
            v_old = jnp.einsum('bhij,bhj->bhi', R, kt)
            R = R + (bt * (vt - v_old))[..., :, None] * kt[..., None, :]
            h = zt + jnp.einsum('bhij,bhj->bhi', R, qh)
            return ((R, h), h)
        _, hs = jax.lax.scan(rec_step, (R0, h0), (z, rk, rv, rbeta))
        out = hs.reshape(slen, bsz, H * D) @ W_out.T
        return x + out

    def _L2_ffn_ref(x, Wg, W1, b1, W2, b2):
        import jax, jax.numpy as jnp
        import numpy as np
        B, L, H, E, F, C = (8, 2048, 128, 8, 256, 2)
        b, l, h = x.shape
        e = Wg.shape[1]
        k = min(max(int(l * C / e), 1), l)
        S = jax.nn.softmax(x @ Wg, axis=-1)
        St = jnp.swapaxes(S, 1, 2)
        G, I = jax.lax.top_k(St, k)
        ex = jnp.take_along_axis(x[:, None], I[..., None], axis=2)
        hmid = jax.nn.gelu(jnp.einsum('bekh,ehf->bekf', ex, W1) + b1[None, :, None, :], approximate=False)
        out = jnp.einsum('bekf,efh->bekh', hmid, W2) + b2[None, :, None, :]
        vals = G[..., None] * out
        new_x = jnp.zeros_like(x).at[jnp.arange(b)[:, None, None], I].add(vals)
        return new_x

    def _L3_attn_ref(x, pos_emb, Wq, bq, Wk, bk, Wv, bv, Wp, bp, Wo, bo, pos_bias_u, pos_bias_v):
        import jax, jax.numpy as jnp
        import numpy as np
        H_HEADS = 8
        HIDDEN = 128
        D_K = HIDDEN // H_HEADS

        def rel_shift(x):
            B, H, T, P = x.shape
            x = jnp.pad(x, ((0, 0), (0, 0), (0, 0), (1, 0)))
            x = x.reshape(B, H, P + 1, T)[:, :, 1:, :]
            return x.reshape(B, H, T, P)
        B, T, _ = x.shape
        Hh, d = (H_HEADS, D_K)
        scale = 1.0 / jnp.sqrt(jnp.asarray(d, dtype=x.dtype))
        q = (x @ Wq + bq).reshape(B, T, Hh, d)
        k = (x @ Wk + bk).reshape(B, T, Hh, d).transpose(0, 2, 1, 3)
        v = (x @ Wv + bv).reshape(B, T, Hh, d).transpose(0, 2, 1, 3)
        P = pos_emb.shape[1]
        p = (pos_emb @ Wp + bp).reshape(pos_emb.shape[0], P, Hh, d).transpose(0, 2, 1, 3)
        q_u = (q + pos_bias_u).transpose(0, 2, 1, 3)
        q_v = (q + pos_bias_v).transpose(0, 2, 1, 3)
        matrix_bd = jnp.matmul(q_v, p.transpose(0, 1, 3, 2))
        matrix_bd = rel_shift(matrix_bd)[:, :, :, :T] * scale
        scores = jnp.matmul(q_u, k.transpose(0, 1, 3, 2)) * scale + matrix_bd
        attn = jax.nn.softmax(scores.astype(jnp.float32), axis=-1).astype(x.dtype)
        out = jnp.matmul(attn, v)
        out = out.transpose(0, 2, 1, 3).reshape(B, T, Hh * d)
        return out @ Wo + bo

    def _L3_ffn_ref(x, Wg, bg, We, be):
        import jax, jax.numpy as jnp
        import numpy as np
        B, S, D, E, O = (256, 64, 128, 16, 128)
        scores = jax.nn.softmax(jnp.mean(x, axis=1) @ Wg + bg, axis=-1)
        idx = jnp.argmax(scores, axis=-1)
        gate = jnp.take_along_axis(scores, idx[:, None], axis=-1)
        W_sel = We[idx]
        b_sel = be[idx]
        y = jnp.einsum('bsd,bdo->bso', x, W_sel) + b_sel[:, None, :]
        return gate[:, :, None] * y
    h = _L0_tok_ref(x, L0_tok_W, L0_tok_b, L0_tok_gamma, L0_tok_beta)
    h = h + _L0_attn_ref(_layernorm(h, axis=-1), L0_attn_Lambda_re, L0_attn_Lambda_im, L0_attn_P, L0_attn_B, L0_attn_C, L0_attn_D, L0_attn_log_step)
    h = h + _L0_ffn_ref(_layernorm(h, axis=-1), L0_ffn_W_router, L0_ffn_b_router, L0_ffn_W_up, L0_ffn_b_up, L0_ffn_W_down, L0_ffn_b_down)
    h = h + _L1_attn_ref(_layernorm(h, axis=-1), L1_attn_li_Win, L1_attn_li_Wrec, L1_attn_li_tau, L1_attn_li_b, L1_attn_li_Wout, L1_attn_re_Wq, L1_attn_re_Wk, L1_attn_re_Wv, L1_attn_re_Wo, L1_attn_re_bo, L1_attn_re_theta, L1_attn_re_gnw, L1_attn_re_gnb, L1_attn_la_Wq, L1_attn_la_bq, L1_attn_la_Wk, L1_attn_la_bk, L1_attn_la_Wv, L1_attn_la_bv, L1_attn_la_Wo, L1_attn_la_bo, L1_attn_rt_W1, L1_attn_rt_b1, L1_attn_rt_W2, L1_attn_rt_b2, L1_attn_fusion_w, L1_attn_ln_w, L1_attn_ln_b)
    h = h + _L1_ffn_ref(_layernorm(h, axis=-1), L1_ffn_gate_w, L1_ffn_w1, L1_ffn_b1, L1_ffn_w2, L1_ffn_b2, L1_ffn_sw1, L1_ffn_sb1, L1_ffn_sw2, L1_ffn_sb2)
    h = h + _L2_attn_ref(_layernorm(h, axis=-1), L2_attn_W_slow, L2_attn_W_out, L2_attn_ln_gamma, L2_attn_ln_beta)
    h = h + _L2_ffn_ref(_layernorm(h, axis=-1), L2_ffn_Wg, L2_ffn_W1, L2_ffn_b1, L2_ffn_W2, L2_ffn_b2)
    h = h + _L3_attn_ref(_layernorm(h, axis=-1), L3_attn_pos_emb, L3_attn_Wq, L3_attn_bq, L3_attn_Wk, L3_attn_bk, L3_attn_Wv, L3_attn_bv, L3_attn_Wp, L3_attn_bp, L3_attn_Wo, L3_attn_bo, L3_attn_pos_bias_u, L3_attn_pos_bias_v)
    h = h + _L3_ffn_ref(_layernorm(h, axis=-1), L3_ffn_Wg, L3_ffn_bg, L3_ffn_We, L3_ffn_be)
    return h

_drawn_inputs = setup_inputs


def setup_inputs(seed=0):
    import zlib

    import numpy as np

    out = dict(_drawn_inputs(seed))
    spreads = {'L0_tok_b': (0.0, 0.1),
     'L0_tok_gamma': (1.0, 0.2),
     'L0_tok_beta': (0.0, 0.1),
     'L0_attn_D': (1.0, 0.2),
     'L0_ffn_b_router': (0.0, 0.8),
     'L0_ffn_b_up': (0.0, 0.8),
     'L0_ffn_b_down': (0.0, 0.8),
     'L1_attn_li_tau': (1.100000023841858, 0.6),
     'L1_attn_li_b': (0.0, 0.1),
     'L1_attn_re_bo': (0.0, 0.1),
     'L1_attn_re_gnw': (1.0, 0.2),
     'L1_attn_re_gnb': (0.0, 0.335),
     'L1_attn_la_bq': (0.0, 0.8),
     'L1_attn_la_bk': (0.0, 0.8),
     'L1_attn_la_bv': (0.0, 0.1),
     'L1_attn_la_bo': (0.0, 0.1),
     'L1_attn_rt_b1': (0.0, 0.8),
     'L1_attn_rt_b2': (0.0, 0.331),
     'L1_attn_fusion_w': (1.0, 0.541),
     'L1_attn_ln_w': (1.0, 0.2),
     'L1_attn_ln_b': (0.0, 0.1),
     'L1_ffn_b1': (0.0, 0.8),
     'L1_ffn_b2': (0.0, 0.8),
     'L1_ffn_sb1': (0.0, 0.8),
     'L1_ffn_sb2': (0.0, 0.1),
     'L2_attn_ln_gamma': (1.0, 0.6),
     'L2_attn_ln_beta': (0.0, 0.8),
     'L2_ffn_b1': (0.0, 0.8),
     'L2_ffn_b2': (0.0, 0.682),
     'L3_attn_bq': (0.0, 0.8),
     'L3_attn_bk': (0.0, 2.0),
     'L3_attn_bv': (0.0, 0.8),
     'L3_attn_bp': (0.0, 2.0),
     'L3_attn_bo': (0.0, 0.327)}
    factors = {'L1_attn_li_Wrec': 2.733,
     'L1_attn_re_Wq': 8.0,
     'L1_attn_re_Wk': 8.0,
     'L1_attn_re_theta': 64.0,
     'L1_attn_la_Wq': 8.0,
     'L1_attn_la_Wk': 8.0,
     'L1_attn_rt_W1': 8.0,
     'L1_attn_rt_W2': 8.0,
     'L1_ffn_gate_w': 8.0,
     'L1_ffn_w1': 8.0,
     'L1_ffn_w2': 8.0,
     'L1_ffn_sw1': 2.936,
     'L1_ffn_sw2': 2.716,
     'L3_attn_pos_emb': 8.0,
     'L3_attn_Wq': 8.0,
     'L3_attn_Wk': 8.0,
     'L3_attn_Wv': 8.0,
     'L3_attn_Wp': 8.0,
     'L3_attn_Wo': 8.0,
     'L3_attn_pos_bias_u': 8.0,
     'L3_attn_pos_bias_v': 8.0,
     'L3_ffn_Wg': 4.308,
     'L3_ffn_bg': 8.0,
     'L3_ffn_We': 4.159,
     'L3_ffn_be': 23.903}
    for name, (base, spread) in spreads.items():
        noise = np.random.default_rng([zlib.crc32(name.encode()), seed]).standard_normal(out[name].shape)
        drawn = base * np.exp(spread * noise) if base else spread * noise
        out[name] = jnp.asarray(drawn.astype(out[name].dtype))
    for name, factor in factors.items():
        out[name] = (out[name] * factor).astype(out[name].dtype)
    return out
```

```python
import concourse.bass as bass
from concourse import mybir
from contextlib import ExitStack, contextmanager

F32 = mybir.dt.float32
BF16 = mybir.dt.bfloat16
I32 = mybir.dt.int32
U32 = mybir.dt.uint32
ALU = mybir.AluOpType
ACT = mybir.ActivationFunctionType
AX = mybir.AxisListType

B = 64
TIN = 250
DIN = 24
CTX = 5
T = TIN - CTX + 1
HT = T // 2
D = 128
N = B * T
NT = N // HT
NBI = 4
CT = 2 * NBI
EPS = 1e-5


class Chain:

    def __init__(self, eng, sem):
        self.eng, self.sem, self.n = eng, sem, 0

    def __call__(self, ins):
        self.n += 1
        ins.then_inc(self.sem, 1)
        self.eng.wait_ge(self.sem, self.n)


class Stage:

    def __init__(self, nc, name):
        self.nc, self.name = nc, name
        self.ctx = ExitStack()
        self.sems, self.pool_sems = [], []

    def __enter__(self):
        self.ctx.__enter__()
        return self

    def __exit__(self, *a):
        return self.ctx.__exit__(*a)

    def sb(self, name, shape, dt=F32):
        return self.ctx.enter_context(self.nc.sbuf_tensor(f"{self.name}_{name}", shape, dt))

    def ps(self, name, shape, dt=F32):
        return self.ctx.enter_context(self.nc.psum_tensor(f"{self.name}_{name}", shape, dt))

    def sem(self, name):
        s = self.ctx.enter_context(self.nc.semaphore(f"{self.name}_{name}"))
        self.sems.append(s)
        return s

    def pool_sem(self, name):
        s = self.ctx.enter_context(self.nc.semaphore(f"{self.name}_{name}"))
        self.pool_sems.append(s)
        return s

    @contextmanager
    def step(self):
        with self.nc.Block(no_gpsimd_drain=True) as block:
            yield block
        with self.nc.Block(no_gpsimd_drain=True) as block:
            @block.sync
            def _(sp):
                for s in self.sems:
                    sp.sem_clear(s)

            if self.pool_sems:
                @block.gpsimd
                def _(pool):
                    for s in self.pool_sems:
                        pool.dma_reset(range(s.num, s.num + 1))
                        pool.sem_clear(s)


def wide(ap, p=128):
    return bass.AP(ap.tensor, ap.offset, [[0, p]] + [list(x) for x in ap.ap])


def tiles_of(dram):
    return dram.rearrange("(b c p) d -> b p c d", b=B, c=2)


def consts_stage(nc, st, ident):
    ready = st.sem("ident_ready")
    with st.step() as block:
        @block.gpsimd
        def _(pool):
            nc.gpsimd.memset(ident[:], 0.0).then_inc(ready, 1)
            pool.wait_ge(ready, 1)
            nc.gpsimd.affine_select(out=ident[:], in_=ident[:], compare_op=ALU.not_equal, fill=1.0,
                                    base=0, pattern=[[-1, 128]], channel_multiplier=1).then_inc(ready, 1)
            pool.wait_ge(ready, 2)


def tok_stage(nc, c, x, W, b, gamma, beta, h_out):
    K = CTX * DIN
    with Stage(nc, "tok") as st:
        H = st.sb("H", [HT, NT, D])
        wT = st.sb("wT", [K, D])
        wn = st.sb("wn", [D, K])
        brow = st.sb("brow", [1, D])
        ones = st.sb("ones", [HT, D])
        fr = st.sb("fr", [HT, CT, K])
        frT = st.sb("frT", [K, CT, HT])
        tp = [st.ps(f"tp{i}", [K, 4, 128]) for i in range(2)]
        hp = [st.ps(f"hp{i}", [HT, 4, D]) for i in range(2)]
        acc = st.ps("acc", [D, 4 * D])
        sq2 = [st.sb(f"sq{i}", [HT, 4 * D]) for i in range(2)]
        gb = st.sb("gb", [D, 2, D])
        mean = st.sb("mean", [D, D])
        var = st.sb("var", [D, D])
        s_in = st.sem("inputs")
        s_tp = st.sem("transposed")
        s_cp = st.sem("copied")
        s_mm = st.sem("multiplied")
        s_h = st.sem("h_ready")
        s_own = st.sem("own")
        s_out = st.sem("stored")

        with st.step() as block:
            @block.sync
            def _(sp):
                sp.dma_start(wn[:], W[:, :]).then_inc(s_in, 16)
                sp.dma_start(brow[:], b.rearrange("(a d) -> a d", a=1)).then_inc(s_in, 16)
                sp.dma_start(gb[:, 0, :], wide(gamma)).then_inc(s_in, 16)
                sp.dma_start(gb[:, 1, :], wide(beta)).then_inc(s_in, 16)
                sp.wait_ge(s_in, 64)

            @block.vector
            def _(dve):
                nc.vector.memset(ones[:], 1.0).then_inc(s_h, 1)
                dve.wait_ge(s_tp, 1)
                nc.vector.tensor_copy(wT[:], tp[0][:, 0, :]).then_inc(s_h, 1)
                dve.wait_ge(s_h, 2)

            @block.tensor
            def _(pe):
                pe.wait_ge(s_in, 64)
                nc.tensor.transpose(tp[0][:, 0, :], wn[:], c.ident[:]).then_inc(s_tp, 1)

        frames = bass.AP(x.tensor, 0, [[TIN * DIN, B], [DIN, HT], [HT * DIN, 2], [1, K]])
        with nc.Fori(0, B // NBI) as i, st.step() as block:
            @block.sync
            def _(sp):
                for k in range(NBI):
                    sp.dma_start(fr[:, 2 * k:2 * k + 2, :], frames[i * NBI + k]).then_inc(s_in, 16)

            @block.tensor
            def _(pe):
                pe.wait_ge(s_in, 16 * NBI)
                for j in range(CT):
                    nc.tensor.transpose(tp[j // 4][:, j % 4, 0:HT], fr[:, j, :],
                                        c.ident[0:HT, 0:HT]).then_inc(s_tp, 1)
                for j in range(CT):
                    pe.wait_ge(s_cp, j // 4 + 1)
                    nc.tensor.matmul(hp[j // 4][:, j % 4, :], frT[:, j, :], wT[:], start=True, stop=False)
                    nc.tensor.matmul(hp[j // 4][:, j % 4, :], ones[0:1, 0:HT], brow[:], start=False,
                                     stop=True).then_inc(s_mm, 1)

            @block.vector
            def _(dve):
                for g in range(2):
                    dve.wait_ge(s_tp, 4 * g + 4)
                    nc.vector.tensor_copy(frT[:, 4 * g:4 * g + 4, :], tp[g][:, :, 0:HT]).then_inc(s_cp, 1)

            @block.scalar
            def _(act):
                for g in range(2):
                    act.wait_ge(s_mm, 4 * g + 4)
                    nc.scalar.activation(H[:, bass.ds(i * CT + 4 * g, 4), :], hp[g][:], ACT.Relu).then_inc(s_h, 1)

        NG = NT // 4
        with st.step() as block:
            @block.tensor
            def _(pe):
                for g in range(NG):
                    nc.tensor.matmul(acc[:], ones[:], H[:, 4 * g:4 * g + 4, :].rearrange("p a d -> p (a d)"),
                                     start=(g == 0), stop=(g == NG - 1)).then_inc(s_mm, 1)
                for g in range(NG):
                    pe.wait_ge(s_h, g + 1)
                    if g == 0:
                        pe.wait_ge(s_cp, 1)
                    nc.tensor.matmul(acc[:], ones[:], sq2[g % 2][:], start=(g == 0), stop=(g == NG - 1)).then_inc(s_mm, 1)

            @block.vector
            def _(dve):
                own = Chain(dve, s_own)
                dve.wait_ge(s_mm, NG)
                own(nc.vector.tensor_reduce(mean[:], acc[:].rearrange("p (a d) -> p d a", a=4), AX.X, ALU.add))
                nc.vector.tensor_scalar(mean[:], mean[:], 1.0 / N, None, ALU.mult).then_inc(s_cp, 1)
                dve.wait_ge(s_cp, 1)
                for g in range(NG):
                    t = H[:, 4 * g:4 * g + 4, :]
                    own(nc.vector.tensor_tensor(t, t, mean[0:HT, None, :].to_broadcast([HT, 4, D]), ALU.subtract))
                    if g >= 2:
                        dve.wait_ge(s_mm, NG + g - 1)
                    u = t.rearrange("p a d -> p (a d)")
                    nc.vector.tensor_tensor(sq2[g % 2][:], u, u, ALU.mult).then_inc(s_h, 1)
                dve.wait_ge(s_mm, 2 * NG)
                own(nc.vector.tensor_reduce(var[:], acc[:].rearrange("p (a d) -> p d a", a=4), AX.X, ALU.add))
                nc.vector.tensor_scalar(var[:], var[:], 1.0 / N, EPS, ALU.mult, ALU.add).then_inc(s_cp, 1)
                dve.wait_ge(s_tp, 1)
                own(nc.vector.reciprocal(var[:], var[:]))
                own(nc.vector.tensor_tensor(var[:], var[:], gb[:, 0, :], ALU.mult))
                for g in range(8):
                    t = H[:, 16 * g:16 * g + 16, :]
                    own(nc.vector.tensor_tensor(t, t, var[0:HT, None, :].to_broadcast([HT, 16, D]), ALU.mult))
                    nc.vector.tensor_tensor(t, t, gb[0:HT, None, 1, :].to_broadcast([HT, 16, D]), ALU.add).then_inc(s_in, 1)

            @block.scalar
            def _(act):
                act.wait_ge(s_cp, 2)
                nc.scalar.activation(var[:], var[:], ACT.Sqrt).then_inc(s_tp, 1)

            @block.sync
            def _(sp):
                hv = h_out.rearrange("(j p) d -> p j d", p=HT)
                for g in range(8):
                    sp.wait_ge(s_in, g + 1)
                    sp.dma_start(hv[:, 16 * g:16 * g + 16, :], H[:, 16 * g:16 * g + 16, :]).then_inc(s_out, 16)
                sp.wait_ge(s_out, 16 * 8)


def ln_stage(nc, c, name, src, dst, dstT, gamma=None, beta=None):
    with Stage(nc, name) as st:
        h = st.sb("h", [HT, CT, D])
        stats = st.sb("stats", [HT, CT, 6])
        mv = st.sb("mv", [HT, CT, 2])
        rstd = st.sb("rstd", [HT, CT])
        xT = st.sb("xT", [D, CT, HT])
        tp = [st.ps(f"tp{i}", [D, 4, 128]) for i in range(2)]
        gb = st.sb("gb", [HT, 2, D])
        epsc = st.sb("eps", [HT, 1])
        s_in = st.sem("loaded")
        s_own = st.sem("own")
        s_mv = st.sem("var_ready")
        s_sq = st.sem("root_ready")
        s_x = st.sem("x_ready")
        s_tp = st.sem("transposed")
        s_cp = st.sem("xT_ready")
        s_out = st.sem("stored")
        with st.step() as block:
            @block.sync
            def _(sp):
                if gamma is not None:
                    sp.dma_start(gb[:, 0, :], wide(gamma, HT)).then_inc(s_in, 16)
                    sp.dma_start(gb[:, 1, :], wide(beta, HT)).then_inc(s_in, 16)
                    sp.wait_ge(s_in, 32)

            @block.vector
            def _(dve):
                nc.vector.memset(epsc[:], EPS).then_inc(s_own, 1)
                dve.wait_ge(s_own, 1)
        srcv, dstv = tiles_of(src), None if dst is None else tiles_of(dst)
        with nc.Fori(0, B // NBI) as i, st.step() as block:
            @block.sync
            def _(sp):
                for k in range(NBI):
                    sp.dma_start(h[:, 2 * k:2 * k + 2, :], srcv[i * NBI + k]).then_inc(s_in, 16)
                sp.wait_ge(s_x, CT)
                for k in range(NBI if dst is not None else 0):
                    sp.dma_start(dstv[i * NBI + k], h[:, 2 * k:2 * k + 2, :]).then_inc(s_out, 16)
                if dstT is not None:
                    sp.wait_ge(s_cp, 2)
                    sp.dma_start(dstT[:, bass.ds(i * (CT * HT), CT * HT)], xT[:].rearrange("p a d -> p (a d)")).then_inc(s_out, 16)
                sp.wait_ge(s_out, 16 * (NBI * (dst is not None) + (dstT is not None)))

            @block.vector
            def _(dve):
                own = Chain(dve, s_own)
                for k in range(CT):
                    if k % 2 == 0:
                        dve.wait_ge(s_in, 16 * NBI)
                    nc.vector.bn_stats(stats[:, k, :], h[:, k, :]).then_inc(s_mv, 1)
                dve.wait_ge(s_mv, CT)
                for k in range(CT):
                    nc.vector.bn_aggr(mv[:, k, :], stats[:, k, :]).then_inc(s_mv, 1)
                dve.wait_ge(s_mv, 2 * CT)
                dve.wait_ge(s_sq, 1)
                own(nc.vector.reciprocal(rstd[:], rstd[:]))
                for k in range(CT):
                    ins = nc.vector.tensor_scalar(h[:, k, :], h[:, k, :], mv[:, k, 0:1], rstd[:, k:k + 1],
                                                  ALU.subtract, ALU.mult)
                    if gamma is None:
                        ins.then_inc(s_x, 1)
                    else:
                        own(ins)
                        own(nc.vector.tensor_tensor(h[:, k, :], h[:, k, :], gb[:, 0, :], ALU.mult))
                        nc.vector.tensor_tensor(h[:, k, :], h[:, k, :], gb[:, 1, :], ALU.add).then_inc(s_x, 1)

            @block.scalar
            def _(act):
                act.wait_ge(s_mv, 2 * CT)
                nc.scalar.activation(rstd[:], mv[:, :, 1], ACT.Sqrt, bias=epsc[:, 0:1]).then_inc(s_sq, 1)
                for g in range(2 if dstT is not None else 0):
                    act.wait_ge(s_tp, 4 * g + 4)
                    nc.scalar.activation(xT[:, 4 * g:4 * g + 4, :], tp[g][:, :, 0:HT], ACT.Copy).then_inc(s_cp, 1)

            @block.tensor
            def _(pe):
                for k in range(CT if dstT is not None else 0):
                    pe.wait_ge(s_x, k + 1)
                    nc.tensor.transpose(tp[k // 4][:, k % 4, 0:HT], h[:, k, :], c.ident[0:HT, 0:HT]).then_inc(s_tp, 1)


SN = 64
SC = 8
CH = 8
KP = HT + T


def s4_constants():
    import numpy as np
    l = np.arange(T)
    half = np.pi * l / T
    j = np.arange(T)
    phase = 2 * np.pi * ((np.outer(l, j)) % T) / T + half[:, None]
    cos = np.cos(half)
    cos[T // 2] = 0.0
    f = np.float32
    return {"s4_cos": cos.astype(f), "s4_sin": np.sin(half).astype(f),
            "s4_dft_re": (np.cos(phase) / T).astype(f), "s4_dft_im": (-np.sin(phase) / T).astype(f)}


def s4_kernel_stage(nc, c, Lre, Lim, P, Bm, C, Dv, log_step, cos, sin, dre, dim, kpad):
    with Stage(nc, "s4k") as st:
        lr = st.sb("lr", [D, SN])
        pbc = st.sb("pbc", [D, 3, SN, 2])
        ls = st.sb("ls", [D, 1])
        dcol = st.sb("dcol", [D, 1])
        q = st.sb("q", [D, 11, 2, SN])
        t1 = st.sb("t1", [D, SN])
        tps = [st.ps(f"tp{i}", [D, 4, D]) for i in range(3)]
        coef = st.sb("coef", [D, 3, SN])
        v = st.sb("v", [D, 2, SN, 2, 8])
        cosb = st.sb("cosb", [D, T])
        sinb = st.sb("sinb", [D, T])
        ctheta = st.sb("ctheta", [HT, 2])
        dft = st.sb("dft", [HT, 2, 2, T])
        den = st.sb("den", [D, 2, SC, T])
        m1 = st.sb("m1", [D, SC, T])
        m2 = st.sb("m2", [D, SC, T])
        sp_ = [st.ps(f"s{i}", [HT, SC, 2, 8]) for i in range(2)]
        S = st.sb("S", [HT, 2, 2, SN, 8])
        w = [st.sb(f"w{i}", [HT, 2, D]) for i in range(8)]
        kps = st.ps("kps", [D, T])
        K = st.sb("K", [D, KP])
        s_in = st.sem("loaded")
        s_own = st.sem("own")
        s_act = st.sem("act")
        s_q = st.sem("columns_ready")
        s_tp = st.sem("transposed")
        s_r = st.sem("r_ready")
        s_mm = st.sem("summed")
        s_out = st.sem("stored")

        with st.step() as block:
            @block.sync
            def _(sp):
                sp.dma_start(lr[:], Lre[:, :]).then_inc(s_in, 16)
                sp.dma_start(q[:, 1, 0, :], Lim[:, :]).then_inc(s_in, 16)
                for k, x in enumerate((P, Bm, C)):
                    sp.dma_start(pbc[:, k, :, :], x[:, :, :]).then_inc(s_in, 16)
                sp.dma_start(ls[:], log_step.rearrange("(h a) -> h a", a=1)).then_inc(s_in, 16)
                sp.dma_start(dcol[:], Dv.rearrange("(h a) -> h a", a=1)).then_inc(s_in, 16)
                sp.dma_start(cosb[:], wide(cos)).then_inc(s_in, 16)
                sp.dma_start(sinb[:], wide(sin)).then_inc(s_in, 16)
                for k in range(2):
                    sp.dma_start(ctheta[:, k:k + 1], cos[k * HT:(k + 1) * HT].rearrange("(p a) -> p a", a=1)).then_inc(s_in, 16)
                    sp.dma_start(dft[:, 0, k, :], dre[k * HT:(k + 1) * HT, :]).then_inc(s_in, 16)
                    sp.dma_start(dft[:, 1, k, :], dim[k * HT:(k + 1) * HT, :]).then_inc(s_in, 16)
                sp.wait_ge(s_in, 16 * 15)

            @block.scalar
            def _(act):
                act.wait_ge(s_in, 16 * 15)
                nc.scalar.activation(ls[:], ls[:], ACT.Exp, scale=-1.0).then_inc(s_act, 1)

            @block.vector
            def _(dve):
                own = Chain(dve, s_own)
                V = nc.vector
                dve.wait_ge(s_in, 16 * 15)
                own(V.memset(v[:], 0.0))
                own(V.memset(K[:, 0:HT], 0.0))
                own(V.tensor_scalar(q[:, 0, 0, :], lr[:], -0.0001, -1.0, ALU.min, ALU.mult))
                dve.wait_ge(s_act, 1)
                own(V.tensor_scalar(q[:, 2, 0, :], lr[:], 0.0, 2.0, ALU.mult, ALU.add))
                own(V.tensor_scalar(q[:, 2, 0, :], q[:, 2, 0, :], ls[:, 0:1], None, ALU.mult))
                re = lambda k: pbc[:, k, :, 0]
                im = lambda k: pbc[:, k, :, 1]
                for n, (x, y) in enumerate(((2, 1), (2, 0), (0, 1), (0, 0))):
                    own(V.tensor_tensor(t1[:], im(x), im(y), ALU.mult))
                    own(V.tensor_tensor(q[:, 3 + n, 0, :], re(x), re(y), ALU.mult))
                    own(V.tensor_tensor(q[:, 3 + n, 0, :], q[:, 3 + n, 0, :], t1[:], ALU.add))
                    own(V.tensor_tensor(t1[:], im(x), re(y), ALU.mult))
                    own(V.tensor_tensor(q[:, 7 + n, 0, :], re(x), im(y), ALU.mult))
                    own(V.tensor_tensor(q[:, 7 + n, 0, :], q[:, 7 + n, 0, :], t1[:], ALU.subtract))
                V.tensor_copy(q[:, :, 1, :], q[:, :, 0, :]).then_inc(s_q, 1)
                dve.wait_ge(s_tp, 11)
                tp = lambda k: tps[k // 4][:, k % 4, :]
                for g in range(2):
                    r = slice(64 * g, 64 * g + 64)
                    for k in range(3):
                        own(V.tensor_copy(coef[r, k, :], tp(k)[r, r]))
                    for n in range(4):
                        own(V.tensor_copy(v[r, 0, :, g, 2 * n], tp(3 + n)[r, r]))
                        own(V.tensor_copy(v[r, 0, :, g, 2 * n + 1], tp(7 + n)[r, r]))
                        own(V.tensor_copy(v[r, 1, :, g, 2 * n], tp(7 + n)[r, r]))
                        own(V.tensor_scalar(v[r, 1, :, g, 2 * n + 1], tp(3 + n)[r, r], -1.0, None, ALU.mult))

            @block.tensor
            def _(pe):
                pe.wait_ge(s_q, 1)
                for k in range(11):
                    nc.tensor.transpose(tps[k // 4][:, k % 4, :], q[:, k, :, :].rearrange("p a n -> p (a n)"),
                                        c.ident[:]).then_inc(s_tp, 1)

        with nc.Fori(0, SN // SC) as i, st.step() as block:
            full = [D, SC, T]

            @block.vector
            def _(dve):
                own = Chain(dve, s_own)
                V = nc.vector
                cf = lambda k: coef[:, k, bass.ds(i * SC, SC)].unsqueeze(2).to_broadcast(full)
                cs = cosb[:, None, :].to_broadcast(full)
                sn = sinb[:, None, :].to_broadcast(full)
                own(V.tensor_tensor(den[:, 0], cf(0), cs, ALU.mult))
                own(V.tensor_tensor(m1[:], cf(2), sn, ALU.mult))
                own(V.tensor_tensor(m2[:], cf(1), cs, ALU.mult))
                own(V.tensor_tensor(den[:, 1], m1[:], m2[:], ALU.subtract))
                own(V.tensor_tensor(m1[:], den[:, 0], den[:, 0], ALU.mult))
                own(V.tensor_tensor(m2[:], den[:, 1], den[:, 1], ALU.mult))
                own(V.tensor_tensor(m1[:], m1[:], m2[:], ALU.add))
                own(V.reciprocal(m1[:], m1[:]))
                own(V.tensor_tensor(den[:, 0], den[:, 0], m1[:], ALU.mult))
                V.tensor_tensor(den[:, 1], den[:, 1], m1[:], ALU.mult).then_inc(s_r, 1)
                for k in range(2):
                    dve.wait_ge(s_mm, SC * 2 * (k + 1))
                    own(V.tensor_copy(S[:, k, :, bass.ds(i * SC, SC), :], sp_[k][:].rearrange("p i g q -> p g i q")))

            @block.tensor
            def _(pe):
                pe.wait_ge(s_r, 1)
                for k in range(2):
                    for n in range(SC):
                        for part in range(2):
                            nc.tensor.matmul(sp_[k][:, n, :, :].rearrange("p g q -> p (g q)"), den[:, part, n, k * HT:(k + 1) * HT],
                                             v[:, part, bass.ds(i * SC + n, 1), :, :].rearrange("p a g q -> p (a g q)"),
                                             start=(part == 0), stop=(part == 1)).then_inc(s_mm, 1)

        with st.step() as block:
            @block.vector
            def _(dve):
                own = Chain(dve, s_own)
                V = nc.vector
                s = lambda n: S[:, :, :, :, n].rearrange("p c g i -> p c (g i)")
                cb = ctheta[:, :].unsqueeze(2).to_broadcast([HT, 2, D])
                tt = lambda o, a, b, op: own(V.tensor_tensor(o, a, b, op))
                W = [x[:] for x in w]
                tt(W[0], s(6), cb, ALU.mult)
                own(V.tensor_scalar(W[0], W[0], 1.0, None, ALU.add))
                tt(W[1], s(7), cb, ALU.mult)
                tt(W[2], s(2), s(4), ALU.mult)
                tt(W[3], s(3), s(5), ALU.mult)
                tt(W[2], W[2], W[3], ALU.subtract)
                tt(W[3], s(2), s(5), ALU.mult)
                tt(W[4], s(3), s(4), ALU.mult)
                tt(W[3], W[3], W[4], ALU.add)
                tt(W[4], W[0], W[0], ALU.mult)
                tt(W[5], W[1], W[1], ALU.mult)
                tt(W[4], W[4], W[5], ALU.add)
                own(V.reciprocal(W[4], W[4]))
                tt(W[4], W[4], cb, ALU.mult)
                tt(W[5], W[2], W[0], ALU.mult)
                tt(W[6], W[3], W[1], ALU.mult)
                tt(W[5], W[5], W[6], ALU.add)
                tt(W[5], W[5], W[4], ALU.mult)
                tt(W[6], W[3], W[0], ALU.mult)
                tt(W[7], W[2], W[1], ALU.mult)
                tt(W[6], W[6], W[7], ALU.subtract)
                tt(W[6], W[6], W[4], ALU.mult)
                tt(W[5], s(0), W[5], ALU.subtract)
                V.tensor_tensor(W[6], s(1), W[6], ALU.subtract).then_inc(s_r, 1)
                dve.wait_ge(s_mm, 4)
                own(V.tensor_copy(K[:, HT:KP], kps[:]))
                V.tensor_tensor(K[:, HT:HT + 1], K[:, HT:HT + 1], dcol[:], ALU.add).then_inc(s_q, 1)

            @block.tensor
            def _(pe):
                pe.wait_ge(s_r, 1)
                for n in range(4):
                    nc.tensor.matmul(kps[:], w[5 + n // 2][:, n % 2, :], dft[:, n // 2, n % 2, :], start=(n == 0),
                                     stop=(n == 3)).then_inc(s_mm, 1)

            @block.sync
            def _(sp):
                sp.wait_ge(s_q, 1)
                sp.dma_start(kpad[:, :], K[:]).then_inc(s_out, 16)
                sp.wait_ge(s_out, 16)


def s4_conv_stage(nc, c, xn, kpad, h, h_out):
    with Stage(nc, "s4c") as st:
        H = st.sb("H", [HT, NT, D])
        U = st.sb("U", [HT, B, 2, D])
        tz = st.sb("tz", [HT, CH, T])
        flip = st.sb("flip", [HT, HT])
        y = [st.ps(f"y{i}", [HT, CH, B]) for i in range(2)]
        s_in = st.sem("loaded")
        s_t = st.sem("toeplitz_loaded")
        s_mm = st.sem("multiplied")
        s_h = st.sem("added")
        s_out = st.sem("stored")
        hv = lambda x: x.rearrange("(j p) d -> p j d", p=HT)
        with st.step() as block:
            @block.sync
            def _(sp):
                for g in range(8):
                    r = slice(16 * g, 16 * g + 16)
                    sp.dma_start(H[:, r, :], hv(h)[:, r, :]).then_inc(s_in, 16)
                    sp.dma_start(U[:, 8 * g:8 * g + 8, :, :].rearrange("p b c d -> p (b c) d"), hv(xn)[:, r, :]).then_inc(s_in, 16)
                sp.wait_ge(s_in, 16 * 16)

            @block.gpsimd
            def _(pool):
                nc.gpsimd.memset(flip[:], 0.0).then_inc(s_h, 1)
                pool.wait_ge(s_h, 1)
                nc.gpsimd.affine_select(out=flip[:], in_=flip[:], compare_op=ALU.not_equal, fill=1.0, base=1 - HT,
                                        pattern=[[1, HT]], channel_multiplier=1).then_inc(s_h, 1)
                pool.wait_ge(s_h, 2)

        Uf = U[:].rearrange("p b c d -> p (b c d)")
        with nc.Fori(0, NT // 8) as i, st.step() as block:
            @block.tensor
            def _(pe):
                for k in range(2):
                    nc.tensor.matmul(y[k][:].rearrange("p n b -> p (n b)"), flip[:], Uf[:, bass.ds(i * (8 * D) + k * 4 * D, 4 * D)],
                                     start=True, stop=True).then_inc(s_mm, 1)

            @block.vector
            def _(dve):
                for k in range(2):
                    dve.wait_ge(s_mm, k + 1)
                    nc.vector.tensor_copy(Uf[:, bass.ds(i * (8 * D) + k * 4 * D, 4 * D)], y[k][:].rearrange("p n b -> p (n b)")).then_inc(s_h, 1)
                dve.wait_ge(s_h, 2)
        toep = bass.AP(kpad.tensor, 1, [[KP, D], [1, HT], [1, T]])
        with nc.Fori(0, D // CH) as i, st.step() as block:
            @block.sync
            def _(sp):
                sp.dma_start(tz[:], toep[bass.ds(i * CH, CH)].rearrange("h p t -> p h t")).then_inc(s_t, 16)

            @block.tensor
            def _(pe):
                pe.wait_ge(s_t, 16)
                u = lambda n, k: U[:, :, k, bass.ds(i * CH + n, 1)].rearrange("p b a -> p (b a)")
                for n in range(CH):
                    nc.tensor.matmul(y[0][:, n, :], tz[:, n, 0:HT], u(n, 0), start=True, stop=True)
                    nc.tensor.matmul(y[1][:, n, :], tz[:, n, HT:T], u(n, 0), start=True, stop=False)
                    nc.tensor.matmul(y[1][:, n, :], tz[:, n, 0:HT], u(n, 1), start=False, stop=True).then_inc(s_mm, 1)

            @block.vector
            def _(dve):
                dve.wait_ge(s_mm, CH)
                for k in range(2):
                    hk = H[:, :, bass.ds(i * CH, CH)].rearrange("p (b c) d -> p b c d", c=2)[:, :, k, :]
                    nc.vector.tensor_tensor(hk, hk, y[k][:].rearrange("p n b -> p b n"), ALU.add).then_inc(s_h, 1)
                dve.wait_ge(s_h, 2)
        with st.step() as block:
            @block.sync
            def _(sp):
                for g in range(8):
                    r = slice(16 * g, 16 * g + 16)
                    sp.dma_start(hv(h_out)[:, r, :], H[:, r, :]).then_inc(s_out, 16)
                sp.wait_ge(s_out, 16 * 8)


def route_stage(nc, c, name, E, cap, xn, xnT, Wr, br, xp, idx_out):
    C = 128 // E
    TC = NT // C
    M = TC * HT
    G = cap // HT
    with Stage(nc, name) as st:
        L = st.sb("L", [HT, NT, E])
        PT = st.sb("PT", [128, M])
        s1 = st.sb("s1", [128, M])
        s2 = st.sb("s2", [128, M])
        one = st.sb("one", [128, M], BF16)
        wr = st.sb("wr", [D, E])
        brow = st.sb("brow", [1, E])
        onerow = st.sb("onerow", [1, HT])
        xt = st.sb("xt", [D, CT * HT])
        red = st.sb("red", [HT, 2, NT])
        same = st.sb("same", [128, 128])
        before = st.sb("before", [128, 128])
        tau = st.sb("tau", [128, 1])
        cand = st.sb("cand", [128, 1])
        bit = st.sb("bit", [128, 1], I32)
        cnt = st.sb("cnt", [128, 2])
        mask = st.sb("mask", [128, 2])
        stg = st.sb("stg", [128, 4, 128])
        iop = st.sb("iop", [HT, HT], BF16)
        ios = st.sb("ios", [HT, G], F32)
        tid = st.sb("tid", [HT, NT])
        qid = st.sb("qid", [HT, 1])
        hi_i = st.sb("hi_i", [HT, NT, E], I32)
        hi = st.sb("hi", [HT, NT, E])
        lo = st.sb("lo", [HT, NT, E], BF16)
        TS = 2
        A = st.sb("A", [HT, TS, E, HT], BF16)
        Bv = st.sb("Bv", [HT, TS, E, 2, G], BF16)
        lst = st.sb("lst", [HT, E, 2, G])
        idx = st.sb("idx", [HT, E, G], U32)
        lp = st.ps("lp", [HT, CT, E])
        tp = st.ps("tp", [128, 4, 128])
        cp = st.ps("cp", [128, 2])
        ip = st.ps("ip", [HT, E * 2 * G])
        s_in = st.sem("loaded")
        s_own = st.sem("own")
        s_pool = st.sem("constants")
        s_pown = st.sem("pool_own")
        s_mm = st.sem("multiplied")
        s_act = st.sem("act")
        s_x = st.sem("dve_ready")
        s_out = st.sem("stored")
        V = nc.vector
        grp = lambda m: m[:].rearrange("p (e c) -> p e c", c=C)

        with st.step() as block:
            @block.sync
            def _(sp):
                sp.dma_start(wr[:], Wr[:, :]).then_inc(s_in, 16)
                if br is not None:
                    sp.dma_start(brow[:], br.rearrange("(a d) -> a d", a=1)).then_inc(s_in, 16)
                for k in range(8):
                    r = slice(k * (N // 8), (k + 1) * (N // 8))
                    sp.dma_start(xp[r, 0:D], xn[r, :]).then_inc(s_in, 16)
                sp.wait_ge(s_in, 16 * (9 + (br is not None)))

            @block.vector
            def _(dve):
                own = Chain(dve, s_own)
                if br is None:
                    own(V.memset(brow[:], 0.0))
                own(V.memset(onerow[:], 1.0))
                own(V.memset(tau[:], 0.0))
                own(V.memset(bit[:], 1 << 29))
                own(V.memset(lst[:], 0.0))

            @block.gpsimd
            def _(pool):
                own = Chain(pool, s_pown)
                P = nc.gpsimd
                own(P.memset(same[:], 1.0))
                own(P.affine_select(out=grp(same), in_=grp(same), compare_op=ALU.is_ge, fill=0.0, base=0,
                                    pattern=[[-C, E], [0, C]], channel_multiplier=1))
                own(P.affine_select(out=grp(same), in_=grp(same), compare_op=ALU.is_ge, fill=0.0, base=C - 1,
                                    pattern=[[C, E], [0, C]], channel_multiplier=-1))
                own(P.affine_select(out=grp(before), in_=grp(same), compare_op=ALU.is_gt, fill=0.0, base=0,
                                    pattern=[[C, E], [1, C]], channel_multiplier=-1))
                own(P.memset(one[:], 1.0))
                own(P.iota(iop[:], pattern=[[1, HT]], base=0, channel_multiplier=0, allow_small_or_imprecise_dtypes=True))
                own(P.iota(ios[:], pattern=[[1, G]], base=0, channel_multiplier=0, allow_small_or_imprecise_dtypes=True))
                own(P.iota(tid[:], pattern=[[1, NT]], base=0, channel_multiplier=0, allow_small_or_imprecise_dtypes=True))
                own(P.iota(qid[:], pattern=[[0, 1]], base=0, channel_multiplier=1, allow_small_or_imprecise_dtypes=True))

        with nc.Fori(0, NT // CT) as i, st.step() as block:
            @block.sync
            def _(sp):
                sp.dma_start(xt[:], xnT[:, bass.ds(i * (CT * HT), CT * HT)]).then_inc(s_in, 16)

            @block.tensor
            def _(pe):
                pe.wait_ge(s_in, 16)
                for k in range(CT):
                    nc.tensor.matmul(lp[:, k, :], xt[:, k * HT:(k + 1) * HT], wr[:], start=True, stop=False)
                    nc.tensor.matmul(lp[:, k, :], onerow[:], brow[:], start=False, stop=True).then_inc(s_mm, 1)

            @block.vector
            def _(dve):
                dve.wait_ge(s_mm, CT)
                V.tensor_copy(L[:, bass.ds(i * CT, CT), :], lp[:]).then_inc(s_x, 1)
                dve.wait_ge(s_x, 1)

        with st.step() as block:
            @block.vector
            def _(dve):
                own = Chain(dve, s_own)
                rb = lambda k: red[:, k, :].unsqueeze(2).to_broadcast([HT, NT, E])
                own(V.tensor_reduce(red[:, 0, :], L[:], AX.X, ALU.max))
                V.tensor_tensor(L[:], L[:], rb(0), ALU.subtract).then_inc(s_x, 1)
                dve.wait_ge(s_act, 1)
                own(V.tensor_reduce(red[:, 1, :], L[:], AX.X, ALU.add))
                own(V.reciprocal(red[:, 1, :], red[:, 1, :]))
                V.tensor_tensor(L[:], L[:], rb(1), ALU.mult).then_inc(s_x, 1)

            @block.scalar
            def _(act):
                act.wait_ge(s_x, 1)
                nc.scalar.activation(L[:], L[:], ACT.Exp).then_inc(s_act, 1)

            @block.sync
            def _(sp):
                sp.wait_ge(s_x, 2)
                for k in range(8):
                    sp.dma_start(xp.rearrange("(j p) d -> p j d", p=HT)[:, 16 * k:16 * k + 16, D:D + E],
                                 L[:, 16 * k:16 * k + 16, :]).then_inc(s_out, 16)
                sp.wait_ge(s_out, 16 * 8)

        Lc = L[:].rearrange("p (c i) e -> p i e c", c=C)
        with nc.Fori(0, TC // 4) as i, st.step() as block:
            @block.vector
            def _(dve):
                for k in range(4):
                    V.tensor_copy(stg[0:HT, k, :].rearrange("p (a e c) -> p a e c", a=1, c=C),
                                  Lc[:, bass.ds(i * 4 + k, 1)]).then_inc(s_x, 1)
                dve.wait_ge(s_mm, 4)
                V.tensor_copy(PT[:, bass.ds(i * (4 * HT), 4 * HT)].rearrange("p (a t) -> p a t", a=4),
                              tp[:, :, 0:HT]).then_inc(s_x, 1)
                dve.wait_ge(s_x, 5)

            @block.tensor
            def _(pe):
                for k in range(4):
                    pe.wait_ge(s_x, k + 1)
                    nc.tensor.transpose(tp[:, k, 0:HT], stg[0:HT, k, :], c.ident[0:HT, 0:HT]).then_inc(s_mm, 1)

        with nc.Fori(0, 30) as i, st.step() as block:
            @block.vector
            def _(dve):
                own = Chain(dve, s_own)
                own(V.tensor_tensor(cand[:].bitcast(I32), tau[:].bitcast(I32), bit[:], ALU.bitwise_or))
                own(V.tensor_scalar(bit[:], bit[:], 1, None, ALU.logical_shift_right))
                V.tensor_scalar(s1[:], PT[:], cand[:, 0:1], None, ALU.is_ge, ALU.add, accum_out=cnt[:, 0:1]).then_inc(s_x, 1)
                dve.wait_ge(s_mm, 1)
                own(V.tensor_scalar(mask[:, 0:1], cp[:, 0:1], float(cap), cand[:, 0:1], ALU.is_ge, ALU.mult))
                own(V.tensor_tensor(tau[:], tau[:], mask[:, 0:1], ALU.max))

            @block.tensor
            def _(pe):
                pe.wait_ge(s_x, 1)
                nc.tensor.matmul(cp[:, 0:1], same[:], cnt[:, 0:1], start=True, stop=True).then_inc(s_mm, 1)

        with st.step() as block:
            @block.vector
            def _(dve):
                own = Chain(dve, s_own)
                own(V.tensor_scalar(s1[:], PT[:], tau[:, 0:1], None, ALU.is_gt, ALU.add, accum_out=cnt[:, 0:1]))
                V.tensor_scalar(s2[:], PT[:], tau[:, 0:1], None, ALU.is_equal, ALU.add, accum_out=cnt[:, 1:2]).then_inc(s_x, 1)
                dve.wait_ge(s_mm, 2)
                own(V.tensor_scalar(mask[:, 0:1], cp[:, 0:1], -1.0, float(cap), ALU.mult, ALU.add))
                own(V.tensor_copy(mask[:, 1:2], cp[:, 1:2]))
                own(V.tensor_tensor_scan(PT[:], one[:], s2[:], mask[:, 1:2], ALU.mult, ALU.add))
                own(V.tensor_scalar(PT[:], PT[:], mask[:, 0:1], None, ALU.is_le))
                own(V.tensor_tensor(s2[:], s2[:], PT[:], ALU.mult))
                own(V.tensor_tensor(s1[:], s1[:], s2[:], ALU.add))
                V.tensor_reduce(cnt[:, 0:1], s1[:], AX.X, ALU.add).then_inc(s_x, 1)
                dve.wait_ge(s_mm, 3)
                own(V.tensor_copy(mask[:, 1:2], cp[:, 1:2]))
                own(V.tensor_tensor_scan(PT[:], one[:], s1[:], mask[:, 1:2], ALU.mult, ALU.add))
                own(V.tensor_tensor(PT[:], PT[:], s1[:], ALU.mult))
                own(V.tensor_scalar(PT[:], PT[:], -1.0, None, ALU.add))

            @block.tensor
            def _(pe):
                pe.wait_ge(s_x, 1)
                nc.tensor.matmul(cp[:, 0:1], same[:], cnt[:, 0:1], start=True, stop=True).then_inc(s_mm, 1)
                nc.tensor.matmul(cp[:, 1:2], before[:], cnt[:, 1:2], start=True, stop=True).then_inc(s_mm, 1)
                pe.wait_ge(s_x, 2)
                nc.tensor.matmul(cp[:, 1:2], before[:], cnt[:, 0:1], start=True, stop=True).then_inc(s_mm, 1)

        with nc.Fori(0, TC // 4) as i, st.step() as block:
            @block.vector
            def _(dve):
                V.tensor_copy(stg[:, :, 0:HT], PT[:, bass.ds(i * (4 * HT), 4 * HT)].rearrange("p (a t) -> p a t", a=4)).then_inc(s_x, 1)
                for k in range(4):
                    dve.wait_ge(s_mm, 4)
                    V.tensor_copy(Lc[:, bass.ds(i * 4 + k, 1)],
                                  tp[0:HT, k, :].rearrange("p (a e c) -> p a e c", a=1, c=C)).then_inc(s_x, 1)
                dve.wait_ge(s_x, 5)

            @block.tensor
            def _(pe):
                pe.wait_ge(s_x, 1)
                for k in range(4):
                    nc.tensor.transpose(tp[0:HT, k, :], stg[:, k, 0:HT], c.ident[:]).then_inc(s_mm, 1)

        with st.step() as block:
            @block.vector
            def _(dve):
                own = Chain(dve, s_own)
                own(V.tensor_scalar(hi[:], L[:], 0.0, -1.0, ALU.is_ge, ALU.add))
                for g in range(1, G):
                    own(V.scalar_tensor_tensor(hi[:], L[:], float(g * HT), hi[:], ALU.is_ge, ALU.add))
                own(V.scalar_tensor_tensor(lo[:], hi[:], -float(HT), L[:], ALU.mult, ALU.add))

        with nc.Fori(0, NT // TS) as i, st.step() as block:
            @block.vector
            def _(dve):
                own = Chain(dve, s_own)
                for k in range(TS):
                    j = bass.ds(i * TS + k, 1)
                    lj = lo[:, j, :].rearrange("p a e -> p (a e)").unsqueeze(2).to_broadcast([HT, E, HT])
                    hj = hi[:, j, :].rearrange("p a e -> p (a e)").unsqueeze(2).to_broadcast([HT, E, G])
                    V.tensor_tensor(A[:, k], lj, iop[:, None, :].to_broadcast([HT, E, HT]), ALU.is_equal).then_inc(s_x, 1)
                    own(V.tensor_tensor(Bv[:, k, :, 0, :], hj, ios[:, None, :].to_broadcast([HT, E, G]), ALU.is_equal))
                    own(V.tensor_scalar(Bv[:, k, :, 1, :], Bv[:, k, :, 0, :], qid[:, 0:1], None, ALU.mult))
                    V.tensor_scalar(Bv[:, k, :, 0, :], Bv[:, k, :, 0, :], tid[:, j], None, ALU.mult).then_inc(s_x, 1)
                dve.wait_ge(s_mm, E)
                lf = lst[:].rearrange("p e v g -> p (e v g)")
                own(V.tensor_tensor(lf, lf, ip[:], ALU.add))

            @block.tensor
            def _(pe):
                pe.wait_ge(s_x, 2 * TS)
                for e in range(E):
                    for k in range(TS):
                        ins = nc.tensor.matmul(ip[:, e * 2 * G:(e + 1) * 2 * G], A[:, k, e, :],
                                               Bv[:, k, e].rearrange("p v g -> p (v g)"), start=(k == 0), stop=(k == TS - 1))
                    ins.then_inc(s_mm, 1)

        with st.step() as block:
            @block.vector
            def _(dve):
                V.scalar_tensor_tensor(idx[:], lst[:, :, 0, :], float(HT), lst[:, :, 1, :], ALU.mult, ALU.add).then_inc(s_x, 1)

            @block.sync
            def _(sp):
                sp.wait_ge(s_x, 1)
                sp.dma_start(idx_out[:, :, :], idx[:]).then_inc(s_out, 16)
                sp.wait_ge(s_out, 16)


def experts_stage(nc, c, name, E, cap, F, share, fn, xp, idx_in, Wup, bup, Wdn, bdn, acc):
    G = cap // HT
    FC = -(-F // 128)
    fw = [min(128, F - 128 * k) for k in range(FC)]
    R = D + E
    NG = G // 4
    JOBS = share * NG
    with Stage(nc, name) as st:
        idx = st.sb("idx", [HT, E, G], U32)
        ij = st.sb("ij", [HT, JOBS, 4], U32)
        xg = st.sb("xg", [HT, JOBS, 4, R])
        up = st.sb("up", [D, F])
        dn = st.sb("dn", [128, share, FC, D])
        bu = st.sb("bu", [128, FC])
        bd = st.sb("bd", [1, share, D])
        onerow = st.sb("onerow", [1, HT])
        xT = [st.sb(f"xT{i}", [D, 4 * HT]) for i in range(2)]
        a = [st.sb(f"a{i}", [128, FC, 4 * HT]) for i in range(2)]
        y = st.sb("y", [HT, JOBS, 4, D])
        tp = st.ps("tp", [D, 4, 128])
        hp = [st.ps(f"hp{i}", [128, 4 * HT]) for i in range(2)]
        yp = [st.ps(f"yp{i}", [HT, 4, D]) for i in range(2)]
        s_in = st.sem("loaded")
        s_idx = st.sem("indices")
        s_g = [st.pool_sem(f"gathered{k}") for k in range(JOBS)]
        s_tp = st.sem("transposed")
        s_xT = st.sem("xT_ready")
        s_up = st.sem("up_done")
        s_a = st.sem("act_done")
        s_dn = st.sem("down_done")
        s_y = st.sem("y_ready")
        s_sc = st.pool_sem("scattered")
        V = nc.vector
        with st.step() as block:
            @block.sync
            def _(sp):
                sp.dma_start(idx[:], idx_in[:, :, :]).then_inc(s_in, 16)
                sp.wait_ge(s_in, 16)

            @block.vector
            def _(dve):
                V.memset(onerow[:], 1.0).then_inc(s_y, 1)
                dve.wait_ge(s_y, 1)

        with nc.Fori(0, E // share) as i, st.step() as block:
            @block.sync
            def _(sp):
                sp.dma_start(up[:], Wup[i]).then_inc(s_in, 16)
                nf = F // 128
                if nf:
                    sp.dma_start(bu[:, 0:nf], bup[i][0:nf * 128].rearrange("(c p) -> p c", p=128),
                                 allow_slow_non_contiguous=True).then_inc(s_in, 16)
                if fw[-1] < 128:
                    sp.dma_start(bu[0:fw[-1], nf:nf + 1], bup[i][nf * 128:F].rearrange("(p c) -> p c", c=1)).then_inc(s_in, 16)
                for s in range(share):
                    for k in range(FC):
                        sp.dma_start(dn[0:fw[k], s, k, :], Wdn[i * share + s][k * 128:k * 128 + fw[k], :]).then_inc(s_in, 16)
                    sp.dma_start(bd[:, s, :], bdn[bass.ds(i * share + s, 1), :]).then_inc(s_in, 16)
            loads = 16 * (2 + (fw[-1] < 128) + share * (FC + 1))

            @block.gpsimd
            def _(pool):
                pool.wait_ge(s_idx, 1)
                for k in range(JOBS):
                    for t in range(4):
                        nc.gpsimd.indirect_dma_start(xg[:, k, t, :], None, xp[:, :],
                                                     bass.IndirectOffsetOnAxis(ap=ij[:, k, t:t + 1], axis=0)).then_inc(s_g[k], 16)
                for k in range(JOBS):
                    pool.wait_ge(s_y, k + 1)
                    if k % NG == 0 and k > 0:
                        pool.wait_ge(s_sc, 64 * k)
                    for t in range(4):
                        nc.gpsimd.indirect_dma_start(acc[:, :], bass.IndirectOffsetOnAxis(ap=ij[:, k, t:t + 1], axis=0),
                                                     y[:, k, t, :], None, compute_op=ALU.add).then_inc(s_sc, 16)
                pool.wait_ge(s_sc, 64 * JOBS)

            @block.vector
            def _(dve):
                V.tensor_copy(ij[:].rearrange("p (s g) t -> p s (g t)", s=share), idx[:, bass.ds(i * share, share), :]).then_inc(s_idx, 1)
                for k in range(JOBS + 1):
                    if k < JOBS:
                        dve.wait_ge(s_tp, 4 * k + 4)
                        if k >= 2:
                            dve.wait_ge(s_up, FC * (k - 1))
                        V.tensor_copy(xT[k % 2][:].rearrange("p (a t) -> p a t", a=4), tp[:, :, 0:HT]).then_inc(s_xT, 1)
                    if k >= 1:
                        m = k - 1
                        dve.wait_ge(s_dn, m + 1)
                        for t in range(4):
                            gate = xg[:, m, t, bass.ds(D + i * share + m // NG, 1)]
                            ins = V.tensor_scalar(y[:, m, t, :], yp[m % 2][:, t, :], gate, None, ALU.mult)
                        ins.then_inc(s_y, 1)

            @block.scalar
            def _(act):
                act.wait_ge(s_in, loads)
                for k in range(JOBS):
                    for f in range(FC):
                        act.wait_ge(s_up, k * FC + f + 1)
                        if k >= 2:
                            act.wait_ge(s_dn, k - 1)
                        nc.scalar.activation(a[k % 2][0:fw[f], f, :], hp[f % 2][0:fw[f], :], fn,
                                             bias=bu[0:fw[f], f:f + 1]).then_inc(s_a, 1)

            @block.tensor
            def _(pe):
                def turn(k):
                    pe.wait_ge(s_g[k], 64)
                    if k >= 1:
                        pe.wait_ge(s_xT, k)
                    for t in range(4):
                        nc.tensor.transpose(tp[:, t, 0:HT], xg[:, k, t, 0:D], c.ident[0:HT, 0:HT]).then_inc(s_tp, 1)

                turn(0)
                pe.wait_ge(s_in, loads)
                for k in range(JOBS):
                    pe.wait_ge(s_xT, k + 1)
                    for f in range(FC):
                        if k * FC + f >= 2:
                            pe.wait_ge(s_a, k * FC + f - 1)
                        nc.tensor.matmul(hp[f % 2][0:fw[f], :], up[:, f * 128:f * 128 + fw[f]], xT[k % 2][:],
                                         start=True, stop=True).then_inc(s_up, 1)
                    if k + 1 < JOBS:
                        turn(k + 1)
                    pe.wait_ge(s_a, (k + 1) * FC)
                    if k >= 2:
                        pe.wait_ge(s_y, k - 1)
                    s = k // NG
                    for t in range(4):
                        for f in range(FC):
                            nc.tensor.matmul(yp[k % 2][:, t, :], a[k % 2][0:fw[f], f, t * HT:(t + 1) * HT], dn[0:fw[f], s, f, :],
                                             start=(f == 0), stop=False)
                        ins = nc.tensor.matmul(yp[k % 2][:, t, :], onerow[:], bd[:, s, :], start=False, stop=True)
                    ins.then_inc(s_dn, 1)


def shared_stage(nc, c, xnT, sw1, sb1, sw2, sb2, h, h_out, F=512):
    FC = F // 128
    with Stage(nc, "shared") as st:
        up = st.sb("up", [D, F])
        dn = st.sb("dn", [128, FC, D])
        bu = st.sb("bu", [128, FC])
        bd = st.sb("bd", [1, D])
        onerow = st.sb("onerow", [1, HT])
        xT = st.sb("xT", [D, CT * HT])
        ht = st.sb("ht", [HT, CT, D])
        a = [st.sb(f"a{i}", [128, FC, 4 * HT]) for i in range(2)]
        hp = [st.ps(f"hp{i}", [128, 4 * HT]) for i in range(2)]
        yp = [st.ps(f"yp{i}", [HT, 4, D]) for i in range(2)]
        s_in = st.sem("loaded")
        s_x = st.sem("x_loaded")
        s_up = st.sem("up_done")
        s_a = st.sem("act_done")
        s_dn = st.sem("down_done")
        s_y = st.sem("y_ready")
        s_out = st.sem("stored")
        with st.step() as block:
            @block.sync
            def _(sp):
                sp.dma_start(up[:], sw1[:, :]).then_inc(s_in, 16)
                sp.dma_start(dn[:], sw2.rearrange("(c p) d -> p c d", p=128)).then_inc(s_in, 16)
                sp.dma_start(bu[:], sb1.rearrange("(c p) -> p c", p=128), allow_slow_non_contiguous=True).then_inc(s_in, 16)
                sp.dma_start(bd[:], sb2.rearrange("(a d) -> a d", a=1)).then_inc(s_in, 16)
                sp.wait_ge(s_in, 64)

            @block.vector
            def _(dve):
                nc.vector.memset(onerow[:], 1.0).then_inc(s_y, 1)
                dve.wait_ge(s_y, 1)
        hv, ov = tiles_of(h), tiles_of(h_out)
        with nc.Fori(0, NT // CT) as i, st.step() as block:
            @block.sync
            def _(sp):
                sp.dma_start(xT[:], xnT[:, bass.ds(i * (CT * HT), CT * HT)]).then_inc(s_x, 16)
                for k in range(NBI):
                    sp.dma_start(ht[:, 2 * k:2 * k + 2, :], hv[i * NBI + k]).then_inc(s_in, 16)
                for g in range(2):
                    sp.wait_ge(s_y, g + 1)
                    for k in range(2):
                        sp.dma_start(ov[i * NBI + 2 * g + k], ht[:, 4 * g + 2 * k:4 * g + 2 * k + 2, :]).then_inc(s_out, 16)
                sp.wait_ge(s_out, 64)

            @block.tensor
            def _(pe):
                pe.wait_ge(s_x, 16)
                for k in range(2):
                    for f in range(FC):
                        if k * FC + f >= 2:
                            pe.wait_ge(s_a, k * FC + f - 1)
                        nc.tensor.matmul(hp[f % 2][:], up[:, f * 128:(f + 1) * 128], xT[:, k * 4 * HT:(k + 1) * 4 * HT],
                                         start=True, stop=True).then_inc(s_up, 1)
                    pe.wait_ge(s_a, (k + 1) * FC)
                    for t in range(4):
                        for f in range(FC):
                            nc.tensor.matmul(yp[k][:, t, :], a[k][:, f, t * HT:(t + 1) * HT], dn[:, f, :], start=(f == 0), stop=False)
                        ins = nc.tensor.matmul(yp[k][:, t, :], onerow[:], bd[:], start=False, stop=True)
                    ins.then_inc(s_dn, 1)

            @block.scalar
            def _(act):
                for k in range(2):
                    for f in range(FC):
                        act.wait_ge(s_up, k * FC + f + 1)
                        nc.scalar.activation(a[k][:, f, :], hp[f % 2][:], ACT.Gelu_apprx_tanh, bias=bu[:, f:f + 1]).then_inc(s_a, 1)

            @block.vector
            def _(dve):
                dve.wait_ge(s_in, 64)
                for k in range(2):
                    dve.wait_ge(s_dn, k + 1)
                    t = ht[:, 4 * k:4 * k + 4, :]
                    nc.vector.tensor_tensor(t, t, yp[k][:], ALU.add).then_inc(s_y, 1)


NH = 8
HD = D // NH
DT = 0.1
US = 6


def turn_weights_stage(nc, c, name, weights, dst):
    n = len(weights)
    with Stage(nc, name) as st:
        w = st.sb("w", [D, n, D])
        wt = st.sb("wt", [D, n, D])
        tp = [st.ps(f"tp{i}", [D, 4, D]) for i in range(2)]
        s_in = st.sem("loaded")
        s_tp = st.sem("transposed")
        s_cp = st.sem("copied")
        s_out = st.sem("stored")
        with st.step() as block:
            @block.sync
            def _(sp):
                for k, x in enumerate(weights):
                    sp.dma_start(w[:, k, :], x[:, :]).then_inc(s_in, 16)
                sp.wait_ge(s_cp, n)
                sp.dma_start(dst.rearrange("n p d -> p n d"), wt[:]).then_inc(s_out, 16)
                sp.wait_ge(s_out, 16)

            @block.tensor
            def _(pe):
                pe.wait_ge(s_in, 16 * n)
                for k in range(n):
                    if k >= 2:
                        pe.wait_ge(s_cp, k - 1)
                    nc.tensor.transpose(tp[k % 2][:, 0, :], w[:, k, :], c.ident[:]).then_inc(s_tp, 1)

            @block.vector
            def _(dve):
                for k in range(n):
                    dve.wait_ge(s_tp, k + 1)
                    nc.vector.tensor_copy(wt[:, k, :], tp[k % 2][:, 0, :]).then_inc(s_cp, 1)


def liquid_stage(nc, c, xnT, wt, li_tau, li_b, liqT):
    with Stage(nc, "liquid") as st:
        S = st.sb("S", [D, B, T])
        x = [st.sb(f"x{i}", [D, 2 * T]) for i in range(2)]
        ab = st.sb("ab", [D, B, T])
        w = st.sb("w", [D, 3, D])
        cols = st.sb("cols", [D, 2])
        tau = st.sb("tau", [D, T])
        t1 = st.sb("t1", [D, T])
        a = [st.sb(f"a{i}", [D, B]) for i in range(2)]
        p = [st.sb(f"p{i}", [D, B]) for i in range(2)]
        hc = st.sb("hc", [D, B])
        pp = [st.ps(f"pp{i}", [D, 512]) for i in range(2)]
        s_in = st.sem("loaded")
        s_own = st.sem("own")
        s_mm = st.sem("multiplied")
        s_cp = st.sem("copied")
        s_act = st.sem("act")
        s_p = st.sem("decayed_state")
        s_h = st.sem("state")
        s_out = st.sem("stored")
        V = nc.vector
        with st.step() as block:
            @block.sync
            def _(sp):
                sp.dma_start(w[:, 0:2, :], wt[0:2].rearrange("n p d -> p n d")).then_inc(s_in, 16)
                sp.dma_start(cols[:, 0:1], li_tau.rearrange("(p a) -> p a", a=1)).then_inc(s_in, 16)
                sp.dma_start(cols[:, 1:2], li_b.rearrange("(p a) -> p a", a=1)).then_inc(s_in, 16)
                sp.wait_ge(s_in, 48)

            @block.vector
            def _(dve):
                own = Chain(dve, s_own)
                dve.wait_ge(s_in, 48)
                own(V.tensor_scalar(w[:, 2, :], w[:, 1, :], DT, None, ALU.mult))
                for z in (a[1], p[1], hc):
                    own(V.memset(z[:], 0.0))

        with nc.Fori(0, B // 4) as i, st.step() as block:
            @block.sync
            def _(sp):
                for k in range(2):
                    sp.dma_start(x[k][:], xnT[:, bass.ds(i * (4 * T) + k * 2 * T, 2 * T)]).then_inc(s_in, 16)

            @block.tensor
            def _(pe):
                pe.wait_ge(s_in, 32)
                for k in range(2):
                    nc.tensor.matmul(pp[k][:, 0:2 * T], w[:, 0, :], x[k][:], start=True, stop=True).then_inc(s_mm, 1)

            @block.vector
            def _(dve):
                for k in range(2):
                    dve.wait_ge(s_mm, k + 1)
                    V.tensor_copy(S[:, bass.ds(i * 4 + 2 * k, 2), :], pp[k][:, 0:2 * T].rearrange("p (b t) -> p b t", b=2)).then_inc(s_cp, 1)
                dve.wait_ge(s_cp, 2)

        with st.step() as block:
            @block.scalar
            def _(act):
                nc.scalar.activation(ab[:], S[:], ACT.Abs).then_inc(s_act, 1)
                act.wait_ge(s_p, 1)
                nc.scalar.activation(t1[:], t1[:], ACT.Exp).then_inc(s_act, 1)
                act.wait_ge(s_act, 2)
                nc.scalar.activation(t1[:], t1[:], ACT.Ln, bias=1.0).then_inc(s_act, 1)

            @block.vector
            def _(dve):
                own = Chain(dve, s_own)
                dve.wait_ge(s_act, 1)
                own(V.tensor_reduce(tau[:], ab[:].rearrange("p b t -> p t b"), AX.X, ALU.add))
                own(V.tensor_scalar(tau[:], tau[:], 0.1 / B, cols[:, 0:1], ALU.mult, ALU.add))
                own(V.tensor_scalar(t1[:], tau[:], -1.0, None, ALU.mult))
                V.tensor_tensor(t1[:], tau[:], t1[:], ALU.min).then_inc(s_p, 1)
                dve.wait_ge(s_act, 3)
                own(V.scalar_tensor_tensor(tau[:], tau[:], 0.0, t1[:], ALU.max, ALU.add))
                own(V.reciprocal(tau[:], tau[:]))
                own(V.tensor_scalar(tau[:], tau[:], -DT, 1.0, ALU.mult, ALU.add))

        col = lambda t: S[:, :, t].rearrange("p b a -> p (b a)")
        with nc.Fori(0, T // US) as i, st.step() as block:
            @block.tensor
            def _(pe):
                for k in range(US):
                    nc.tensor.matmul(pp[k % 2][:, 0:B], c.ident[:], col(bass.ds(i * US + k, 1)), start=True, stop=False)
                    if k >= 1:
                        pe.wait_ge(s_p, k)
                    nc.tensor.matmul(pp[k % 2][:, 0:B], w[:, 1, :], p[(k + 1) % 2][:], start=False, stop=False)
                    if k >= 1:
                        pe.wait_ge(s_act, k)
                    nc.tensor.matmul(pp[k % 2][:, 0:B], w[:, 2, :], a[(k + 1) % 2][:], start=False, stop=True).then_inc(s_mm, 1)

            @block.scalar
            def _(act):
                for k in range(US):
                    act.wait_ge(s_mm, k + 1)
                    if k >= 2:
                        act.wait_ge(s_h, k - 1)
                    nc.scalar.activation(a[k % 2][:], pp[k % 2][:, 0:B], ACT.Tanh, bias=cols[:, 1:2]).then_inc(s_act, 1)

            @block.vector
            def _(dve):
                for k in range(US):
                    t = bass.ds(i * US + k, 1)
                    if k >= 1:
                        dve.wait_ge(s_cp, k)
                        dve.wait_ge(s_mm, k)
                    V.tensor_scalar(p[k % 2][:], hc[:], tau[:, t], None, ALU.mult).then_inc(s_p, 1)
                    dve.wait_ge(s_p, k + 1)
                    dve.wait_ge(s_act, k + 1)
                    V.scalar_tensor_tensor(hc[:], a[k % 2][:], DT, p[k % 2][:], ALU.mult, ALU.add).then_inc(s_cp, 1)
                    dve.wait_ge(s_cp, k + 1)
                    V.tensor_copy(col(t), hc[:]).then_inc(s_h, 1)
                dve.wait_ge(s_h, US)

        with st.step() as block:
            @block.sync
            def _(sp):
                lv = liqT.rearrange("p (b t) -> p b t", b=B)
                for k in range(8):
                    sp.dma_start(lv[:, 8 * k:8 * k + 8, :], S[:, 8 * k:8 * k + 8, :]).then_inc(s_out, 16)
                sp.wait_ge(s_out, 16 * 8)


def mix_weights_stage(nc, c, xnT, W1, b1, W2, b2, fusion, wgt):
    R = D // 4
    with Stage(nc, "mixw") as st:
        x = st.sb("x", [D, B, T])
        m = st.sb("m", [D, B])
        w1 = st.sb("w1", [R, D])
        w2 = st.sb("w2", [3, R])
        w1T = st.sb("w1T", [D, R])
        w2T = st.sb("w2T", [R, 3])
        b1c = st.sb("b1c", [R, 1])
        r1 = st.sb("r1", [R, B])
        rows = st.sb("rows", [B, 2, 3])
        z = st.sb("z", [B, 2, 3])
        red = st.sb("red", [B, 2])
        p = [st.ps(f"p{i}", [128, 512]) for i in range(4)]
        s_in = st.sem("loaded")
        s_own = st.sem("own")
        s_mm = st.sem("multiplied")
        s_x = st.sem("ready")
        s_act = st.sem("act")
        s_out = st.sem("stored")
        V = nc.vector
        with st.step() as block:
            @block.sync
            def _(sp):
                sp.dma_start(w1[:], W1[:, :]).then_inc(s_in, 16)
                sp.dma_start(w2[:], W2[:, :]).then_inc(s_in, 16)
                sp.dma_start(b1c[:], b1.rearrange("(p a) -> p a", a=1)).then_inc(s_in, 16)
                sp.dma_start(rows[:, 0, :], wide(b2, B)).then_inc(s_in, 16)
                sp.dma_start(rows[:, 1, :], wide(fusion, B)).then_inc(s_in, 16)
                xv = xnT.rearrange("p (b t) -> p b t", b=B)
                for k in range(8):
                    sp.dma_start(x[:, 8 * k:8 * k + 8, :], xv[:, 8 * k:8 * k + 8, :]).then_inc(s_in, 16)
                sp.wait_ge(s_x, 6)
                sp.dma_start(wgt[:, :], z[:, 0, :]).then_inc(s_out, 16)
                sp.wait_ge(s_out, 16)

            @block.tensor
            def _(pe):
                pe.wait_ge(s_in, 16 * 13)
                nc.tensor.transpose(p[0][:, 0:R], w1[:], c.ident[0:R, 0:R]).then_inc(s_mm, 1)
                nc.tensor.transpose(p[1][0:R, 0:3], w2[:], c.ident[0:3, 0:3]).then_inc(s_mm, 1)
                pe.wait_ge(s_x, 3)
                nc.tensor.matmul(p[2][0:R, 0:B], w1T[:], m[:], start=True, stop=True).then_inc(s_mm, 1)
                pe.wait_ge(s_x, 4)
                nc.tensor.matmul(p[3][0:B, 0:3], r1[:], w2T[:], start=True, stop=True).then_inc(s_mm, 1)

            @block.vector
            def _(dve):
                own = Chain(dve, s_own)
                dve.wait_ge(s_in, 16 * 13)
                own(V.tensor_reduce(m[:], x[:], AX.X, ALU.add))
                V.tensor_scalar(m[:], m[:], 1.0 / T, None, ALU.mult).then_inc(s_x, 1)
                dve.wait_ge(s_mm, 2)
                V.tensor_copy(w1T[:], p[0][:, 0:R]).then_inc(s_x, 1)
                V.tensor_copy(w2T[:], p[1][0:R, 0:3]).then_inc(s_x, 1)
                dve.wait_ge(s_mm, 3)
                V.tensor_scalar(r1[:], p[2][0:R, 0:B], b1c[:, 0:1], 0.0, ALU.add, ALU.max).then_inc(s_x, 1)
                dve.wait_ge(s_mm, 4)
                own(V.tensor_tensor(z[:, 0, :], p[3][0:B, 0:3], rows[:, 0, :], ALU.add))
                own(V.tensor_copy(z[:, 1, :], rows[:, 1, :]))
                own(V.tensor_reduce(red[:], z[:], AX.X, ALU.max))
                V.tensor_tensor(z[:], z[:], red[:].unsqueeze(2).to_broadcast([B, 2, 3]), ALU.subtract).then_inc(s_x, 1)
                dve.wait_ge(s_act, 1)
                own(V.tensor_reduce(red[:], z[:], AX.X, ALU.add))
                own(V.reciprocal(red[:], red[:]))
                own(V.tensor_tensor(z[:], z[:], red[:].unsqueeze(2).to_broadcast([B, 2, 3]), ALU.mult))
                V.tensor_tensor(z[:, 0, :], z[:, 0, :], z[:, 1, :], ALU.mult).then_inc(s_x, 1)

            @block.scalar
            def _(act):
                act.wait_ge(s_x, 5)
                nc.scalar.activation(z[:], z[:], ACT.Exp).then_inc(s_act, 1)


def head_masks(pool, nc, own, headmask, blockmask=None):
    P = nc.gpsimd
    for m, wd in ((headmask, 1),) + (((blockmask, HD),) if blockmask is not None else ()):
        v = m[:].rearrange("p (h d) -> p h d", h=NH)
        own(P.memset(m[:], 1.0))
        own(P.affine_select(out=v, in_=v, compare_op=ALU.is_ge, fill=0.0, base=0, pattern=[[-HD, NH], [0, wd]], channel_multiplier=1))
        own(P.affine_select(out=v, in_=v, compare_op=ALU.is_ge, fill=0.0, base=HD - 1, pattern=[[HD, NH], [0, wd]], channel_multiplier=-1))


def retention_stage(nc, c, xnT, liqT, wt, vecs, theta, wgt, h, h_out):
    with Stage(nc, "ret") as st:
        w = st.sb("w", [D, 9, D])
        WOUT, RQ, RK, RV, RO, LQ, LK, LV, LO = range(9)
        gnw, gnb, rbo, lbq, lbk, lbv, lbo, lnw, lnb = vecs
        wv = st.sb("wv", [HT, 4, D])
        br = st.sb("br", [1, 4, D])
        bq = st.sb("bq", [D, 1])
        th = st.sb("th", [HT, NH])
        ones = st.sb("ones", [HT, HT])
        diff = st.sb("diff", [HT, 2, T])
        dm = st.sb("dm", [HT, 2, T])
        ng = st.sb("ng", [HT, 2, T])
        hm = st.sb("hm", [D, NH])
        bm = st.sb("bm", [D, D])
        eps = st.sb("eps", [HT, 1])
        x = st.sb("x", [D, T])
        lq = st.sb("lq", [D, T])
        hb = st.sb("hb", [HT, 2, D])
        mw = st.sb("mw", [HT, 3])
        QM = st.sb("QM", [D, NH, T])
        KT = st.sb("KT", [D, T])
        Vt = st.sb("Vt", [HT, 2, D])
        q2 = st.sb("q2", [D, T])
        e2 = st.sb("e2", [D, T])
        k2 = st.sb("k2", [HT, 2, D])
        f2 = st.sb("f2", [HT, 2, D])
        v2 = st.sb("v2", [HT, 2, D])
        kv = st.sb("kv", [D, D])
        ks = st.sb("ks", [D, NH])
        lin = st.sb("lin", [HT, 2, D])
        den = st.sb("den", [HT, 2, NH])
        sc = [st.sb(f"sc{i}", [HT, NH, HT * (i + 1)]) for i in range(2)]
        mx = st.sb("mx", [HT, 2, NH])
        rs = st.sb("rs", [HT, 2, NH])
        ri = st.sb("ri", [HT, 2, NH])
        PT = st.sb("PT", [HT, NH, 2, HT])
        ret = st.sb("ret", [HT, 2, D])
        sq = st.sb("sq", [HT, 2, D])
        gm = st.sb("gm", [HT, 2, NH])
        oT = st.sb("oT", [D, 4, HT])
        fu = st.sb("fu", [HT, 2, D])
        stt = st.sb("stt", [HT, 2, 6])
        mv = st.sb("mv", [HT, 2, 2])
        sd = st.sb("sd", [HT, 2])
        scp = st.ps("scp", [HT, 4, 512])
        gp = [st.ps(f"gp{i}", [128, 512]) for i in range(2)]
        tp = [st.ps(f"tp{i}", [HT, 4, 128]) for i in range(2)]
        s_w = st.sem("weights")
        s_own = st.sem("own")
        s_po = st.sem("pool_own")
        s_in = st.sem("loaded")
        s_hb = st.sem("h_loaded")
        s_g = st.sem("product_done")
        s_e = st.sem("product_read")
        s_sc = st.sem("scores_done")
        s_mx = st.sem("max_ready")
        s_ex = st.sem("exp_done")
        s_el = st.sem("elu_args")
        s_el2 = st.sem("elu_exp")
        s_q2 = st.sem("elu_done")
        s_tp = st.sem("p_transposed")
        s_pt = st.sem("p_copied")
        s_rt = st.sem("branches_ready")
        s_vr = st.sem("variances")
        s_sd = st.sem("roots")
        s_out = st.sem("stored")
        V = nc.vector
        tmp_ = lambda k: QM[0:HT, 2 * (k % 2):2 * (k % 2) + 2, :]

        with st.step() as block:
            @block.sync
            def _(sp):
                sp.dma_start(w[:], wt[2:11].rearrange("n p d -> p n d")).then_inc(s_w, 16)
                for k, v in enumerate((gnw, gnb, lnw, lnb)):
                    sp.dma_start(wv[:, k, :], wide(v, HT)).then_inc(s_w, 16)
                for k, v in enumerate((rbo, lbk, lbv, lbo)):
                    sp.dma_start(br[:, k, :], v.rearrange("(a d) -> a d", a=1)).then_inc(s_w, 16)
                sp.dma_start(bq[:], lbq.rearrange("(p a) -> p a", a=1)).then_inc(s_w, 16)
                sp.dma_start(th[:], wide(theta, HT)).then_inc(s_w, 16)
                sp.wait_ge(s_w, 16 * 11)

            @block.gpsimd
            def _(pool):
                own = Chain(pool, s_po)
                P = nc.gpsimd
                own(P.iota(diff[:], pattern=[[HT, 2], [-1, T]], base=0, channel_multiplier=1, allow_small_or_imprecise_dtypes=True))
                P.memset(ones[:], 1.0).then_inc(s_in, 1)
                head_masks(pool, nc, own, hm, bm)
                own(P.memset(ng[:], 0.0))
                own(P.affine_select(out=ng[:], in_=ng[:], compare_op=ALU.is_ge, fill=-1e30, base=0,
                                    pattern=[[HT, 2], [-1, T]], channel_multiplier=1))
                pool.wait_ge(s_ex, 1)
                own(P.affine_select(out=dm[:], in_=dm[:], compare_op=ALU.is_ge, fill=0.0, base=0,
                                    pattern=[[HT, 2], [-1, T]], channel_multiplier=1))
                pool.wait_ge(s_in, 1)

            @block.vector
            def _(dve):
                own = Chain(dve, s_own)
                own(V.memset(eps[:], EPS))
                dve.wait_ge(s_w, 16 * 11)
                own(V.tensor_scalar(th[:], th[:], -1.0, None, ALU.mult))
                dve.wait_ge(s_po, 1)
                V.tensor_scalar(diff[:], diff[:], 0.0, None, ALU.max).then_inc(s_mx, 1)
                for k in range(NH):
                    dve.wait_ge(s_e, k + 1)
                    if k == 0:
                        ins = V.tensor_copy(dm[:], tmp_(0))
                    else:
                        ins = V.tensor_tensor(dm[:], dm[:], tmp_(k), ALU.add)
                    own(ins)
                    V.engine_nop().then_inc(s_g, 1)
                V.tensor_scalar(dm[:], dm[:], 1.0 / NH / HD ** 0.5, None, ALU.mult).then_inc(s_ex, 1)

            @block.scalar
            def _(act):
                act.wait_ge(s_mx, 1)
                for k in range(NH):
                    if k >= 2:
                        act.wait_ge(s_g, k - 1)
                    nc.scalar.activation(tmp_(k), diff[:], ACT.Exp, scale=th[:, k:k + 1]).then_inc(s_e, 1)

        hv, ov = tiles_of(h), tiles_of(h_out)
        with nc.Fori(0, B) as b, st.step() as block:
            @block.sync
            def _(sp):
                sp.dma_start(x[:], xnT[:, bass.ds(b * T, T)]).then_inc(s_in, 16)
                sp.dma_start(lq[:], liqT[:, bass.ds(b * T, T)]).then_inc(s_hb, 16)
                sp.dma_start(hb[:], hv[b]).then_inc(s_hb, 16)
                sp.dma_start(mw[:], bass.AP(wgt.tensor, 0, [[3, B], [0, HT], [1, 3]])[b]).then_inc(s_hb, 16)
                sp.wait_ge(s_rt, 2)
                sp.dma_start(ov[b], hb[:]).then_inc(s_out, 16)
                sp.wait_ge(s_out, 16)

            @block.tensor
            def _(pe):
                n = [0]

                def job(fn):
                    k = n[0]
                    if k >= 2:
                        pe.wait_ge(s_e, k - 1)
                    fn(gp[k % 2]).then_inc(s_g, 1)
                    n[0] += 1

                def mm(o, l, r, first=True, last=True):
                    return nc.tensor.matmul(o, l, r, start=first, stop=last)

                def tokens(wi, bias):
                    def fn(p):
                        for k in range(2):
                            o = p[0:HT, k * D:(k + 1) * D]
                            ins = mm(o, x[:, k * HT:(k + 1) * HT], w[:, wi, :], True, bias is None)
                            if bias is not None:
                                ins = mm(o, ones[0:1, :], br[:, bias, :], False, True)
                        return ins
                    return fn

                def scores(f):
                    if f:
                        pe.wait_ge(s_mx, 1)
                    for hd in range(NH):
                        ins = mm(scp[:, hd // 2, (hd % 2) * T:(hd % 2) * T + HT * (f + 1)],
                                 QM[:, hd, f * HT:(f + 1) * HT], KT[:, 0:HT * (f + 1)])
                    ins.then_inc(s_sc, 1)

                def turn(f):
                    n0 = 0 if f == 0 else 2
                    for m in range(NH * (f + 1) // 4):
                        if n0 + m >= 2:
                            pe.wait_ge(s_pt, n0 + m - 1)
                        for r in range(4):
                            hd, sh = divmod(4 * m + r, f + 1)
                            pe.wait_ge(s_ex, f * NH + hd + 1)
                            nc.tensor.transpose(tp[m % 2][:, r, 0:HT], sc[f][:, hd, sh * HT:(sh + 1) * HT],
                                                c.ident[0:HT, 0:HT]).then_inc(s_tp, 1)

                def pv(f):
                    def fn(p):
                        pe.wait_ge(s_pt, 2 if f == 0 else 6)
                        for hd in range(NH):
                            for sh in range(f + 1):
                                ins = mm(p[0:HT, hd * HD:(hd + 1) * HD], PT[:, hd, sh, :], Vt[:, sh, hd * HD:(hd + 1) * HD],
                                         sh == 0, sh == f)
                        return ins
                    return fn

                pe.wait_ge(s_in, 16)
                job(lambda p: mm(p[:, 0:T], w[:, RQ, :], x[:]))
                job(lambda p: mm(p[:, 0:T], w[:, RK, :], x[:]))
                job(tokens(RV, None))
                pe.wait_ge(s_e, 2)
                scores(0)
                job(lambda p: mm(p[:, 0:T], w[:, LQ, :], x[:]))
                job(tokens(LK, 1))
                job(tokens(LV, 2))
                turn(0)
                pe.wait_ge(s_e, 3)
                job(pv(0))
                scores(1)
                pe.wait_ge(s_q2, 2)
                pe.wait_ge(s_e, 6)

                def kvs(p):
                    for k in range(2):
                        mm(p[:, 0:D], k2[:, k, :], v2[:, k, :], k == 0, k == 1)
                    for k in range(2):
                        ins = mm(p[:, D:D + 1], k2[:, k, :], ones[:, 0:1], k == 0, k == 1)
                    return ins
                job(kvs)
                pe.wait_ge(s_e, 8)

                def numden(p):
                    for k in range(2):
                        mm(p[0:HT, k * D:(k + 1) * D], q2[:, k * HT:(k + 1) * HT], kv[:])
                        ins = mm(p[0:HT, 256 + k * NH:256 + (k + 1) * NH], q2[:, k * HT:(k + 1) * HT], ks[:])
                    return ins
                job(numden)
                turn(1)
                job(pv(1))
                pe.wait_ge(s_rt, 1)

                def turn_out(p):
                    for k in range(2):
                        nc.tensor.transpose(p[:, k * 128:k * 128 + HT], ret[:, k, :], c.ident[0:HT, 0:HT])
                    for k in range(2):
                        ins = nc.tensor.transpose(p[:, (2 + k) * 128:(2 + k) * 128 + HT], lin[:, k, :], c.ident[0:HT, 0:HT])
                    return ins
                job(turn_out)
                pe.wait_ge(s_e, 11)
                pe.wait_ge(s_hb, 48)

                def outs(p):
                    for k in range(2):
                        mm(p[0:HT, k * D:(k + 1) * D], lq[:, k * HT:(k + 1) * HT], w[:, WOUT, :])
                    for k in range(2):
                        o = p[0:HT, (2 + k) * D:(3 + k) * D]
                        mm(o, oT[:, k, :], w[:, RO, :], True, False)
                        ins = mm(o, ones[0:1, :], br[:, 0, :], False, True)
                    return ins
                job(outs)

                def outl(p):
                    for k in range(2):
                        o = p[0:HT, k * D:(k + 1) * D]
                        mm(o, oT[:, 2 + k, :], w[:, LO, :], True, False)
                        ins = mm(o, ones[0:1, :], br[:, 3, :], False, True)
                    return ins
                job(outl)

            @block.vector
            def _(dve):
                own = Chain(dve, s_own)

                def read(k, ins):
                    ins.then_inc(s_e, 1)
                    dve.wait_ge(s_e, k)

                def soft(f):
                    dve.wait_ge(s_sc, f + 1)
                    wd = HT * (f + 1)
                    sv = sc[f][:].rearrange("p (a c) s -> p a c s", c=2)
                    pv = scp[:, :, 0:2 * T].rearrange("p a (c s) -> p a c s", c=2)[:, :, :, 0:wd]
                    own(V.tensor_tensor(sv, pv, dm[:, f, None, None, 0:wd].to_broadcast([HT, 4, 2, wd]), ALU.mult))
                    own(V.tensor_tensor(sc[f][:], sc[f][:], ng[:, f, None, 0:wd].to_broadcast([HT, NH, wd]), ALU.add))
                    own(V.tensor_reduce(mx[:, f, :], sc[f][:], AX.X, ALU.max))
                    V.tensor_scalar(mx[:, f, :], mx[:, f, :], -1.0, None, ALU.mult).then_inc(s_mx, 1)

                def heads(f, k, src):
                    p = gp[(k - 1) % 2]
                    dve.wait_ge(s_g, k)
                    own(V.reciprocal(ri[:, f, :], rs[:, f, :]))
                    read(k, V.tensor_tensor(ret[:, f, :].rearrange("p (h d) -> p h d", h=NH), p[0:HT, 0:D].rearrange("p (h d) -> p h d", h=NH),
                                            ri[:, f, :].unsqueeze(2).to_broadcast([HT, NH, HD]), ALU.mult))

                dve.wait_ge(s_g, 1)
                read(1, V.tensor_tensor(QM[:], gp[0][:, None, 0:T].to_broadcast([D, NH, T]),
                                        hm[:].unsqueeze(2).to_broadcast([D, NH, T]), ALU.mult))
                dve.wait_ge(s_g, 2)
                read(2, V.tensor_copy(KT[:], gp[1][:, 0:T]))
                dve.wait_ge(s_g, 3)
                read(3, V.tensor_copy(Vt[:].rearrange("p a d -> p (a d)"), gp[0][0:HT, 0:2 * D]))
                soft(0)
                dve.wait_ge(s_g, 4)
                read(4, V.tensor_scalar(q2[:], gp[1][:, 0:T], bq[:, 0:1], None, ALU.add))
                V.tensor_scalar(e2[:], q2[:], 0.0, None, ALU.min).then_inc(s_el, 1)
                dve.wait_ge(s_g, 5)
                read(5, V.tensor_copy(k2[:].rearrange("p a d -> p (a d)"), gp[0][0:HT, 0:2 * D]))
                V.tensor_scalar(f2[:], k2[:], 0.0, None, ALU.min).then_inc(s_el, 1)
                dve.wait_ge(s_g, 6)
                read(6, V.tensor_copy(v2[:].rearrange("p a d -> p (a d)"), gp[1][0:HT, 0:2 * D]))
                dve.wait_ge(s_el2, 2)
                V.scalar_tensor_tensor(q2[:], q2[:], 0.0, e2[:], ALU.max, ALU.add).then_inc(s_q2, 1)
                V.scalar_tensor_tensor(k2[:], k2[:], 0.0, f2[:], ALU.max, ALU.add).then_inc(s_q2, 1)
                heads(0, 7, 0)
                soft(1)
                dve.wait_ge(s_g, 8)
                own(V.tensor_scalar(ks[:], hm[:], gp[1][:, D:D + 1], None, ALU.mult))
                read(8, V.tensor_tensor(kv[:], bm[:], gp[1][:, 0:D], ALU.mult))
                dve.wait_ge(s_g, 9)
                own(V.tensor_scalar(den[:].rearrange("p a h -> p (a h)"), gp[0][0:HT, 256:256 + 2 * NH], 1e-8, None, ALU.add))
                own(V.reciprocal(den[:], den[:]))
                read(9, V.tensor_tensor(lin[:].rearrange("p a (h d) -> p (a h) d", h=NH),
                                        gp[0][0:HT, 0:2 * D].rearrange("p (a d) -> p a d", d=HD),
                                        den[:].rearrange("p a h -> p (a h)").unsqueeze(2).to_broadcast([HT, 2 * NH, HD]), ALU.mult))
                heads(1, 10, 1)
                rh = ret[:].rearrange("p a (h d) -> p (a h) d", h=NH)
                sh = sq[:].rearrange("p a (h d) -> p (a h) d", h=NH)
                gh = gm[:].rearrange("p a h -> p (a h)")
                gb = gh.unsqueeze(2).to_broadcast([HT, 2 * NH, HD])
                own(V.tensor_reduce(gh, rh, AX.X, ALU.add))
                own(V.tensor_scalar(gh, gh, 1.0 / HD, None, ALU.mult))
                own(V.tensor_tensor(rh, rh, gb, ALU.subtract))
                own(V.tensor_tensor(sh, rh, rh, ALU.mult))
                V.tensor_reduce(gh, sh, AX.X, ALU.add).then_inc(s_vr, 1)
                dve.wait_ge(s_sd, 1)
                own(V.reciprocal(gh, gh))
                own(V.tensor_tensor(rh, rh, gb, ALU.mult))
                vb = lambda k: wv[:, k, None, :].to_broadcast([HT, 2, D])
                own(V.tensor_tensor(ret[:], ret[:], vb(0), ALU.mult))
                V.tensor_tensor(ret[:], ret[:], vb(1), ALU.add).then_inc(s_rt, 1)
                dve.wait_ge(s_g, 11)
                read(11, V.tensor_copy(oT[:], gp[0][:, 0:512].rearrange("p (a t) -> p a t", a=4)[:, :, 0:HT]))
                dve.wait_ge(s_hb, 48)
                dve.wait_ge(s_g, 12)
                f = lambda t: t[:].rearrange("p a d -> p (a d)")
                own(V.tensor_scalar(f(fu), gp[1][0:HT, 0:256], mw[:, 0:1], None, ALU.mult))
                read(12, V.scalar_tensor_tensor(f(fu), gp[1][0:HT, 256:512], mw[:, 1:2], f(fu), ALU.mult, ALU.add))
                dve.wait_ge(s_g, 13)
                read(13, V.scalar_tensor_tensor(f(fu), gp[0][0:HT, 0:256], mw[:, 2:3], f(fu), ALU.mult, ALU.add))
                for k in range(2):
                    own(V.bn_stats(stt[:, k, :], fu[:, k, :]))
                    own(V.bn_aggr(mv[:, k, :], stt[:, k, :]))
                V.engine_nop().then_inc(s_vr, 1)
                dve.wait_ge(s_sd, 2)
                own(V.reciprocal(sd[:], sd[:]))
                for k in range(2):
                    own(V.tensor_scalar(fu[:, k, :], fu[:, k, :], mv[:, k, 0:1], sd[:, k:k + 1], ALU.subtract, ALU.mult))
                own(V.tensor_tensor(fu[:], fu[:], vb(2), ALU.mult))
                own(V.tensor_tensor(fu[:], fu[:], vb(3), ALU.add))
                V.tensor_tensor(hb[:], hb[:], fu[:], ALU.add).then_inc(s_rt, 1)

            @block.scalar
            def _(act):
                def exps(f):
                    act.wait_ge(s_mx, f + 1)
                    for hd in range(NH):
                        nc.scalar.activation(sc[f][:, hd, :], sc[f][:, hd, :], ACT.Exp, bias=mx[:, f, hd:hd + 1],
                                             accum_out=rs[:, f, hd:hd + 1]).then_inc(s_ex, 1)

                def copies(f):
                    n0 = 0 if f == 0 else 2
                    if f:
                        act.wait_ge(s_g, 7)
                    for m in range(NH * (f + 1) // 4):
                        act.wait_ge(s_tp, 4 * (n0 + m + 1))
                        if f == 0:
                            dst = PT[:, 4 * m:4 * m + 4, 0, :]
                        else:
                            dst = PT[:, 2 * m:2 * m + 2, :, :].rearrange("p a s t -> p (a s) t")
                        nc.scalar.activation(dst, tp[m % 2][:, :, 0:HT], ACT.Copy).then_inc(s_pt, 1)

                exps(0)
                act.wait_ge(s_el, 2)
                nc.scalar.activation(e2[:], e2[:], ACT.Exp).then_inc(s_el2, 1)
                nc.scalar.activation(f2[:], f2[:], ACT.Exp).then_inc(s_el2, 1)
                copies(0)
                exps(1)
                copies(1)
                act.wait_ge(s_vr, 1)
                nc.scalar.activation(gm[:], gm[:], ACT.Sqrt, bias=eps[:, 0:1], scale=1.0 / HD).then_inc(s_sd, 1)
                act.wait_ge(s_vr, 2)
                nc.scalar.activation(sd[:], mv[:, :, 1], ACT.Sqrt, bias=eps[:, 0:1]).then_inc(s_sd, 1)


FH = 8
FD = 64
SL = B
LEV = 6
PROJ = FH * (5 * FD + 2)
KW = FH * FD


def slow_weights_stage(nc, c, W, dst, Wout, dst_out):
    NR = 5 * KW // 128
    with Stage(nc, "slow") as st:
        w = st.sb("w", [128, NR + 1, D])
        wt = st.sb("wt", [D, NR + 1, 128])
        wo = st.sb("wo", [D, 4, 128])
        wot = st.sb("wot", [128, 4, D])
        tp = [st.ps(f"tp{i}", [D, 4, 128]) for i in range(2)]
        s_in = st.sem("loaded")
        s_tp = st.sem("transposed")
        s_cp = st.sem("copied")
        s_out = st.sem("stored")
        HR = 5 * FD + 2
        src_kind = [0, 1, 3, 2, 4]
        with st.step() as block:
            @block.sync
            def _(sp):
                for n in range(NR):
                    kind, hp = divmod(n, 4)
                    for a in range(2):
                        r = (2 * hp + a) * HR + src_kind[kind] * FD
                        sp.dma_start(w[a * FD:(a + 1) * FD, n, :], W[r:r + FD, :]).then_inc(s_in, 16)
                for hd in range(FH):
                    r = hd * HR + 5 * FD
                    sp.dma_start(w[2 * hd:2 * hd + 2, NR, :], W[r:r + 2, :]).then_inc(s_in, 16)
                sp.dma_start(wo[:], Wout.rearrange("o (c k) -> o c k", c=4)).then_inc(s_in, 16)
                sp.wait_ge(s_cp, NR + 5)
                sp.dma_start(dst[:, 0:5 * KW], wt[:, 0:NR, :].rearrange("p n k -> p (n k)")).then_inc(s_out, 16)
                sp.dma_start(dst[:, 5 * KW:PROJ], wt[:, NR, 0:2 * FH]).then_inc(s_out, 16)
                sp.dma_start(dst_out[:, :, :], wot[:]).then_inc(s_out, 16)
                sp.wait_ge(s_out, 48)

            @block.tensor
            def _(pe):
                pe.wait_ge(s_in, 16 * (2 * NR + FH + 1))
                for n in range(NR + 5):
                    if n >= 2:
                        pe.wait_ge(s_cp, n - 1)
                    if n < NR:
                        ins = nc.tensor.transpose(tp[n % 2][:, 0, :], w[:, n, :], c.ident[:])
                    elif n == NR:
                        ins = nc.tensor.transpose(tp[n % 2][:, 0, 0:2 * FH], w[0:2 * FH, n, :], c.ident[0:2 * FH, 0:2 * FH])
                    else:
                        ins = nc.tensor.transpose(tp[n % 2][:, 0, :], wo[:, n - NR - 1, :], c.ident[:])
                    ins.then_inc(s_tp, 1)

            @block.vector
            def _(dve):
                for n in range(NR + 5):
                    dve.wait_ge(s_tp, n + 1)
                    if n < NR:
                        ins = nc.vector.tensor_copy(wt[:, n, :], tp[n % 2][:, 0, :])
                    elif n == NR:
                        ins = nc.vector.tensor_copy(wt[:, n, 0:2 * FH], tp[n % 2][:, 0, 0:2 * FH])
                    else:
                        ins = nc.vector.tensor_copy(wot[:, n - NR - 1, :], tp[n % 2][:, 0, :])
                    ins.then_inc(s_cp, 1)


def delta_stage(nc, c, xT, wslow, kr, ur, zz):
    with Stage(nc, "delta") as st:
        X = st.sb("X", [D, SL, T])
        W = st.sb("W", [D, PROJ])
        xc = st.sb("xc", [D, 2, SL])
        QK = st.sb("QK", [128, 5, KW])
        sb_ = st.sb("sb", [128, FH, 2])
        mx = st.sb("mx", [128, 3 * FH])
        sm = st.sb("sm", [128, 3 * FH])
        KT = st.sb("KT", [128, 12, 128])
        maskL = st.sb("maskL", [128, 128])
        maskU = st.sb("maskU", [128, 128])
        maskZ = st.sb("maskZ", [128, 128])
        nl = [[st.sb(f"nl{k}{i}", [128, 4, 128]) for i in range(2)] for k in range(2)]
        nu = [[st.sb(f"nu{k}{i}", [128, 4, 128]) for i in range(2)] for k in range(2)]
        az = st.sb("az", [128, 4, 128])
        Z = st.sb("Z", [128, KW])
        gp = [st.ps(f"gp{i}", [128, 512]) for i in range(2)]
        pA = [st.ps(f"pA{k}", [128, 4, 128]) for k in range(2)]
        pB = [st.ps(f"pB{k}", [128, 4, 128]) for k in range(2)]
        pC = [st.ps(f"pC{k}", [128, 4, FD]) for k in range(2)]
        s_w = st.sem("weights")
        s_own = st.sem("own")
        s_x = st.sem("x_ready")
        s_g = st.sem("product_done")
        s_e = st.sem("product_read")
        s_be = st.sem("beta_ready")
        s_mx = st.sem("shifted")
        s_ex = st.sem("exp_done")
        s_k = st.sem("keys_ready")
        s_G = [st.sem(f"gram{k}") for k in range(2)]
        s_m = [st.sem(f"masked{k}") for k in range(2)]
        s_sq = [st.sem(f"squared{k}") for k in range(2)]
        s_n = [st.sem(f"power_ready{k}") for k in range(2)]
        s_c = [st.sem(f"applied{k}") for k in range(2)]
        s_u = [st.sem(f"u_ready{k}") for k in range(2)]
        s_z = st.sem("z_read")
        s_out = st.sem("stored")
        V = nc.vector
        NSQ = 2 * LEV - 3

        with st.step() as block:
            @block.sync
            def _(sp):
                xv = xT.rearrange("p (b t) -> p b t", b=B)
                for k in range(8):
                    sp.dma_start(X[:, 8 * k:8 * k + 8, :], xv[:, 8 * k:8 * k + 8, :]).then_inc(s_w, 16)
                sp.dma_start(W[:], wslow[:, :]).then_inc(s_w, 16)
                sp.wait_ge(s_w, 16 * 9)

            @block.gpsimd
            def _(pool):
                own = Chain(pool, s_own)
                P = nc.gpsimd
                own(P.memset(maskZ[:], 1.0))
                own(P.memset(maskZ[0:64, 64:128], 0.0))
                own(P.memset(maskZ[64:128, 0:64], 0.0))
                own(P.affine_select(out=maskU[:], in_=maskZ[:], compare_op=ALU.is_gt, fill=0.0, base=0,
                                    pattern=[[1, 128]], channel_multiplier=-1))
                own(P.affine_select(out=maskL[:], in_=maskZ[:], compare_op=ALU.is_gt, fill=0.0, base=0,
                                    pattern=[[-1, 128]], channel_multiplier=1))
                own(P.affine_select(out=maskZ[:], in_=maskZ[:], compare_op=ALU.is_ge, fill=0.0, base=0,
                                    pattern=[[1, 128]], channel_multiplier=-1))

        with nc.Fori(0, T // 2) as i, st.step() as block:
            @block.tensor
            def _(pe):
                n = [0]

                def job(fn):
                    k = n[0]
                    if k >= 2:
                        pe.wait_ge(s_e, k - 1)
                    fn(gp[k % 2]).then_inc(s_g, 1)
                    n[0] += 1

                def mm(o, l, r):
                    return nc.tensor.matmul(o, l, r, start=True, stop=True)

                pe.wait_ge(s_x, 1)
                xv = xc[:].rearrange("p a s -> p (a s)")
                job(lambda p: mm(p[:, 0:2 * FH], xv, W[:, 5 * KW:PROJ]))
                for kind in range(5):
                    job(lambda p: mm(p[:], xv, W[:, kind * KW:(kind + 1) * KW]))
                pe.wait_ge(s_k, 1)
                for kind in range(3):
                    def turn(p):
                        for m in range(4):
                            ins = nc.tensor.transpose(p[:, m * 128:(m + 1) * 128], QK[:, kind, m * 128:(m + 1) * 128], c.ident[:])
                        return ins
                    job(turn)
                pe.wait_ge(s_e, 9)
                kt = lambda kind, hd: KT[FD * (hd % 2):FD * (hd % 2) + FD, 4 * kind + hd // 2, :]
                for g in range(2):
                    for k in range(2):
                        for a in range(4):
                            ins = mm(pA[k][:, a, :], kt(1 + k, 2 * a + g), kt(1 + k, 2 * a + g))
                        ins.then_inc(s_G[k], 1)
                    for a in range(4):
                        ins = mm(pB[0][:, a, :], kt(1, 2 * a + g), kt(0, 2 * a + g))
                    ins.then_inc(s_G[0], 1)
                    for l in range(LEV):
                        for k in range(2):
                            if l == 0:
                                pe.wait_ge(s_m[k], (3 if k == 0 else 2) * (g + 1))
                                if g and k == 0:
                                    pe.wait_ge(s_z, 1)
                            else:
                                pe.wait_ge(s_n[k], NSQ * g + min(2 * l, NSQ))
                            pe.wait_ge(s_u[k], 1 + LEV * g + l)
                            for a in range(4):
                                hd = 2 * a + g
                                ins = mm(pC[k][:, a, :], nu[k][l % 2][:, a, :], QK[:, 3 + k, hd * FD:(hd + 1) * FD])
                            ins.then_inc(s_c[k], 1)
                            if l < LEV - 2:
                                for a in range(4):
                                    ins = mm(pA[k][:, a, :], nu[k][l % 2][:, a, :], nl[k][l % 2][:, a, :])
                                ins.then_inc(s_sq[k], 1)
                            if l < LEV - 1:
                                for a in range(4):
                                    ins = mm(pB[k][:, a, :], nl[k][l % 2][:, a, :], nu[k][l % 2][:, a, :])
                                ins.then_inc(s_sq[k], 1)
                    pe.wait_ge(s_u[0], 1 + LEV * (g + 1))
                    for a in range(4):
                        hd = 2 * a + g
                        ins = mm(pC[0][:, a, :], az[:, a, :], QK[:, 3, hd * FD:(hd + 1) * FD])
                    ins.then_inc(s_c[0], 1)

            @block.scalar
            def _(act):
                act.wait_ge(s_g, 1)
                nc.scalar.activation(sb_[:].rearrange("p h a -> p (h a)"), gp[0][:, 0:2 * FH], ACT.Sigmoid).then_inc(s_e, 1)
                for kind in range(5):
                    act.wait_ge(s_g, kind + 2)
                    nc.scalar.activation(QK[:, kind, :], gp[(kind + 1) % 2][:], ACT.Copy).then_inc(s_e, 1)
                nc.scalar.activation(sb_[:], sb_[:], ACT.Sqrt).then_inc(s_be, 1)
                act.wait_ge(s_mx, 1)
                nc.scalar.activation(QK[:, 0:3, :], QK[:, 0:3, :], ACT.Exp).then_inc(s_ex, 1)
                for kind in range(3):
                    act.wait_ge(s_g, 7 + kind)
                    nc.scalar.activation(KT[:, 4 * kind:4 * kind + 4, :], gp[kind % 2][:].rearrange("p (a s) -> p a s", a=4),
                                         ACT.Copy).then_inc(s_e, 1)
                for g in range(2):
                    for l in range(LEV - 1):
                        for k in range(2):
                            m = NSQ * g + 2 * l
                            if l < LEV - 2:
                                act.wait_ge(s_sq[k], m + 1)
                                nc.scalar.activation(nl[k][(l + 1) % 2][:], pA[k][:], ACT.Copy).then_inc(s_n[k], 1)
                                m += 1
                            act.wait_ge(s_sq[k], m + 1)
                            nc.scalar.activation(nu[k][(l + 1) % 2][:], pB[k][:], ACT.Copy).then_inc(s_n[k], 1)

            @block.vector
            def _(dve):
                own = Chain(dve, s_own)
                V.tensor_copy(xc[:].rearrange("p a s -> p s a"), X[:, :, bass.ds(2 * i, 2)]).then_inc(s_x, 1)
                qk = QK[:, 0:3, :].rearrange("p k (h d) -> p (k h) d", d=FD)
                dve.wait_ge(s_e, 4)
                own(V.tensor_reduce(mx[:], qk, AX.X, ALU.max))
                V.tensor_tensor(qk, qk, mx[:].unsqueeze(2).to_broadcast([128, 3 * FH, FD]), ALU.subtract).then_inc(s_mx, 1)
                dve.wait_ge(s_e, 6)
                dve.wait_ge(s_be, 1)
                for k in range(2):
                    vv = QK[:, 3 + k, :].rearrange("p (h d) -> p h d", d=FD)
                    V.tensor_tensor(vv, vv, sb_[:, :, k].unsqueeze(2).to_broadcast([128, FH, FD]), ALU.mult).then_inc(s_u[k], 1)
                dve.wait_ge(s_ex, 1)
                own(V.tensor_reduce(sm[:], qk, AX.X, ALU.add))
                own(V.reciprocal(sm[:], sm[:]))
                for k in range(2):
                    r = slice((1 + k) * FH, (2 + k) * FH)
                    own(V.tensor_tensor(sm[:, r], sm[:, r], sb_[:, :, k], ALU.mult))
                V.tensor_tensor(qk, qk, sm[:].unsqueeze(2).to_broadcast([128, 3 * FH, FD]), ALU.mult).then_inc(s_k, 1)
                bc = lambda m: m[:, None, :].to_broadcast([128, 4, 128])
                for g in range(2):
                    for k in range(2):
                        dve.wait_ge(s_G[k], (2 if k == 0 else 1) * g + 1)
                        V.tensor_tensor(nl[k][0][:], pA[k][:], bc(maskL), ALU.mult).then_inc(s_m[k], 1)
                        V.tensor_tensor(nu[k][0][:], pA[k][:], bc(maskU), ALU.mult).then_inc(s_m[k], 1)
                    dve.wait_ge(s_G[0], 2 * g + 2)
                    V.tensor_tensor(az[:], pB[0][:], bc(maskZ), ALU.mult).then_inc(s_m[0], 1)
                    for l in range(LEV):
                        for k in range(2):
                            dve.wait_ge(s_c[k], (LEV + 1 - k) * g + l + 1)
                            u = QK[:, 3 + k, :].rearrange("p (a g d) -> p g a d", a=4, g=2)[:, g]
                            V.tensor_tensor(u, u, pC[k][:], ALU.subtract if l == 0 else ALU.add).then_inc(s_u[k], 1)
                    dve.wait_ge(s_c[0], (LEV + 1) * (g + 1))
                    V.tensor_copy(Z[:].rearrange("p (a g d) -> p g a d", a=4, g=2)[:, g], pC[0][:]).then_inc(s_z, 1)

            @block.sync
            def _(sp):
                rows = lambda t: t.rearrange("(n a) s d -> n (a s) d", a=2)[i]
                sp.wait_ge(s_k, 1)
                sp.dma_start(rows(kr), QK[:, 2, :]).then_inc(s_out, 16)
                sp.wait_ge(s_u[1], 1 + 2 * LEV)
                sp.dma_start(rows(ur), QK[:, 4, :]).then_inc(s_out, 16)
                sp.wait_ge(s_z, 2)
                sp.dma_start(rows(zz), Z[:]).then_inc(s_out, 16)
                sp.wait_ge(s_out, 48)


def recur_stage(nc, c, kr, ur, zz, hs):
    with Stage(nc, "recur") as st:
        K = [st.sb(f"K{a}", [HT, SL, FD]) for a in range(2)]
        U = [st.sb(f"U{a}", [HT, SL, FD]) for a in range(2)]
        Hh = [st.sb(f"H{a}", [HT, SL, FD]) for a in range(2)]
        pr = [st.sb(f"pr{a}", [HT, SL * FD]) for a in range(2)]
        e = [st.sb(f"e{a}", [HT, FD]) for a in range(2)]
        w = [st.sb(f"w{a}", [HT, SL]) for a in range(2)]
        sm = [st.sb(f"sm{a}", [HT, FD]) for a in range(2)]
        mx = [st.sb(f"mx{a}", [HT, 1]) for a in range(2)]
        rs = [st.sb(f"rs{a}", [HT, 1]) for a in range(2)]
        s_in = st.sem("loaded")
        s_own = [st.sem(f"own{a}") for a in range(2)]
        s_mx = [st.sem(f"max{a}") for a in range(2)]
        s_ex = [st.sem(f"exp{a}") for a in range(2)]
        s_out = st.sem("stored")
        V = nc.vector
        view = lambda t: t.rearrange("(c p) s (h d) -> c h p s d", c=2, h=FH)
        with nc.Fori(0, FH) as i, st.step() as block:
            @block.sync
            def _(sp):
                for a in range(2):
                    for src, dst in ((kr, K), (ur, U), (zz, Hh)):
                        sp.dma_start(dst[a][:], view(src)[a, i]).then_inc(s_in, 16)
                for a in range(2):
                    sp.wait_ge(s_mx[a], SL)
                    sp.dma_start(hs.rearrange("s (c p) (h d) -> c h p s d", c=2, h=FH)[a, i], Hh[a][:]).then_inc(s_out, 16)
                sp.wait_ge(s_out, 32)

            @block.scalar
            def _(act):
                for t in range(1, SL):
                    for a in range(2):
                        act.wait_ge(s_mx[a], t)
                        nc.scalar.activation(e[a][:], Hh[a][:, t - 1, :], ACT.Exp, bias=mx[a][:, 0:1],
                                             accum_out=rs[a][:, 0:1]).then_inc(s_ex[a], 1)

            @block.vector
            def _(dve):
                own = [Chain(dve, s_own[a]) for a in range(2)]
                both = range(2)

                def each(fn):
                    for a in both:
                        fn(a).then_inc(s_own[a], 1)
                        own[a].n += 1

                def ready(a):
                    dve.wait_ge(s_own[a], own[a].n)

                dve.wait_ge(s_in, 16 * 6)
                for a in both:
                    V.memset(e[a][:], 1.0).then_inc(s_own[a], 1)
                    V.memset(rs[a][:], float(FD)).then_inc(s_own[a], 1)
                    own[a].n += 2
                for t in range(SL):
                    n = t + 1
                    full = [HT, n, FD]

                    def keys(a):
                        ready(a)
                        if t:
                            dve.wait_ge(s_ex[a], t)
                        return V.tensor_tensor(pr[a][:, 0:n * FD].rearrange("p (s d) -> p s d", d=FD), K[a][:, 0:n, :],
                                               e[a][:, None, :].to_broadcast(full), ALU.mult)

                    def dots(a):
                        ready(a)
                        return V.tensor_reduce(w[a][:, 0:n], pr[a][:, 0:n * FD].rearrange("p (s d) -> p s d", d=FD), AX.X, ALU.add)

                    def values(a):
                        ready(a)
                        return V.tensor_tensor(pr[a][:, 0:n * FD].rearrange("p (s d) -> p s d", d=FD), U[a][:, 0:n, :],
                                               w[a][:, 0:n].unsqueeze(2).to_broadcast(full), ALU.mult)

                    def sums(a):
                        ready(a)
                        return V.tensor_reduce(sm[a][:], pr[a][:, 0:n * FD].rearrange("p (s d) -> p d s", d=FD), AX.X, ALU.add)

                    def state(a):
                        ready(a)
                        return V.scalar_tensor_tensor(Hh[a][:, t, :], sm[a][:], rs[a][:, 0:1], Hh[a][:, t, :], ALU.mult, ALU.add)

                    each(keys)
                    each(dots)
                    each(lambda a: V.reciprocal(rs[a][:], rs[a][:]))
                    each(values)
                    each(sums)
                    each(state)
                    for a in both:
                        ready(a)
                        V.tensor_reduce(mx[a][:], Hh[a][:, t, :], AX.X, ALU.max, negate=True).then_inc(s_mx[a], 1)


def delta_out_stage(nc, c, hs, wout, xn, h, h_out):
    with Stage(nc, "dout") as st:
        wo = st.sb("wo", [128, 4, D])
        t = st.sb("t", [HT, 2, KW])
        tT = st.sb("tT", [128, 2, 4, HT])
        hb = st.sb("hb", [HT, 2, D])
        xb = st.sb("xb", [HT, 2, D])
        tp = [st.ps(f"tp{i}", [128, 4, 128]) for i in range(2)]
        yp = st.ps("yp", [HT, 2, D])
        s_w = st.sem("weights")
        s_in = st.sem("loaded")
        s_tp = st.sem("transposed")
        s_cp = st.sem("copied")
        s_mm = st.sem("multiplied")
        s_y = st.sem("y_ready")
        s_out = st.sem("stored")
        with st.step() as block:
            @block.sync
            def _(sp):
                sp.dma_start(wo[:], wout[:, :, :]).then_inc(s_w, 16)
                sp.wait_ge(s_w, 16)
        with nc.Fori(0, B) as b, st.step() as block:
            @block.sync
            def _(sp):
                sp.dma_start(t[:], hs.rearrange("s (c p) d -> s p c d", c=2)[b]).then_inc(s_in, 16)
                sp.dma_start(hb[:], tiles_of(h)[b]).then_inc(s_w, 16)
                sp.dma_start(xb[:], tiles_of(xn)[b]).then_inc(s_w, 16)
                sp.wait_ge(s_y, 2)
                sp.dma_start(tiles_of(h_out)[b], hb[:]).then_inc(s_out, 16)
                sp.wait_ge(s_out, 16)

            @block.tensor
            def _(pe):
                pe.wait_ge(s_in, 16)
                for k in range(2):
                    for m in range(4):
                        ins = nc.tensor.transpose(tp[k][:, m, 0:HT], t[:, k, m * 128:(m + 1) * 128], c.ident[0:HT, 0:HT])
                    ins.then_inc(s_tp, 1)
                for k in range(2):
                    pe.wait_ge(s_cp, k + 1)
                    for m in range(4):
                        ins = nc.tensor.matmul(yp[:, k, :], tT[:, k, m, :], wo[:, m, :], start=(m == 0), stop=(m == 3))
                ins.then_inc(s_mm, 1)

            @block.scalar
            def _(act):
                for k in range(2):
                    act.wait_ge(s_tp, k + 1)
                    nc.scalar.activation(tT[:, k], tp[k][:, :, 0:HT], ACT.Copy).then_inc(s_cp, 1)

            @block.vector
            def _(dve):
                dve.wait_ge(s_w, 32)
                nc.vector.tensor_tensor(hb[:], hb[:], xb[:], ALU.add).then_inc(s_y, 1)
                dve.wait_ge(s_y, 1)
                dve.wait_ge(s_mm, 1)
                nc.vector.tensor_tensor(hb[:], hb[:], yp[:], ALU.add).then_inc(s_y, 1)


CE = 8
CK = 2 * T // CE
CF = 256
CS = 64
RG = B * CE // 128


def choice_stage(nc, c, xn, xnT, Wg, W1, b1, W2, b2, h, h_out):
    with Stage(nc, "choice") as st:
        L = st.sb("L", [HT, 2, B, CE])
        PO = st.sb("PO", [HT, 2, B, CE])
        wg = st.sb("wg", [D, CE])
        xt = st.sb("xt", [D, CT * HT])
        red = st.sb("red", [HT, 2, NT])
        PT = st.sb("PT", [128, RG, T])
        t1 = st.sb("t1", [128, RG, T])
        t2 = st.sb("t2", [128, RG, T])
        one = st.sb("one", [128, T])
        tau = st.sb("tau", [128, RG])
        cand = st.sb("cand", [128, RG])
        bit = st.sb("bit", [128, RG], I32)
        cnt = st.sb("cnt", [128, RG])
        w1 = st.sb("w1", [D, CE, CF])
        w2 = st.sb("w2", [128, CE, 2, D])
        bu = st.sb("bu", [128, CE, 2])
        bd = st.sb("bd", [128, CE // 2, D])
        ios = st.sb("ios", [HT, CS])
        x = st.sb("x", [HT, 2, 2, D])
        hb = st.sb("hb", [HT, 2, 2, D])
        P = [st.sb(f"P{i}", [HT, 2, CE, CS]) for i in range(2)]
        PG = [st.sb(f"PG{i}", [HT, 2, CE, CS]) for i in range(2)]
        PGT = [st.sb(f"PGT{i}", [128, 2, CE // 2, HT]) for i in range(2)]
        xg = st.sb("xg", [D, CE, 2, CS])
        a = st.sb("a", [128, CE, 2, 2, CS])
        Y = [st.sb(f"Y{i}", [128, CE // 2, D]) for i in range(2)]
        gp = [st.ps(f"gp{i}", [128, 512]) for i in range(2)]
        tp = [st.ps(f"tp{i}", [128, 4, 128]) for i in range(2)]
        up = [st.ps(f"up{i}", [128, 2, 2, CS]) for i in range(2)]
        s_in = st.sem("loaded")
        s_own = st.sem("own")
        s_po = st.sem("pool_own")
        s_mm = st.sem("multiplied")
        s_act = st.sem("act")
        s_x = st.sem("ready")
        s_P = st.sem("onehot_ready")
        s_g = st.sem("product_done")
        s_e = st.sem("product_read")
        s_tp = st.sem("transposed")
        s_pt = st.sem("scatter_ready")
        s_up = st.sem("up_done")
        s_a = st.sem("act_done")
        s_h = st.sem("h_loaded")
        s_out = st.sem("stored")
        V = nc.vector
        with st.step() as block:
            @block.sync
            def _(sp):
                sp.dma_start(wg[:], Wg[:, :]).then_inc(s_in, 16)
                sp.dma_start(w1[:], W1.rearrange("e d f -> d e f")).then_inc(s_in, 16)
                for k in range(2):
                    sp.dma_start(w2[:, :, k, :], W2[:, k * 128:(k + 1) * 128, :].rearrange("e f d -> f e d")).then_inc(s_in, 16)
                    sp.dma_start(bu[:, :, k], b1[:, k * 128:(k + 1) * 128].rearrange("e f -> f e"),
                                 allow_slow_non_contiguous=True).then_inc(s_in, 16)
                    sp.dma_start(bd[k * CS:(k + 1) * CS, :, :], bass.AP(b2.tensor, k * D, [[0, CS], [2 * D, CE // 2], [1, D]])).then_inc(s_in, 16)
                sp.wait_ge(s_in, 16 * 8)

            @block.vector
            def _(dve):
                own = Chain(dve, s_own)
                own(V.memset(tau[:], 0.0))
                own(V.memset(one[:], 1.0))
                own(V.memset(bit[:], 1 << 29))

            @block.gpsimd
            def _(pool):
                nc.gpsimd.iota(ios[:], pattern=[[1, CS]], base=0, channel_multiplier=0,
                               allow_small_or_imprecise_dtypes=True).then_inc(s_po, 1)
                pool.wait_ge(s_po, 1)

        with nc.Fori(0, NT // CT) as i, st.step() as block:
            @block.sync
            def _(sp):
                sp.dma_start(xt[:], xnT[:, bass.ds(i * (CT * HT), CT * HT)]).then_inc(s_in, 16)

            @block.tensor
            def _(pe):
                pe.wait_ge(s_in, 16)
                for k in range(CT):
                    nc.tensor.matmul(gp[0][0:HT, k * CE:(k + 1) * CE], xt[:, k * HT:(k + 1) * HT], wg[:], start=True,
                                     stop=True).then_inc(s_mm, 1)

            @block.vector
            def _(dve):
                dve.wait_ge(s_mm, CT)
                V.tensor_copy(L[:, :, bass.ds(i * NBI, NBI), :], gp[0][0:HT, 0:CT * CE].rearrange("p (b c e) -> p c b e", c=2, e=CE)).then_inc(s_x, 1)
                dve.wait_ge(s_x, 1)

        with st.step() as block:
            @block.vector
            def _(dve):
                own = Chain(dve, s_own)
                Lf = L[:].rearrange("p c b e -> p (c b) e")
                rb = lambda k: red[:, k, :].unsqueeze(2).to_broadcast([HT, NT, CE])
                own(V.tensor_reduce(red[:, 0, :], Lf, AX.X, ALU.max))
                V.tensor_tensor(Lf, Lf, rb(0), ALU.subtract).then_inc(s_x, 1)
                dve.wait_ge(s_act, 1)
                own(V.tensor_reduce(red[:, 1, :], Lf, AX.X, ALU.add))
                own(V.reciprocal(red[:, 1, :], red[:, 1, :]))
                V.tensor_tensor(Lf, Lf, rb(1), ALU.mult).then_inc(s_x, 1)
                for k in range(2):
                    dve.wait_ge(s_mm, 4 * k + 4)
                    V.tensor_copy(PT[:, 2 * k:2 * k + 2, :].rearrange("p r (c t) -> p r c t", c=2),
                                  tp[k][:].rearrange("p (r c) t -> p r c t", r=2)[:, :, :, 0:HT]).then_inc(s_x, 1)
                dve.wait_ge(s_x, 4)

            @block.scalar
            def _(act):
                act.wait_ge(s_x, 1)
                nc.scalar.activation(L[:], L[:], ACT.Exp).then_inc(s_act, 1)

            @block.tensor
            def _(pe):
                pe.wait_ge(s_x, 2)
                for r in range(RG):
                    for k in range(2):
                        m = 2 * r + k
                        nc.tensor.transpose(tp[m // 4][:, m % 4, 0:HT], L[:, k, 16 * r:16 * r + 16, :].rearrange("p b e -> p (b e)"), c.ident[0:HT, 0:HT]).then_inc(s_mm, 1)

        full = [128, RG, T]
        with nc.Fori(0, 30) as i, st.step() as block:
            @block.vector
            def _(dve):
                own = Chain(dve, s_own)
                own(V.tensor_tensor(cand[:].bitcast(I32), tau[:].bitcast(I32), bit[:], ALU.bitwise_or))
                own(V.tensor_scalar(bit[:], bit[:], 1, None, ALU.logical_shift_right))
                own(V.tensor_tensor(t1[:], PT[:], cand[:].unsqueeze(2).to_broadcast(full), ALU.is_ge))
                own(V.tensor_reduce(cnt[:], t1[:], AX.X, ALU.add))
                own(V.scalar_tensor_tensor(cand[:], cnt[:], float(CK), cand[:], ALU.is_ge, ALU.mult))
                own(V.tensor_tensor(tau[:], tau[:], cand[:], ALU.max))

        with st.step() as block:
            @block.vector
            def _(dve):
                own = Chain(dve, s_own)
                tb = tau[:].unsqueeze(2).to_broadcast(full)
                own(V.tensor_tensor(t1[:], PT[:], tb, ALU.is_gt))
                own(V.tensor_tensor(t2[:], PT[:], tb, ALU.is_equal))
                own(V.tensor_reduce(cnt[:], t1[:], AX.X, ALU.add))
                own(V.tensor_scalar(cnt[:], cnt[:], -1.0, float(CK), ALU.mult, ALU.add))
                for r in range(RG):
                    own(V.tensor_tensor_scan(PT[:, r, :], one[:], t2[:, r, :], 0.0, ALU.mult, ALU.add))
                own(V.tensor_tensor(PT[:], PT[:], cnt[:].unsqueeze(2).to_broadcast(full), ALU.is_le))
                own(V.tensor_tensor(t2[:], t2[:], PT[:], ALU.mult))
                own(V.tensor_tensor(t1[:], t1[:], t2[:], ALU.add))
                for r in range(RG):
                    own(V.tensor_tensor_scan(PT[:, r, :], one[:], t1[:, r, :], 0.0, ALU.mult, ALU.add))
                own(V.tensor_tensor(PT[:], PT[:], t1[:], ALU.mult))
                V.tensor_scalar(PT[:], PT[:], -1.0, None, ALU.add).then_inc(s_x, 1)
                for k in range(2):
                    dve.wait_ge(s_mm, 4 * k + 4)
                    for m in range(4):
                        r, cc = divmod(4 * k + m, 2)
                        V.tensor_copy(PO[:, cc, 16 * r:16 * r + 16, :], tp[k][0:HT, m, :].rearrange("p (b e) -> p b e", e=CE)).then_inc(s_x, 1)
                dve.wait_ge(s_x, 9)

            @block.tensor
            def _(pe):
                pe.wait_ge(s_x, 1)
                for m in range(8):
                    r, cc = divmod(m, 2)
                    nc.tensor.transpose(tp[m // 4][0:HT, m % 4, :], PT[:, r, cc * HT:(cc + 1) * HT], c.ident[:]).then_inc(s_mm, 1)

        xv, hv, ov = tiles_of(xn), tiles_of(h), tiles_of(h_out)
        with nc.Fori(0, B // 2) as i, st.step() as block:
            @block.sync
            def _(sp):
                for k in range(2):
                    sp.dma_start(x[:, k], xv[2 * i + k]).then_inc(s_in, 16)
                for k in range(2):
                    sp.dma_start(hb[:, k], hv[2 * i + k]).then_inc(s_h, 16)
                for k in range(2):
                    sp.wait_ge(s_x, k + 1)
                    sp.dma_start(ov[2 * i + k], hb[:, k]).then_inc(s_out, 16)
                sp.wait_ge(s_out, 32)

            @block.gpsimd
            def _(pool):
                pool.wait_ge(s_P, 1)
                for k in range(2):
                    pool.wait_ge(s_P, k + 1)
                    for cc in range(2):
                        nc.gpsimd.tensor_tensor(PG[k][:, cc], P[k][:, cc],
                                                L[:, cc, bass.ds(2 * i + k, 1), :].rearrange("p b e -> p (b e)").unsqueeze(2).to_broadcast([HT, CE, CS]),
                                                ALU.mult).then_inc(s_po, 1)

            @block.tensor
            def _(pe):
                pe.wait_ge(s_in, 32)
                for k in range(2):
                    pe.wait_ge(s_P, k + 1)
                    for cc in range(2):
                        ins = nc.tensor.matmul(gp[k][:], x[:, k, cc, :], P[k][:, cc].rearrange("p e s -> p (e s)"),
                                               start=(cc == 0), stop=(cc == 1))
                    ins.then_inc(s_g, 1)
                for k in range(2):
                    for cc in range(2):
                        if k:
                            pe.wait_ge(s_pt, cc + 1)
                        for m in range(4):
                            pe.wait_ge(s_po, 2 * k + cc + 1)
                            ins = nc.tensor.transpose(tp[cc][:, m, 0:HT], PG[k][:, cc, 2 * m:2 * m + 2, :].rearrange("p e s -> p (e s)"),
                                                      c.ident[0:HT, 0:HT])
                        ins.then_inc(s_tp, 1)
                pe.wait_ge(s_e, 2)
                for e in range(CE):
                    if e >= 2:
                        pe.wait_ge(s_a, 2 * (e - 1))
                    for f in range(2):
                        ins = nc.tensor.matmul(up[e % 2][:, f].rearrange("p b s -> p (b s)"), w1[:, e, f * 128:(f + 1) * 128],
                                               xg[:, e].rearrange("p b s -> p (b s)"), start=True, stop=True)
                    ins.then_inc(s_up, 1)
                pe.wait_ge(s_a, 2 * CE)
                for k in range(2):
                    for e in range(CE):
                        o = gp[k][CS * (e % 2):CS * (e % 2) + CS, (e // 2) * D:(e // 2 + 1) * D]
                        for f in range(2):
                            ins = nc.tensor.matmul(o, a[:, e, f, k, :], w2[:, e, f, :], start=(f == 0), stop=(f == 1))
                    ins.then_inc(s_g, 1)
                for k in range(2):
                    pe.wait_ge(s_e, 3 + k)
                    pe.wait_ge(s_pt, 2 * k + 2)
                    for cc in range(2):
                        for m in range(CE // 2):
                            ins = nc.tensor.matmul(up[k][0:HT].rearrange("p f b s -> p (f b s)")[:, cc * D:(cc + 1) * D],
                                                   PGT[k][:, cc, m, :], Y[k][:, m, :], start=(m == 0), stop=(m == CE // 2 - 1))
                    ins.then_inc(s_mm, 1)

            @block.vector
            def _(dve):
                for k in range(2):
                    for cc in range(2):
                        ins = V.tensor_tensor(P[k][:, cc], PO[:, cc, bass.ds(2 * i + k, 1)].rearrange("p b e -> p (b e)").unsqueeze(2).to_broadcast([HT, CE, CS]),
                                              ios[:, None, :].to_broadcast([HT, CE, CS]), ALU.is_equal)
                    ins.then_inc(s_P, 1)
                for k in range(2):
                    dve.wait_ge(s_g, k + 1)
                    V.tensor_copy(xg[:, :, k, :], gp[k][:].rearrange("p (e s) -> p e s", e=CE)).then_inc(s_e, 1)
                for k in range(2):
                    dve.wait_ge(s_g, 3 + k)
                    V.tensor_tensor(Y[k][:].rearrange("p m d -> p (m d)"), gp[k][:], bd[:].rearrange("p m d -> p (m d)"), ALU.add).then_inc(s_e, 1)
                dve.wait_ge(s_h, 32)
                for k in range(2):
                    dve.wait_ge(s_mm, k + 1)
                    hf = hb[:, k].rearrange("p c d -> p (c d)")
                    V.tensor_tensor(hf, hf, up[k][0:HT].rearrange("p f b s -> p (f b s)"), ALU.add).then_inc(s_x, 1)

            @block.scalar
            def _(act):
                for k in range(2):
                    for cc in range(2):
                        act.wait_ge(s_tp, 2 * k + cc + 1)
                        nc.scalar.activation(PGT[k][:, cc], tp[cc][:, :, 0:HT], ACT.Copy).then_inc(s_pt, 1)
                for e in range(CE):
                    act.wait_ge(s_up, e + 1)
                    for f in range(2):
                        nc.scalar.activation(a[:, e, f].rearrange("p b s -> p (b s)"), up[e % 2][:, f].rearrange("p b s -> p (b s)"),
                                             ACT.Gelu, bias=bu[:, e, f:f + 1]).then_inc(s_a, 1)


RP = 2 * T - 1
WB = T + HT - 1


def position_stage(nc, c, pos, Wp, bp, pT):
    with Stage(nc, "pos") as st:
        e = st.sb("e", [HT, 4, D])
        eT = st.sb("eT", [D, 4, HT])
        w = st.sb("w", [D, D])
        b = st.sb("b", [D, 1])
        o = st.sb("o", [D, 4 * HT])
        tp = st.ps("tp", [D, 4, 128])
        op = st.ps("op", [D, 4 * HT])
        s_in = st.sem("loaded")
        s_pe = st.sem("pe")
        s_x = st.sem("ready")
        s_out = st.sem("stored")
        with st.step() as block:
            @block.sync
            def _(sp):
                sp.dma_start(e[:], pos[0, 0:4 * HT, :].rearrange("(a p) d -> p a d", a=4)).then_inc(s_in, 16)
                sp.dma_start(w[:], Wp[:, :]).then_inc(s_in, 16)
                sp.dma_start(b[:], bp.rearrange("(p a) -> p a", a=1)).then_inc(s_in, 16)
                sp.wait_ge(s_x, 2)
                sp.dma_start(pT[:, :], o[:]).then_inc(s_out, 16)
                sp.wait_ge(s_out, 16)

            @block.tensor
            def _(pe):
                pe.wait_ge(s_in, 48)
                for k in range(4):
                    ins = nc.tensor.transpose(tp[:, k, 0:HT], e[:, k, :], c.ident[0:HT, 0:HT])
                ins.then_inc(s_pe, 1)
                pe.wait_ge(s_x, 1)
                nc.tensor.matmul(op[:], w[:], eT[:].rearrange("p a t -> p (a t)"), start=True, stop=True).then_inc(s_pe, 1)

            @block.vector
            def _(dve):
                dve.wait_ge(s_pe, 1)
                nc.vector.tensor_copy(eT[:], tp[:, :, 0:HT]).then_inc(s_x, 1)
                dve.wait_ge(s_pe, 2)
                nc.vector.tensor_scalar(o[:], op[:], b[:, 0:1], None, ALU.add).then_inc(s_x, 1)


def relative_stage(nc, c, xnT, pT, Wq, bq, Wk, bk, Wv, bv, Wo, bo, pu, pv_, scr, h, h_out):
    SCALE = HD ** -0.5
    with Stage(nc, "rel") as st:
        w = st.sb("w", [D, 4, D])
        cols = st.sb("cols", [D, 5])
        br = st.sb("br", [1, 2, D])
        hm = st.sb("hm", [D, NH])
        ones = st.sb("ones", [1, HT])
        pt = st.sb("pt", [D, RP + 1])
        x = st.sb("x", [D, 2, T])
        hb = st.sb("hb", [HT, 2, 2, D])
        QU = [st.sb(f"QU{k}", [D, NH, T]) for k in range(2)]
        QV = st.sb("QV", [D, NH, T])
        KT = [st.sb(f"KT{k}", [D, T]) for k in range(2)]
        Vt = [st.sb(f"V{k}", [HT, 2, D]) for k in range(2)]
        BD = [st.sb(f"BD{f}", [HT, NH, WB]) for f in range(2)]
        sc = [[st.sb(f"sc{k}{f}", [HT, NH, T]) for f in range(2)] for k in range(2)]
        PT = st.sb("PT", [HT, NH, 2, HT])
        mx = st.sb("mx", [HT, 2, 2, NH])
        rs = st.sb("rs", [HT, 2, 2, NH])
        ri = st.sb("ri", [HT, 2, 2, NH])
        o = [st.sb(f"o{k}", [HT, 2, D]) for k in range(2)]
        oT = [st.sb(f"oT{k}", [D, 2, HT]) for k in range(2)]
        scp = st.ps("scp", [HT, 4, 512])
        gp = [st.ps(f"gp{i}", [128, 512]) for i in range(2)]
        ap = [st.ps(f"ap{i}", [128, 4, 128]) for i in range(2)]
        s_w = st.sem("weights")
        s_own = st.sem("own")
        s_po = st.sem("pool_own")
        s_in = st.sem("loaded")
        s_hb = st.sem("h_loaded")
        s_g = st.sem("product_done")
        s_e = st.sem("product_read")
        s_ag = st.sem("act_product_done")
        s_ae = st.sem("act_product_read")
        s_qv = st.sem("qv_ready")
        s_bw = [st.sem(f"positions_stored{f}") for f in range(2)]
        s_bd = [st.sem(f"positions_back{m}") for m in range(4)]
        s_sc = st.sem("scores_done")
        s_sr = st.sem("scores_read")
        s_mx = st.sem("max_ready")
        s_ex = st.sem("exp_done")
        s_y = st.sem("h_ready")
        s_out = st.sem("stored")
        V = nc.vector
        with st.step() as block:
            @block.sync
            def _(sp):
                for k, m in enumerate((Wq, Wk, Wv, Wo)):
                    sp.dma_start(w[:, k, :], m[:, :]).then_inc(s_w, 16)
                for k, v in enumerate((bq, bk)):
                    sp.dma_start(cols[:, k:k + 1], v.rearrange("(p a) -> p a", a=1)).then_inc(s_w, 16)
                for k, v in enumerate((pu, pv_)):
                    sp.dma_start(cols[:, 2 + k:3 + k], bass.AP(v.tensor, 0, [[1, D], [1, 1]])).then_inc(s_w, 16)
                for k, v in enumerate((bv, bo)):
                    sp.dma_start(br[:, k, :], v.rearrange("(a d) -> a d", a=1)).then_inc(s_w, 16)
                sp.dma_start(pt[:], pT[:, :]).then_inc(s_w, 16)
                sp.wait_ge(s_w, 16 * 11)

            @block.gpsimd
            def _(pool):
                own = Chain(pool, s_po)
                head_masks(pool, nc, own, hm)

            @block.vector
            def _(dve):
                own = Chain(dve, s_own)
                own(V.memset(ones[:], 1.0))
                dve.wait_ge(s_w, 16 * 11)
                own(V.tensor_tensor(cols[:, 2:3], cols[:, 2:3], cols[:, 0:1], ALU.add))
                own(V.tensor_tensor(cols[:, 3:4], cols[:, 3:4], cols[:, 0:1], ALU.add))

        NB = 2 * NH
        NTR = 2 * NH // 4 * 2
        hv, ov = tiles_of(h), tiles_of(h_out)
        with nc.Fori(0, B // 2) as i, st.step() as block:
            @block.sync
            def _(sp):
                sp.dma_start(x[:].rearrange("p a t -> p (a t)"), xnT[:, bass.ds(i * (2 * T), 2 * T)]).then_inc(s_in, 16)
                for k in range(2):
                    for f in range(2):
                        m = 2 * k + f
                        sp.wait_ge(s_ae, NH * (m + 1))
                        sp.dma_start(scr[m], BD[f][:]).then_inc(s_bw[f], 16)
                        sp.wait_ge(s_bw[f], 16 * (k + 1))
                        sp.dma_start(sc[k][f][:], bass.AP(scr.tensor, m * HT * NH * WB + HT - 1, [[NH * WB - 1, HT], [WB, NH], [1, T]])).then_inc(s_bd[m], 16)
                for k in range(2):
                    sp.dma_start(hb[:, k], hv[2 * i + k]).then_inc(s_hb, 16)
                for k in range(2):
                    sp.wait_ge(s_y, k + 1)
                    sp.dma_start(ov[2 * i + k], hb[:, k]).then_inc(s_out, 16)
                sp.wait_ge(s_out, 32)

            @block.tensor
            def _(pe):
                n = [0, 0]

                def mm(o_, l, r, first=True, last=True):
                    return nc.tensor.matmul(o_, l, r, start=first, stop=last)

                def job(fn):
                    m = n[0]
                    if m >= 2:
                        pe.wait_ge(s_e, m - 1)
                    fn(gp[m % 2]).then_inc(s_g, 1)
                    n[0] += 1

                def ajob(fn):
                    m = n[1]
                    if m >= 2:
                        pe.wait_ge(s_ae, m - 1)
                    fn(ap[m % 2]).then_inc(s_ag, 1)
                    n[1] += 1

                pe.wait_ge(s_in, 16)
                for k in range(2):
                    xk = x[:, k, :]
                    job(lambda p: mm(p[:, 0:T], w[:, 0, :], xk))
                    job(lambda p: mm(p[:, 0:T], w[:, 1, :], xk))

                    def values(p):
                        for cc in range(2):
                            mm(p[0:HT, cc * D:(cc + 1) * D], x[:, k, cc * HT:(cc + 1) * HT], w[:, 2, :], True, False)
                            ins = mm(p[0:HT, cc * D:(cc + 1) * D], ones[:], br[:, 0, :], False, True)
                        return ins
                    job(values)
                    pe.wait_ge(s_qv, 2 * k + 2)
                    for f in range(2):
                        for hd in range(NH):
                            ajob(lambda p: mm(p[0:HT].rearrange("p a t -> p (a t)")[:, 0:WB], QV[:, hd, f * HT:(f + 1) * HT],
                                              pt[:, (1 - f) * HT:(1 - f) * HT + WB]))
                def finish(k):
                    def turn_out(p):
                        pe.wait_ge(s_e, n[0])
                        for cc in range(2):
                            ins = nc.tensor.transpose(p[:, cc * 128:cc * 128 + HT], o[k][:, cc, :], c.ident[0:HT, 0:HT])
                        return ins
                    job(turn_out)

                    def outs(p):
                        pe.wait_ge(s_e, n[0])
                        for cc in range(2):
                            mm(p[0:HT, cc * D:(cc + 1) * D], oT[k][:, cc, :], w[:, 3, :], True, False)
                            ins = mm(p[0:HT, cc * D:(cc + 1) * D], ones[:], br[:, 1, :], False, True)
                        return ins
                    job(outs)

                for k in range(2):
                    for f in range(2):
                        m = 2 * k + f
                        pe.wait_ge(s_e, 6)
                        if m:
                            pe.wait_ge(s_sr, m)
                        for hd in range(NH):
                            ins = mm(scp[:, hd // 2, (hd % 2) * T:(hd % 2 + 1) * T], QU[k][:, hd, f * HT:(f + 1) * HT], KT[k][:])
                        ins.then_inc(s_sc, 1)
                        if m == 2:
                            finish(0)
                        for g in range(4):
                            def turn(p):
                                for r in range(4):
                                    hd, sh = divmod(4 * g + r, 2)
                                    pe.wait_ge(s_ex, m * NH + hd + 1)
                                    ins = nc.tensor.transpose(p[0:HT, r, 0:HT], sc[k][f][:, hd, sh * HT:(sh + 1) * HT], c.ident[0:HT, 0:HT])
                                return ins
                            ajob(turn)

                        def pv(p):
                            pe.wait_ge(s_ae, 2 * NB + 4 * (m + 1))
                            for hd in range(NH):
                                for sh in range(2):
                                    ins = mm(p[0:HT, hd * HD:(hd + 1) * HD], PT[:, hd, sh, :], Vt[k][:, sh, hd * HD:(hd + 1) * HD],
                                             sh == 0, sh == 1)
                            return ins
                        job(pv)
                finish(1)

            @block.vector
            def _(dve):
                own = Chain(dve, s_own)
                n = [0]

                def read(fn):
                    n[0] += 1
                    dve.wait_ge(s_g, n[0])
                    fn(gp[(n[0] - 1) % 2]).then_inc(s_e, 1)

                full = [D, NH, T]
                for k in range(2):
                    def queries(p):
                        mask = hm[:].unsqueeze(2).to_broadcast(full)
                        src = p[:, None, 0:T].to_broadcast(full)
                        if k:
                            dve.wait_ge(s_ag, NB)
                        V.scalar_tensor_tensor(QV[:], src, cols[:, 3:4], mask, ALU.add, ALU.mult).then_inc(s_qv, 1)
                        return V.scalar_tensor_tensor(QU[k][:], src, cols[:, 2:3], mask, ALU.add, ALU.mult)
                    read(queries)
                    V.engine_nop().then_inc(s_qv, 1)
                    read(lambda p: V.tensor_scalar(KT[k][:], p[:, 0:T], cols[:, 1:2], None, ALU.add))
                    read(lambda p: V.tensor_copy(Vt[k][:].rearrange("p a d -> p (a d)"), p[0:HT, 0:2 * D]))
                def heads(k, f):
                    def fn(p):
                        own(V.reciprocal(ri[:, k, f, :], rs[:, k, f, :]))
                        return V.tensor_tensor(o[k][:, f, :].rearrange("p (h d) -> p h d", h=NH),
                                               p[0:HT, 0:D].rearrange("p (h d) -> p h d", h=NH),
                                               ri[:, k, f, :].unsqueeze(2).to_broadcast([HT, NH, HD]), ALU.mult)
                    read(fn)

                def finish(k):
                    read(lambda p: V.tensor_copy(oT[k][:], p[:, 0:256].rearrange("p (a t) -> p a t", a=2)[:, :, 0:HT]))
                    dve.wait_ge(s_hb, 32)
                    hf = hb[:, k].rearrange("p c d -> p (c d)")
                    read(lambda p: V.tensor_tensor(hf, hf, p[0:HT, 0:256], ALU.add))
                    V.engine_nop().then_inc(s_y, 1)

                for k in range(2):
                    for f in range(2):
                        m = 2 * k + f
                        dve.wait_ge(s_sc, m + 1)
                        dve.wait_ge(s_bd[m], 16)
                        sv = sc[k][f][:].rearrange("p (a b) s -> p a (b s)", b=2)
                        V.tensor_tensor(sv, sv, scp[:, :, 0:2 * T], ALU.add).then_inc(s_sr, 1)
                        dve.wait_ge(s_sr, m + 1)
                        own(V.tensor_reduce(mx[:, k, f, :], sc[k][f][:], AX.X, ALU.max))
                        V.tensor_scalar(mx[:, k, f, :], mx[:, k, f, :], -SCALE, None, ALU.mult).then_inc(s_mx, 1)
                        if m:
                            heads(*divmod(m - 1, 2))
                        if m == 2:
                            finish(0)
                heads(1, 1)
                finish(1)

            @block.scalar
            def _(act):
                n = [0]

                def read(fn):
                    n[0] += 1
                    act.wait_ge(s_ag, n[0])
                    fn(ap[(n[0] - 1) % 2]).then_inc(s_ae, 1)

                for k in range(2):
                    for f in range(2):
                        if k:
                            act.wait_ge(s_bw[f], 16)
                        for hd in range(NH):
                            read(lambda p: nc.scalar.activation(BD[f][:, hd, :], p[0:HT].rearrange("p a t -> p (a t)")[:, 0:WB], ACT.Copy))
                for k in range(2):
                    for f in range(2):
                        m = 2 * k + f
                        act.wait_ge(s_mx, m + 1)
                        for hd in range(NH):
                            nc.scalar.activation(sc[k][f][:, hd, :], sc[k][f][:, hd, :], ACT.Exp, bias=mx[:, k, f, hd:hd + 1], scale=SCALE,
                                                 accum_out=rs[:, k, f, hd:hd + 1]).then_inc(s_ex, 1)
                        if m:
                            act.wait_ge(s_g, 6 + m + (2 if k and f else 0))
                        for g in range(4):
                            read(lambda p: nc.scalar.activation(PT[:, 2 * g:2 * g + 2].rearrange("p a s t -> p (a s) t"), p[0:HT, :, 0:HT], ACT.Copy))


def last_stage(nc, c, xnT, Wg, bg, We, be, h, out):
    E = 16
    with Stage(nc, "last") as st:
        xa = st.sb("xa", [D, B, T])
        m = st.sb("m", [D, B])
        wg = st.sb("wg", [D, E])
        bgb = st.sb("bgb", [B, E])
        z = st.sb("z", [B, E])
        red = st.sb("red", [B, 4])
        ie = st.sb("ie", [B, E])
        pid = st.sb("pid", [128, 1])
        wide2 = st.sb("wide2", [B, 2, 128])
        gate = st.sb("gate", [128, B])
        rows = st.sb("rows", [128, 2, B], U32)
        cur = st.sb("cur", [128, 2, 4], U32)
        hb = st.sb("hb", [HT, 4, 2, D])
        x = st.sb("x", [D, 4, T])
        ws = st.sb("ws", [D, 4, D])
        bs = st.sb("bs", [D, 4, D])
        y = st.sb("y", [HT, 4, 2, D])
        p = [st.ps(f"p{i}", [128, 512]) for i in range(4)]
        s_in = st.sem("loaded")
        s_own = st.sem("own")
        s_po = st.sem("pool_own")
        s_mm = st.sem("multiplied")
        s_x = st.sem("ready")
        s_act = st.sem("act")
        s_g = [st.pool_sem(f"gathered{k}") for k in range(4)]
        s_h = st.sem("h_loaded")
        s_out = st.sem("stored")
        V = nc.vector
        with st.step() as block:
            @block.sync
            def _(sp):
                sp.dma_start(wg[:], Wg[:, :]).then_inc(s_in, 16)
                sp.dma_start(bgb[:], wide(bg, B)).then_inc(s_in, 16)
                xv = xnT.rearrange("p (b t) -> p b t", b=B)
                for k in range(8):
                    sp.dma_start(xa[:, 8 * k:8 * k + 8, :], xv[:, 8 * k:8 * k + 8, :]).then_inc(s_in, 16)
                sp.wait_ge(s_in, 160)

            @block.gpsimd
            def _(pool):
                P = nc.gpsimd
                own = Chain(pool, s_po)
                own(P.iota(ie[:], pattern=[[1, E]], base=0, channel_multiplier=0, allow_small_or_imprecise_dtypes=True))
                own(P.iota(pid[:], pattern=[[0, 1]], base=0, channel_multiplier=1, allow_small_or_imprecise_dtypes=True))

            @block.tensor
            def _(pe):
                pe.wait_ge(s_x, 1)
                nc.tensor.matmul(p[0][0:B, 0:E], m[:], wg[:], start=True, stop=True).then_inc(s_mm, 1)
                pe.wait_ge(s_x, 3)
                for k in range(2):
                    ins = nc.tensor.matmul(p[1][:, k * B:(k + 1) * B], wide2[:, k, :], c.ident[0:B, 0:B], start=True, stop=True)
                ins.then_inc(s_mm, 1)

            @block.scalar
            def _(act):
                act.wait_ge(s_x, 2)
                nc.scalar.activation(z[:], z[:], ACT.Exp).then_inc(s_act, 1)

            @block.vector
            def _(dve):
                own = Chain(dve, s_own)
                dve.wait_ge(s_in, 160)
                own(V.tensor_reduce(m[:], xa[:], AX.X, ALU.add))
                V.tensor_scalar(m[:], m[:], 1.0 / T, None, ALU.mult).then_inc(s_x, 1)
                dve.wait_ge(s_mm, 1)
                own(V.tensor_tensor(z[:], p[0][0:B, 0:E], bgb[:], ALU.add))
                own(V.tensor_reduce(red[:, 0:1], z[:], AX.X, ALU.max))
                V.tensor_scalar(z[:], z[:], red[:, 0:1], None, ALU.subtract).then_inc(s_x, 1)
                dve.wait_ge(s_act, 1)
                dve.wait_ge(s_po, 2)
                own(V.tensor_reduce(red[:, 1:2], z[:], AX.X, ALU.add))
                own(V.reciprocal(red[:, 1:2], red[:, 1:2]))
                own(V.tensor_scalar(z[:], z[:], red[:, 1:2], None, ALU.mult))
                own(V.tensor_reduce(red[:, 2:3], z[:], AX.X, ALU.max))
                own(V.tensor_scalar(z[:], z[:], red[:, 2:3], float(-E), ALU.is_equal, ALU.mult))
                own(V.tensor_tensor(z[:], z[:], ie[:], ALU.add))
                own(V.tensor_reduce(red[:, 3:4], z[:], AX.X, ALU.min))
                own(V.tensor_scalar(red[:, 3:4], red[:, 3:4], float(E), None, ALU.add))
                own(V.tensor_copy(wide2[:, 0, :], red[:, 2:3].to_broadcast([B, 128])))
                V.tensor_copy(wide2[:, 1, :], red[:, 3:4].to_broadcast([B, 128])).then_inc(s_x, 1)
                dve.wait_ge(s_mm, 2)
                own(V.tensor_copy(gate[:], p[1][:, 0:B]))
                own(V.tensor_scalar(rows[:, 0, :], p[1][:, B:2 * B], float(D), pid[:, 0:1], ALU.mult, ALU.add))
                own(V.tensor_copy(rows[:, 1, :], p[1][:, B:2 * B]))

        wrows = We.rearrange("e d o -> (e d) o")
        with nc.Fori(0, B // 4) as i, st.step() as block:
            @block.vector
            def _(dve):
                V.tensor_copy(cur[:], rows[:, :, bass.ds(4 * i, 4)]).then_inc(s_x, 1)
                dve.wait_ge(s_h, 64)
                for k in range(4):
                    dve.wait_ge(s_mm, k + 1)
                    yk = y[:, k]
                    V.tensor_tensor(yk, p[k][0:HT, 0:256].rearrange("p (a d) -> p a d", a=2),
                                    bs[0:HT, k, None, :].to_broadcast([HT, 2, D]), ALU.add).then_inc(s_act, 1)
                    dve.wait_ge(s_act, k + 1)
                    V.scalar_tensor_tensor(hb[:, k], yk, gate[0:HT, bass.ds(4 * i + k, 1)], hb[:, k], ALU.mult, ALU.add).then_inc(s_x, 1)

            @block.gpsimd
            def _(pool):
                pool.wait_ge(s_x, 1)
                for k in range(4):
                    nc.gpsimd.indirect_dma_start(ws[:, k, :], None, wrows, bass.IndirectOffsetOnAxis(ap=cur[:, 0, k:k + 1], axis=0)).then_inc(s_g[k], 16)
                    nc.gpsimd.indirect_dma_start(bs[:, k, :], None, be[:, :], bass.IndirectOffsetOnAxis(ap=cur[:, 1, k:k + 1], axis=0)).then_inc(s_g[k], 16)

            @block.sync
            def _(sp):
                sp.dma_start(x[:].rearrange("p a t -> p (a t)"), xnT[:, bass.ds(i * (4 * T), 4 * T)]).then_inc(s_in, 16)
                for k in range(4):
                    sp.dma_start(hb[:, k], tiles_of(h)[4 * i + k]).then_inc(s_h, 16)
                for k in range(4):
                    sp.wait_ge(s_x, k + 2)
                    sp.dma_start(out.rearrange("b (c p) d -> b p c d", c=2)[4 * i + k], hb[:, k]).then_inc(s_out, 16)
                sp.wait_ge(s_out, 64)

            @block.tensor
            def _(pe):
                pe.wait_ge(s_in, 16)
                for k in range(4):
                    pe.wait_ge(s_g[k], 32)
                    for a in range(2):
                        ins = nc.tensor.matmul(p[k][0:HT, a * D:(a + 1) * D], x[:, k, a * HT:(a + 1) * HT], ws[:, k, :], start=True, stop=True)
                    ins.then_inc(s_mm, 1)


def build_audio_tower(nc, a, out):
    scratch = lambda name, *shape, dt=F32: nc.dram_tensor(name, list(shape), dt).ap()
    hA, hB = scratch("hA", N, D), scratch("hB", N, D)
    xn = scratch("xn", N, D)
    xnT, xn2T = scratch("xnT", D, N), scratch("xn2T", D, N)
    kpad = scratch("kpad", D, KP)
    wt1 = scratch("wt1", 11, D, D)
    liqT, wgt = scratch("liqT", D, N), scratch("wgt", B, 3)
    wslow, wout = scratch("wslow", D, PROJ), scratch("wout", D, 4, D)
    kr, ur, zz = (scratch(n, T, SL, KW) for n in ("kr", "ur", "zz"))
    hs = scratch("hs", SL, T, KW)
    pT, scr = scratch("pT", D, RP + 1), scratch("scr", 4, HT, NH, WB)
    of = lambda layer: (lambda *names: [a[f"{layer}_{n}"] for n in names])

    with Stage(nc, "const") as st:
        class c:
            ident = st.sb("ident", [128, 128])
        consts_stage(nc, st, c.ident)

        tok_stage(nc, c, a["x"], *of("L0_tok")("W", "b", "gamma", "beta"), hA)

        ln_stage(nc, c, "ln0", hA, xn, None)
        s4_kernel_stage(nc, c, *of("L0_attn")("Lambda_re", "Lambda_im", "P", "B", "C", "D", "log_step"),
                        a["s4_cos"], a["s4_sin"], a["s4_dft_re"], a["s4_dft_im"], kpad)
        s4_conv_stage(nc, c, xn, kpad, hA, hB)

        ln_stage(nc, c, "ln1", hB, xn, xnT)
        g = of("L0_ffn")
        E, cap = 32, N // 32
        xp, idx = scratch("xp0", N, D + E), scratch("idx0", HT, E, cap // HT, dt=U32)
        route_stage(nc, c, "route0", E, cap, xn, xnT, *g("W_router", "b_router"), xp, idx)
        experts_stage(nc, c, "experts0", E, cap, a["L0_ffn_W_up"].shape[2], 4, ACT.Silu, xp, idx,
                      *g("W_up", "b_up", "W_down", "b_down"), hB)

        ln_stage(nc, c, "ln2", hB, None, xnT)
        g = of("L1_attn")
        turn_weights_stage(nc, c, "turn1", g("li_Win", "li_Wrec", "li_Wout", "re_Wq", "re_Wk", "re_Wv", "re_Wo",
                                             "la_Wq", "la_Wk", "la_Wv", "la_Wo"), wt1)
        liquid_stage(nc, c, xnT, wt1, *g("li_tau", "li_b"), liqT)
        mix_weights_stage(nc, c, xnT, *g("rt_W1", "rt_b1", "rt_W2", "rt_b2", "fusion_w"), wgt)
        retention_stage(nc, c, xnT, liqT, wt1, g("re_gnw", "re_gnb", "re_bo", "la_bq", "la_bk", "la_bv", "la_bo",
                                                 "ln_w", "ln_b"), a["L1_attn_re_theta"], wgt, hB, hA)

        ln_stage(nc, c, "ln3", hA, xn, xnT)
        g = of("L1_ffn")
        E, cap = 16, N // 16
        xp, idx = scratch("xp1", N, D + E), scratch("idx1", HT, E, cap // HT, dt=U32)
        route_stage(nc, c, "route1", E, cap, xn, xnT, a["L1_ffn_gate_w"], None, xp, idx)
        shared_stage(nc, c, xnT, *g("sw1", "sb1", "sw2", "sb2"), hA, hB)
        experts_stage(nc, c, "experts1", E, cap, a["L1_ffn_w1"].shape[2], 1, ACT.Gelu_apprx_tanh, xp, idx,
                      *g("w1", "b1", "w2", "b2"), hB)

        ln_stage(nc, c, "ln4", hB, xn, None)
        ln_stage(nc, c, "ln5", xn, None, xn2T, *of("L2_attn")("ln_gamma", "ln_beta"))
        slow_weights_stage(nc, c, a["L2_attn_W_slow"], wslow, a["L2_attn_W_out"], wout)
        delta_stage(nc, c, xn2T, wslow, kr, ur, zz)
        recur_stage(nc, c, kr, ur, zz, hs)
        delta_out_stage(nc, c, hs, wout, xn, hB, hA)

        ln_stage(nc, c, "ln6", hA, xn, xnT)
        choice_stage(nc, c, xn, xnT, *of("L2_ffn")("Wg", "W1", "b1", "W2", "b2"), hA, hB)

        ln_stage(nc, c, "ln7", hB, None, xnT)
        g = of("L3_attn")
        position_stage(nc, c, *g("pos_emb", "Wp", "bp"), pT)
        relative_stage(nc, c, xnT, pT, *g("Wq", "bq", "Wk", "bk", "Wv", "bv", "Wo", "bo", "pos_bias_u", "pos_bias_v"),
                       scr, hB, hA)

        ln_stage(nc, c, "ln8", hA, None, xnT)
        last_stage(nc, c, xnT, *of("L3_ffn")("Wg", "bg", "We", "be"), hA, out)


def kernel(**inputs):
    import numpy as _np
    import concourse.bacc as _bacc
    from concourse import mybir as _mybir
    from concourse.bass_utils import run_bass_kernel_spmd as _run

    nc = _bacc.Bacc("TRN2", target_bir_lowering=False, num_devices=1)
    arrays, args = {}, {}
    for name, value in {**inputs, **s4_constants()}.items():
        v = _np.ascontiguousarray(value)
        arrays[f"in_{name}_dram"] = v
        args[name] = nc.dram_tensor(f"in_{name}_dram", v.shape, _mybir.dt.from_np(v.dtype), kind="ExternalInput").ap()
    out = nc.dram_tensor("out_0_dram", (B, T, D), _mybir.dt.float32, kind="ExternalOutput").ap()
    build_audio_tower(nc, args, out)
    r = _run(nc, [arrays], core_ids=[0])
    return r.results[0]["out_0_dram"]
```

```python
import concourse.bass as bass
from concourse import mybir
from contextlib import ExitStack, contextmanager

F32 = mybir.dt.float32
BF16 = mybir.dt.bfloat16
I32 = mybir.dt.int32
U32 = mybir.dt.uint32
ALU = mybir.AluOpType
ACT = mybir.ActivationFunctionType
AX = mybir.AxisListType

B = 64
TIN = 250
DIN = 24
CTX = 5
T = TIN - CTX + 1
HT = T // 2
D = 128
N = B * T
NT = N // HT
NBI = 4
CT = 2 * NBI
EPS = 1e-5


class Chain:

    def __init__(self, eng, sem):
        self.eng, self.sem, self.n = eng, sem, 0

    def __call__(self, ins):
        self.n += 1
        ins.then_inc(self.sem, 1)
        self.eng.wait_ge(self.sem, self.n)


class Stage:

    def __init__(self, nc, name):
        self.nc, self.name = nc, name
        self.ctx = ExitStack()
        self.sems, self.pool_sems = [], []

    def __enter__(self):
        self.ctx.__enter__()
        return self

    def __exit__(self, *a):
        return self.ctx.__exit__(*a)

    def sb(self, name, shape, dt=F32):
        return self.ctx.enter_context(self.nc.sbuf_tensor(f"{self.name}_{name}", shape, dt))

    def ps(self, name, shape, dt=F32):
        return self.ctx.enter_context(self.nc.psum_tensor(f"{self.name}_{name}", shape, dt))

    def sem(self, name):
        s = self.ctx.enter_context(self.nc.semaphore(f"{self.name}_{name}"))
        self.sems.append(s)
        return s

    def pool_sem(self, name):
        s = self.ctx.enter_context(self.nc.semaphore(f"{self.name}_{name}"))
        self.pool_sems.append(s)
        return s

    @contextmanager
    def step(self):
        with self.nc.Block(no_gpsimd_drain=True) as block:
            yield block
        with self.nc.Block(no_gpsimd_drain=True) as block:
            @block.sync
            def _(sp):
                for s in self.sems:
                    sp.sem_clear(s)

            if self.pool_sems:
                @block.gpsimd
                def _(pool):
                    for s in self.pool_sems:
                        pool.dma_reset(range(s.num, s.num + 1))
                        pool.sem_clear(s)


def wide(ap, p=128):
    return bass.AP(ap.tensor, ap.offset, [[0, p]] + [list(x) for x in ap.ap])


def tiles_of(dram):
    return dram.rearrange("(b c p) d -> b p c d", b=B, c=2)


def consts_stage(nc, st, ident):
    ready = st.sem("ident_ready")
    with st.step() as block:
        @block.gpsimd
        def _(pool):
            nc.gpsimd.memset(ident[:], 0.0).then_inc(ready, 1)
            pool.wait_ge(ready, 1)
            nc.gpsimd.affine_select(out=ident[:], in_=ident[:], compare_op=ALU.not_equal, fill=1.0,
                                    base=0, pattern=[[-1, 128]], channel_multiplier=1).then_inc(ready, 1)
            pool.wait_ge(ready, 2)


def tok_stage(nc, c, x, W, b, gamma, beta, h_out):
    K = CTX * DIN
    with Stage(nc, "tok") as st:
        H = st.sb("H", [HT, NT, D])
        wT = st.sb("wT", [K, D])
        wn = st.sb("wn", [D, K])
        brow = st.sb("brow", [1, D])
        ones = st.sb("ones", [HT, D])
        fr = st.sb("fr", [HT, CT, K])
        frT = st.sb("frT", [K, CT, HT])
        tp = [st.ps(f"tp{i}", [K, 4, 128]) for i in range(2)]
        hp = [st.ps(f"hp{i}", [HT, 4, D]) for i in range(2)]
        acc = st.ps("acc", [D, 4 * D])
        sq2 = [st.sb(f"sq{i}", [HT, 4 * D]) for i in range(2)]
        gb = st.sb("gb", [D, 2, D])
        mean = st.sb("mean", [D, D])
        var = st.sb("var", [D, D])
        s_in = st.sem("inputs")
        s_tp = st.sem("transposed")
        s_cp = st.sem("copied")
        s_mm = st.sem("multiplied")
        s_h = st.sem("h_ready")
        s_own = st.sem("own")
        s_out = st.sem("stored")

        with st.step() as block:
            @block.sync
            def _(sp):
                sp.dma_start(wn[:], W[:, :]).then_inc(s_in, 16)
                sp.dma_start(brow[:], b.rearrange("(a d) -> a d", a=1)).then_inc(s_in, 16)
                sp.dma_start(gb[:, 0, :], wide(gamma)).then_inc(s_in, 16)
                sp.dma_start(gb[:, 1, :], wide(beta)).then_inc(s_in, 16)
                sp.wait_ge(s_in, 64)

            @block.vector
            def _(dve):
                nc.vector.memset(ones[:], 1.0).then_inc(s_h, 1)
                dve.wait_ge(s_tp, 1)
                nc.vector.tensor_copy(wT[:], tp[0][:, 0, :]).then_inc(s_h, 1)
                dve.wait_ge(s_h, 2)

            @block.tensor
            def _(pe):
                pe.wait_ge(s_in, 64)
                nc.tensor.transpose(tp[0][:, 0, :], wn[:], c.ident[:]).then_inc(s_tp, 1)

        frames = bass.AP(x.tensor, 0, [[TIN * DIN, B], [DIN, HT], [HT * DIN, 2], [1, K]])
        with nc.Fori(0, B // NBI) as i, st.step() as block:
            @block.sync
            def _(sp):
                for k in range(NBI):
                    sp.dma_start(fr[:, 2 * k:2 * k + 2, :], frames[i * NBI + k]).then_inc(s_in, 16)

            @block.tensor
            def _(pe):
                pe.wait_ge(s_in, 16 * NBI)
                for j in range(CT):
                    nc.tensor.transpose(tp[j // 4][:, j % 4, 0:HT], fr[:, j, :],
                                        c.ident[0:HT, 0:HT]).then_inc(s_tp, 1)
                for j in range(CT):
                    pe.wait_ge(s_cp, j // 4 + 1)
                    nc.tensor.matmul(hp[j // 4][:, j % 4, :], frT[:, j, :], wT[:], start=True, stop=False)
                    nc.tensor.matmul(hp[j // 4][:, j % 4, :], ones[0:1, 0:HT], brow[:], start=False,
                                     stop=True).then_inc(s_mm, 1)

            @block.vector
            def _(dve):
                for g in range(2):
                    dve.wait_ge(s_tp, 4 * g + 4)
                    nc.vector.tensor_copy(frT[:, 4 * g:4 * g + 4, :], tp[g][:, :, 0:HT]).then_inc(s_cp, 1)

            @block.scalar
            def _(act):
                for g in range(2):
                    act.wait_ge(s_mm, 4 * g + 4)
                    nc.scalar.activation(H[:, bass.ds(i * CT + 4 * g, 4), :], hp[g][:], ACT.Relu).then_inc(s_h, 1)

        NG = NT // 4
        with st.step() as block:
            @block.tensor
            def _(pe):
                for g in range(NG):
                    nc.tensor.matmul(acc[:], ones[:], H[:, 4 * g:4 * g + 4, :].rearrange("p a d -> p (a d)"),
                                     start=(g == 0), stop=(g == NG - 1)).then_inc(s_mm, 1)
                for g in range(NG):
                    pe.wait_ge(s_h, g + 1)
                    if g == 0:
                        pe.wait_ge(s_cp, 1)
                    nc.tensor.matmul(acc[:], ones[:], sq2[g % 2][:], start=(g == 0), stop=(g == NG - 1)).then_inc(s_mm, 1)

            @block.vector
            def _(dve):
                own = Chain(dve, s_own)
                dve.wait_ge(s_mm, NG)
                own(nc.vector.tensor_reduce(mean[:], acc[:].rearrange("p (a d) -> p d a", a=4), AX.X, ALU.add))
                nc.vector.tensor_scalar(mean[:], mean[:], 1.0 / N, None, ALU.mult).then_inc(s_cp, 1)
                dve.wait_ge(s_cp, 1)
                for g in range(NG):
                    t = H[:, 4 * g:4 * g + 4, :]
                    own(nc.vector.tensor_tensor(t, t, mean[0:HT, None, :].to_broadcast([HT, 4, D]), ALU.subtract))
                    if g >= 2:
                        dve.wait_ge(s_mm, NG + g - 1)
                    u = t.rearrange("p a d -> p (a d)")
                    nc.vector.tensor_tensor(sq2[g % 2][:], u, u, ALU.mult).then_inc(s_h, 1)
                dve.wait_ge(s_mm, 2 * NG)
                own(nc.vector.tensor_reduce(var[:], acc[:].rearrange("p (a d) -> p d a", a=4), AX.X, ALU.add))
                nc.vector.tensor_scalar(var[:], var[:], 1.0 / N, EPS, ALU.mult, ALU.add).then_inc(s_cp, 1)
                dve.wait_ge(s_tp, 1)
                own(nc.vector.reciprocal(var[:], var[:]))
                own(nc.vector.tensor_tensor(var[:], var[:], gb[:, 0, :], ALU.mult))
                for g in range(8):
                    t = H[:, 16 * g:16 * g + 16, :]
                    own(nc.vector.tensor_tensor(t, t, var[0:HT, None, :].to_broadcast([HT, 16, D]), ALU.mult))
                    nc.vector.tensor_tensor(t, t, gb[0:HT, None, 1, :].to_broadcast([HT, 16, D]), ALU.add).then_inc(s_in, 1)

            @block.scalar
            def _(act):
                act.wait_ge(s_cp, 2)
                nc.scalar.activation(var[:], var[:], ACT.Sqrt).then_inc(s_tp, 1)

            @block.sync
            def _(sp):
                hv = h_out.rearrange("(j p) d -> p j d", p=HT)
                for g in range(8):
                    sp.wait_ge(s_in, g + 1)
                    sp.dma_start(hv[:, 16 * g:16 * g + 16, :], H[:, 16 * g:16 * g + 16, :]).then_inc(s_out, 16)
                sp.wait_ge(s_out, 16 * 8)


def ln_stage(nc, c, name, src, dst, dstT, gamma=None, beta=None):
    NQ = 4
    with Stage(nc, name) as st:
        h = [st.sb(f"h{q}", [HT, CT, D]) for q in range(NQ)]
        stats = [st.sb(f"stats{q}", [HT, CT, 6]) for q in range(NQ)]
        mv = [st.sb(f"mv{q}", [HT, CT, 2]) for q in range(NQ)]
        rstd = [st.sb(f"rstd{q}", [HT, CT]) for q in range(NQ)]
        xT = [st.sb(f"xT{q}", [D, CT, HT]) for q in range(NQ)]
        tp = [st.ps(f"tp{i}", [D, 4, 128]) for i in range(4)]
        gb = st.sb("gb", [HT, 2, D])
        epsc = st.sb("eps", [HT, 1])
        s_w = st.sem("weights")
        s_in = [st.sem(f"loaded{q}") for q in range(NQ)]
        s_mv = [st.sem(f"var_ready{q}") for q in range(NQ)]
        s_sq = st.sem("root_ready")
        s_own = st.sem("own")
        s_x = st.sem("x_ready")
        s_tp = st.sem("transposed")
        s_cp = st.sem("xT_ready")
        s_out = st.sem("stored")
        with st.step() as block:
            @block.sync
            def _(sp):
                if gamma is not None:
                    sp.dma_start(gb[:, 0, :], wide(gamma, HT)).then_inc(s_w, 16)
                    sp.dma_start(gb[:, 1, :], wide(beta, HT)).then_inc(s_w, 16)
                    sp.wait_ge(s_w, 32)

            @block.vector
            def _(dve):
                nc.vector.memset(epsc[:], EPS).then_inc(s_own, 1)
                dve.wait_ge(s_own, 1)
        srcv, dstv = tiles_of(src), None if dst is None else tiles_of(dst)
        XN = CT if gamma is None else 1
        with nc.Fori(0, B // NBI // NQ) as i, st.step() as block:
            @block.sync
            def _(sp):
                for q in range(NQ):
                    for k in range(NBI):
                        sp.dma_start(h[q][:, 2 * k:2 * k + 2, :], srcv[(i * NQ + q) * NBI + k]).then_inc(s_in[q], 16)
                for q in range(NQ):
                    sp.wait_ge(s_x, XN * (q + 1))
                    for k in range(NBI if dst is not None else 0):
                        sp.dma_start(dstv[(i * NQ + q) * NBI + k], h[q][:, 2 * k:2 * k + 2, :]).then_inc(s_out, 16)
                    if dstT is not None:
                        sp.wait_ge(s_cp, 2 * (q + 1))
                        sp.dma_start(dstT[:, bass.ds((i * NQ + q) * (CT * HT), CT * HT)],
                                     xT[q][:].rearrange("p a d -> p (a d)")).then_inc(s_out, 16)
                sp.wait_ge(s_out, 16 * NQ * (NBI * (dst is not None) + (dstT is not None)))

            @block.vector
            def _(dve):
                own = Chain(dve, s_own)

                def statistics(q):
                    dve.wait_ge(s_in[q], 16 * NBI)
                    for k in range(CT):
                        nc.vector.bn_stats(stats[q][:, k, :], h[q][:, k, :]).then_inc(s_mv[q], 1)
                    dve.wait_ge(s_mv[q], CT)
                    for k in range(CT):
                        nc.vector.bn_aggr(mv[q][:, k, :], stats[q][:, k, :]).then_inc(s_mv[q], 1)

                def scale(q):
                    dve.wait_ge(s_sq, q + 1)
                    own(nc.vector.reciprocal(rstd[q][:], rstd[q][:]))
                    for k in range(CT):
                        ins = nc.vector.tensor_scalar(h[q][:, k, :], h[q][:, k, :], mv[q][:, k, 0:1], rstd[q][:, k:k + 1],
                                                      ALU.subtract, ALU.mult)
                        ins.then_inc(s_x if gamma is None else s_own, 1)
                    if gamma is not None:
                        own.n += CT
                        dve.wait_ge(s_own, own.n)
                        wb = lambda k: gb[:, None, k, :].to_broadcast([HT, CT, D])
                        own(nc.vector.tensor_tensor(h[q][:], h[q][:], wb(0), ALU.mult))
                        nc.vector.tensor_tensor(h[q][:], h[q][:], wb(1), ALU.add).then_inc(s_x, 1)

                statistics(0)
                for q in range(NQ):
                    if q + 1 < NQ:
                        statistics(q + 1)
                    scale(q)

            @block.scalar
            def _(act):
                def roots(q):
                    act.wait_ge(s_mv[q], 2 * CT)
                    nc.scalar.activation(rstd[q][:], mv[q][:, :, 1], ACT.Sqrt, bias=epsc[:, 0:1]).then_inc(s_sq, 1)

                roots(0)
                for q in range(NQ):
                    if q + 1 < NQ:
                        roots(q + 1)
                    for g in range(2 if dstT is not None else 0):
                        act.wait_ge(s_tp, 2 * q + g + 1)
                        nc.scalar.activation(xT[q][:, 4 * g:4 * g + 4, :], tp[2 * (q % 2) + g][:, :, 0:HT], ACT.Copy).then_inc(s_cp, 1)

            @block.tensor
            def _(pe):
                for q in range(NQ if dstT is not None else 0):
                    for g in range(2):
                        if q >= 2:
                            pe.wait_ge(s_cp, 2 * (q - 2) + g + 1)
                        for k in range(4):
                            pe.wait_ge(s_x, XN * q + (4 * g + k + 1 if gamma is None else 1))
                            ins = nc.tensor.transpose(tp[2 * (q % 2) + g][:, k, 0:HT], h[q][:, 4 * g + k, :], c.ident[0:HT, 0:HT])
                        ins.then_inc(s_tp, 1)


SN = 64
SC = 8
CH = 8
KP = HT + T


def s4_constants():
    import numpy as np
    l = np.arange(T)
    half = np.pi * l / T
    j = np.arange(T)
    phase = 2 * np.pi * ((np.outer(l, j)) % T) / T + half[:, None]
    cos = np.cos(half)
    cos[T // 2] = 0.0
    f = np.float32
    return {"s4_cos": cos.astype(f), "s4_sin": np.sin(half).astype(f),
            "s4_dft_re": (np.cos(phase) / T).astype(f), "s4_dft_im": (-np.sin(phase) / T).astype(f)}


def s4_kernel_stage(nc, c, Lre, Lim, P, Bm, C, Dv, log_step, cos, sin, dre, dim, kpad):
    with Stage(nc, "s4k") as st:
        lr = st.sb("lr", [D, SN])
        pbc = st.sb("pbc", [D, 3, SN, 2])
        ls = st.sb("ls", [D, 1])
        dcol = st.sb("dcol", [D, 1])
        q = st.sb("q", [D, 11, 2, SN])
        t1 = st.sb("t1", [D, SN])
        tps = [st.ps(f"tp{i}", [D, 4, D]) for i in range(3)]
        coef = st.sb("coef", [D, 3, SN])
        v = st.sb("v", [D, 2, SN, 2, 8])
        cosb = st.sb("cosb", [D, T])
        sinb = st.sb("sinb", [D, T])
        ctheta = st.sb("ctheta", [HT, 2])
        dft = st.sb("dft", [HT, 2, 2, T])
        den = st.sb("den", [D, 2, SC, T])
        m1 = st.sb("m1", [D, SC, T])
        m2 = st.sb("m2", [D, SC, T])
        sp_ = [st.ps(f"s{i}", [HT, SC, 2, 8]) for i in range(2)]
        S = st.sb("S", [HT, 2, 2, SN, 8])
        w = [st.sb(f"w{i}", [HT, 2, D]) for i in range(8)]
        kps = st.ps("kps", [D, T])
        K = st.sb("K", [D, KP])
        s_in = st.sem("loaded")
        s_own = st.sem("own")
        s_act = st.sem("act")
        s_q = st.sem("columns_ready")
        s_tp = st.sem("transposed")
        s_r = st.sem("r_ready")
        s_mm = st.sem("summed")
        s_out = st.sem("stored")

        with st.step() as block:
            @block.sync
            def _(sp):
                sp.dma_start(lr[:], Lre[:, :]).then_inc(s_in, 16)
                sp.dma_start(q[:, 1, 0, :], Lim[:, :]).then_inc(s_in, 16)
                for k, x in enumerate((P, Bm, C)):
                    sp.dma_start(pbc[:, k, :, :], x[:, :, :]).then_inc(s_in, 16)
                sp.dma_start(ls[:], log_step.rearrange("(h a) -> h a", a=1)).then_inc(s_in, 16)
                sp.dma_start(dcol[:], Dv.rearrange("(h a) -> h a", a=1)).then_inc(s_in, 16)
                sp.dma_start(cosb[:], wide(cos)).then_inc(s_in, 16)
                sp.dma_start(sinb[:], wide(sin)).then_inc(s_in, 16)
                for k in range(2):
                    sp.dma_start(ctheta[:, k:k + 1], cos[k * HT:(k + 1) * HT].rearrange("(p a) -> p a", a=1)).then_inc(s_in, 16)
                    sp.dma_start(dft[:, 0, k, :], dre[k * HT:(k + 1) * HT, :]).then_inc(s_in, 16)
                    sp.dma_start(dft[:, 1, k, :], dim[k * HT:(k + 1) * HT, :]).then_inc(s_in, 16)
                sp.wait_ge(s_in, 16 * 15)

            @block.scalar
            def _(act):
                act.wait_ge(s_in, 16 * 15)
                nc.scalar.activation(ls[:], ls[:], ACT.Exp, scale=-1.0).then_inc(s_act, 1)

            @block.vector
            def _(dve):
                own = Chain(dve, s_own)
                V = nc.vector
                dve.wait_ge(s_in, 16 * 15)
                own(V.memset(v[:], 0.0))
                own(V.memset(K[:, 0:HT], 0.0))
                own(V.tensor_scalar(q[:, 0, 0, :], lr[:], -0.0001, -1.0, ALU.min, ALU.mult))
                dve.wait_ge(s_act, 1)
                own(V.tensor_scalar(q[:, 2, 0, :], lr[:], 0.0, 2.0, ALU.mult, ALU.add))
                own(V.tensor_scalar(q[:, 2, 0, :], q[:, 2, 0, :], ls[:, 0:1], None, ALU.mult))
                re = lambda k: pbc[:, k, :, 0]
                im = lambda k: pbc[:, k, :, 1]
                for n, (x, y) in enumerate(((2, 1), (2, 0), (0, 1), (0, 0))):
                    own(V.tensor_tensor(t1[:], im(x), im(y), ALU.mult))
                    own(V.tensor_tensor(q[:, 3 + n, 0, :], re(x), re(y), ALU.mult))
                    own(V.tensor_tensor(q[:, 3 + n, 0, :], q[:, 3 + n, 0, :], t1[:], ALU.add))
                    own(V.tensor_tensor(t1[:], im(x), re(y), ALU.mult))
                    own(V.tensor_tensor(q[:, 7 + n, 0, :], re(x), im(y), ALU.mult))
                    own(V.tensor_tensor(q[:, 7 + n, 0, :], q[:, 7 + n, 0, :], t1[:], ALU.subtract))
                V.tensor_copy(q[:, :, 1, :], q[:, :, 0, :]).then_inc(s_q, 1)
                dve.wait_ge(s_tp, 11)
                tp = lambda k: tps[k // 4][:, k % 4, :]
                for g in range(2):
                    r = slice(64 * g, 64 * g + 64)
                    for k in range(3):
                        own(V.tensor_copy(coef[r, k, :], tp(k)[r, r]))
                    for n in range(4):
                        own(V.tensor_copy(v[r, 0, :, g, 2 * n], tp(3 + n)[r, r]))
                        own(V.tensor_copy(v[r, 0, :, g, 2 * n + 1], tp(7 + n)[r, r]))
                        own(V.tensor_copy(v[r, 1, :, g, 2 * n], tp(7 + n)[r, r]))
                        own(V.tensor_scalar(v[r, 1, :, g, 2 * n + 1], tp(3 + n)[r, r], -1.0, None, ALU.mult))

            @block.tensor
            def _(pe):
                pe.wait_ge(s_q, 1)
                for k in range(11):
                    nc.tensor.transpose(tps[k // 4][:, k % 4, :], q[:, k, :, :].rearrange("p a n -> p (a n)"),
                                        c.ident[:]).then_inc(s_tp, 1)

        with nc.Fori(0, SN // SC) as i, st.step() as block:
            full = [D, SC, T]

            @block.vector
            def _(dve):
                own = Chain(dve, s_own)
                V = nc.vector
                cf = lambda k: coef[:, k, bass.ds(i * SC, SC)].unsqueeze(2).to_broadcast(full)
                cs = cosb[:, None, :].to_broadcast(full)
                sn = sinb[:, None, :].to_broadcast(full)
                own(V.tensor_tensor(den[:, 0], cf(0), cs, ALU.mult))
                own(V.tensor_tensor(m1[:], cf(2), sn, ALU.mult))
                own(V.tensor_tensor(m2[:], cf(1), cs, ALU.mult))
                own(V.tensor_tensor(den[:, 1], m1[:], m2[:], ALU.subtract))
                own(V.tensor_tensor(m1[:], den[:, 0], den[:, 0], ALU.mult))
                own(V.tensor_tensor(m2[:], den[:, 1], den[:, 1], ALU.mult))
                own(V.tensor_tensor(m1[:], m1[:], m2[:], ALU.add))
                own(V.reciprocal(m1[:], m1[:]))
                own(V.tensor_tensor(den[:, 0], den[:, 0], m1[:], ALU.mult))
                V.tensor_tensor(den[:, 1], den[:, 1], m1[:], ALU.mult).then_inc(s_r, 1)
                for k in range(2):
                    dve.wait_ge(s_mm, SC * 2 * (k + 1))
                    own(V.tensor_copy(S[:, k, :, bass.ds(i * SC, SC), :], sp_[k][:].rearrange("p i g q -> p g i q")))

            @block.tensor
            def _(pe):
                pe.wait_ge(s_r, 1)
                for k in range(2):
                    for n in range(SC):
                        for part in range(2):
                            nc.tensor.matmul(sp_[k][:, n, :, :].rearrange("p g q -> p (g q)"), den[:, part, n, k * HT:(k + 1) * HT],
                                             v[:, part, bass.ds(i * SC + n, 1), :, :].rearrange("p a g q -> p (a g q)"),
                                             start=(part == 0), stop=(part == 1)).then_inc(s_mm, 1)

        with st.step() as block:
            @block.vector
            def _(dve):
                own = Chain(dve, s_own)
                V = nc.vector
                s = lambda n: S[:, :, :, :, n].rearrange("p c g i -> p c (g i)")
                cb = ctheta[:, :].unsqueeze(2).to_broadcast([HT, 2, D])
                tt = lambda o, a, b, op: own(V.tensor_tensor(o, a, b, op))
                W = [x[:] for x in w]
                tt(W[0], s(6), cb, ALU.mult)
                own(V.tensor_scalar(W[0], W[0], 1.0, None, ALU.add))
                tt(W[1], s(7), cb, ALU.mult)
                tt(W[2], s(2), s(4), ALU.mult)
                tt(W[3], s(3), s(5), ALU.mult)
                tt(W[2], W[2], W[3], ALU.subtract)
                tt(W[3], s(2), s(5), ALU.mult)
                tt(W[4], s(3), s(4), ALU.mult)
                tt(W[3], W[3], W[4], ALU.add)
                tt(W[4], W[0], W[0], ALU.mult)
                tt(W[5], W[1], W[1], ALU.mult)
                tt(W[4], W[4], W[5], ALU.add)
                own(V.reciprocal(W[4], W[4]))
                tt(W[4], W[4], cb, ALU.mult)
                tt(W[5], W[2], W[0], ALU.mult)
                tt(W[6], W[3], W[1], ALU.mult)
                tt(W[5], W[5], W[6], ALU.add)
                tt(W[5], W[5], W[4], ALU.mult)
                tt(W[6], W[3], W[0], ALU.mult)
                tt(W[7], W[2], W[1], ALU.mult)
                tt(W[6], W[6], W[7], ALU.subtract)
                tt(W[6], W[6], W[4], ALU.mult)
                tt(W[5], s(0), W[5], ALU.subtract)
                V.tensor_tensor(W[6], s(1), W[6], ALU.subtract).then_inc(s_r, 1)
                dve.wait_ge(s_mm, 4)
                own(V.tensor_copy(K[:, HT:KP], kps[:]))
                V.tensor_tensor(K[:, HT:HT + 1], K[:, HT:HT + 1], dcol[:], ALU.add).then_inc(s_q, 1)

            @block.tensor
            def _(pe):
                pe.wait_ge(s_r, 1)
                for n in range(4):
                    nc.tensor.matmul(kps[:], w[5 + n // 2][:, n % 2, :], dft[:, n // 2, n % 2, :], start=(n == 0),
                                     stop=(n == 3)).then_inc(s_mm, 1)

            @block.sync
            def _(sp):
                sp.wait_ge(s_q, 1)
                sp.dma_start(kpad[:, :], K[:]).then_inc(s_out, 16)
                sp.wait_ge(s_out, 16)


def s4_conv_stage(nc, c, xn, kpad, h, h_out):
    with Stage(nc, "s4c") as st:
        H = st.sb("H", [HT, NT, D])
        U = st.sb("U", [HT, B, 2, D])
        tz = st.sb("tz", [HT, CH, T])
        flip = st.sb("flip", [HT, HT])
        y = [st.ps(f"y{i}", [HT, CH, B]) for i in range(2)]
        s_in = st.sem("loaded")
        s_t = st.sem("toeplitz_loaded")
        s_mm = st.sem("multiplied")
        s_h = st.sem("added")
        s_out = st.sem("stored")
        hv = lambda x: x.rearrange("(j p) d -> p j d", p=HT)
        with st.step() as block:
            @block.sync
            def _(sp):
                for g in range(8):
                    r = slice(16 * g, 16 * g + 16)
                    sp.dma_start(H[:, r, :], hv(h)[:, r, :]).then_inc(s_in, 16)
                    sp.dma_start(U[:, 8 * g:8 * g + 8, :, :].rearrange("p b c d -> p (b c) d"), hv(xn)[:, r, :]).then_inc(s_in, 16)
                sp.wait_ge(s_in, 16 * 16)

            @block.gpsimd
            def _(pool):
                nc.gpsimd.memset(flip[:], 0.0).then_inc(s_h, 1)
                pool.wait_ge(s_h, 1)
                nc.gpsimd.affine_select(out=flip[:], in_=flip[:], compare_op=ALU.not_equal, fill=1.0, base=1 - HT,
                                        pattern=[[1, HT]], channel_multiplier=1).then_inc(s_h, 1)
                pool.wait_ge(s_h, 2)

        Uf = U[:].rearrange("p b c d -> p (b c d)")
        with nc.Fori(0, NT // 8) as i, st.step() as block:
            @block.tensor
            def _(pe):
                for k in range(2):
                    nc.tensor.matmul(y[k][:].rearrange("p n b -> p (n b)"), flip[:], Uf[:, bass.ds(i * (8 * D) + k * 4 * D, 4 * D)],
                                     start=True, stop=True).then_inc(s_mm, 1)

            @block.vector
            def _(dve):
                for k in range(2):
                    dve.wait_ge(s_mm, k + 1)
                    nc.vector.tensor_copy(Uf[:, bass.ds(i * (8 * D) + k * 4 * D, 4 * D)], y[k][:].rearrange("p n b -> p (n b)")).then_inc(s_h, 1)
                dve.wait_ge(s_h, 2)
        toep = bass.AP(kpad.tensor, 1, [[KP, D], [1, HT], [1, T]])
        with nc.Fori(0, D // CH) as i, st.step() as block:
            @block.sync
            def _(sp):
                sp.dma_start(tz[:], toep[bass.ds(i * CH, CH)].rearrange("h p t -> p h t")).then_inc(s_t, 16)

            @block.tensor
            def _(pe):
                pe.wait_ge(s_t, 16)
                u = lambda n, k: U[:, :, k, bass.ds(i * CH + n, 1)].rearrange("p b a -> p (b a)")
                for n in range(CH):
                    nc.tensor.matmul(y[0][:, n, :], tz[:, n, 0:HT], u(n, 0), start=True, stop=True)
                    nc.tensor.matmul(y[1][:, n, :], tz[:, n, HT:T], u(n, 0), start=True, stop=False)
                    nc.tensor.matmul(y[1][:, n, :], tz[:, n, 0:HT], u(n, 1), start=False, stop=True).then_inc(s_mm, 1)

            @block.vector
            def _(dve):
                dve.wait_ge(s_mm, CH)
                for k in range(2):
                    hk = H[:, :, bass.ds(i * CH, CH)].rearrange("p (b c) d -> p b c d", c=2)[:, :, k, :]
                    nc.vector.tensor_tensor(hk, hk, y[k][:].rearrange("p n b -> p b n"), ALU.add).then_inc(s_h, 1)
                dve.wait_ge(s_h, 2)
        with st.step() as block:
            @block.sync
            def _(sp):
                for g in range(8):
                    r = slice(16 * g, 16 * g + 16)
                    sp.dma_start(hv(h_out)[:, r, :], H[:, r, :]).then_inc(s_out, 16)
                sp.wait_ge(s_out, 16 * 8)


def route_stage(nc, c, name, E, cap, xn, xnT, Wr, br, xp, idx_out):
    C = 128 // E
    TC = NT // C
    M = TC * HT
    G = cap // HT
    with Stage(nc, name) as st:
        L = st.sb("L", [HT, NT, E])
        PT = st.sb("PT", [128, M])
        s1 = st.sb("s1", [128, M])
        s2 = st.sb("s2", [128, M])
        one = st.sb("one", [128, M], BF16)
        wr = st.sb("wr", [D, E])
        brow = st.sb("brow", [1, E])
        onerow = st.sb("onerow", [1, HT])
        NQ = 4
        xt = st.sb("xt", [D, NQ, CT * HT])
        red = st.sb("red", [HT, 2, NT])
        same = st.sb("same", [128, 128])
        before = st.sb("before", [128, 128])
        tau = st.sb("tau", [128, 1])
        cand = st.sb("cand", [128, 1])
        bit = st.sb("bit", [128, 1], I32)
        cnt = st.sb("cnt", [128, 2])
        mask = st.sb("mask", [128, 2])
        stg = st.sb("stg", [128, 4, 128])
        iop = st.sb("iop", [HT, HT], BF16)
        ios = st.sb("ios", [HT, G], F32)
        tid = st.sb("tid", [HT, NT])
        qid = st.sb("qid", [HT, 1])
        hi_i = st.sb("hi_i", [HT, NT, E], I32)
        hi = st.sb("hi", [HT, NT, E])
        lo = st.sb("lo", [HT, NT, E], BF16)
        TS = 8
        A = st.sb("A", [HT, TS, E, HT], BF16)
        Bv = st.sb("Bv", [HT, TS, E, 2, G], BF16)
        lst = st.sb("lst", [HT, E, 2, G])
        idx = st.sb("idx", [HT, E, G], U32)
        lp = [st.ps(f"lp{i}", [HT, CT, E]) for i in range(2)]
        tp = st.ps("tp", [128, 4, 128])
        cp = st.ps("cp", [128, 2])
        ip = st.ps("ip", [HT, E * 2 * G])
        s_xt = [st.sem(f"chunk_loaded{q}") for q in range(NQ)]
        s_in = st.sem("loaded")
        s_own = st.sem("own")
        s_pool = st.sem("constants")
        s_pown = st.sem("pool_own")
        s_mm = st.sem("multiplied")
        s_act = st.sem("act")
        s_x = st.sem("dve_ready")
        s_out = st.sem("stored")
        V = nc.vector
        grp = lambda m: m[:].rearrange("p (e c) -> p e c", c=C)

        with st.step() as block:
            @block.sync
            def _(sp):
                sp.dma_start(wr[:], Wr[:, :]).then_inc(s_in, 16)
                if br is not None:
                    sp.dma_start(brow[:], br.rearrange("(a d) -> a d", a=1)).then_inc(s_in, 16)
                for k in range(8):
                    r = slice(k * (N // 8), (k + 1) * (N // 8))
                    sp.dma_start(xp[r, 0:D], xn[r, :]).then_inc(s_in, 16)
                sp.wait_ge(s_in, 16 * (9 + (br is not None)))

            @block.vector
            def _(dve):
                own = Chain(dve, s_own)
                if br is None:
                    own(V.memset(brow[:], 0.0))
                own(V.memset(onerow[:], 1.0))
                own(V.memset(tau[:], 0.0))
                own(V.memset(bit[:], 1 << 29))
                own(V.memset(lst[:], 0.0))

            @block.gpsimd
            def _(pool):
                own = Chain(pool, s_pown)
                P = nc.gpsimd
                own(P.memset(same[:], 1.0))
                own(P.affine_select(out=grp(same), in_=grp(same), compare_op=ALU.is_ge, fill=0.0, base=0,
                                    pattern=[[-C, E], [0, C]], channel_multiplier=1))
                own(P.affine_select(out=grp(same), in_=grp(same), compare_op=ALU.is_ge, fill=0.0, base=C - 1,
                                    pattern=[[C, E], [0, C]], channel_multiplier=-1))
                own(P.affine_select(out=grp(before), in_=grp(same), compare_op=ALU.is_gt, fill=0.0, base=0,
                                    pattern=[[C, E], [1, C]], channel_multiplier=-1))
                own(P.memset(one[:], 1.0))
                own(P.iota(iop[:], pattern=[[1, HT]], base=0, channel_multiplier=0, allow_small_or_imprecise_dtypes=True))
                own(P.iota(ios[:], pattern=[[1, G]], base=0, channel_multiplier=0, allow_small_or_imprecise_dtypes=True))
                own(P.iota(tid[:], pattern=[[1, NT]], base=0, channel_multiplier=0, allow_small_or_imprecise_dtypes=True))
                own(P.iota(qid[:], pattern=[[0, 1]], base=0, channel_multiplier=1, allow_small_or_imprecise_dtypes=True))

        with nc.Fori(0, NT // CT // NQ) as i, st.step() as block:
            @block.sync
            def _(sp):
                for q in range(NQ):
                    sp.dma_start(xt[:, q, :], xnT[:, bass.ds((i * NQ + q) * (CT * HT), CT * HT)]).then_inc(s_xt[q], 16)

            @block.tensor
            def _(pe):
                for q in range(NQ):
                    pe.wait_ge(s_xt[q], 16)
                    if q >= 2:
                        pe.wait_ge(s_x, q - 1)
                    for k in range(CT):
                        nc.tensor.matmul(lp[q % 2][:, k, :], xt[:, q, k * HT:(k + 1) * HT], wr[:], start=True, stop=False)
                        ins = nc.tensor.matmul(lp[q % 2][:, k, :], onerow[:], brow[:], start=False, stop=True)
                    ins.then_inc(s_mm, 1)

            @block.vector
            def _(dve):
                for q in range(NQ):
                    dve.wait_ge(s_mm, q + 1)
                    V.tensor_copy(L[:, bass.ds((i * NQ + q) * CT, CT), :], lp[q % 2][:]).then_inc(s_x, 1)
                dve.wait_ge(s_x, NQ)

        with st.step() as block:
            @block.vector
            def _(dve):
                own = Chain(dve, s_own)
                rb = lambda k: red[:, k, :].unsqueeze(2).to_broadcast([HT, NT, E])
                own(V.tensor_reduce(red[:, 0, :], L[:], AX.X, ALU.max))
                V.tensor_tensor(L[:], L[:], rb(0), ALU.subtract).then_inc(s_x, 1)
                dve.wait_ge(s_act, 1)
                own(V.tensor_reduce(red[:, 1, :], L[:], AX.X, ALU.add))
                own(V.reciprocal(red[:, 1, :], red[:, 1, :]))
                V.tensor_tensor(L[:], L[:], rb(1), ALU.mult).then_inc(s_x, 1)

            @block.scalar
            def _(act):
                act.wait_ge(s_x, 1)
                nc.scalar.activation(L[:], L[:], ACT.Exp).then_inc(s_act, 1)

            @block.sync
            def _(sp):
                sp.wait_ge(s_x, 2)
                for k in range(8):
                    sp.dma_start(xp.rearrange("(j p) d -> p j d", p=HT)[:, 16 * k:16 * k + 16, D:D + E],
                                 L[:, 16 * k:16 * k + 16, :]).then_inc(s_out, 16)
                sp.wait_ge(s_out, 16 * 8)

        Lc = L[:].rearrange("p (c i) e -> p i e c", c=C)
        with nc.Fori(0, TC // 4) as i, st.step() as block:
            @block.vector
            def _(dve):
                for k in range(4):
                    V.tensor_copy(stg[0:HT, k, :].rearrange("p (a e c) -> p a e c", a=1, c=C),
                                  Lc[:, bass.ds(i * 4 + k, 1)]).then_inc(s_x, 1)
                dve.wait_ge(s_mm, 4)
                V.tensor_copy(PT[:, bass.ds(i * (4 * HT), 4 * HT)].rearrange("p (a t) -> p a t", a=4),
                              tp[:, :, 0:HT]).then_inc(s_x, 1)
                dve.wait_ge(s_x, 5)

            @block.tensor
            def _(pe):
                for k in range(4):
                    pe.wait_ge(s_x, k + 1)
                    nc.tensor.transpose(tp[:, k, 0:HT], stg[0:HT, k, :], c.ident[0:HT, 0:HT]).then_inc(s_mm, 1)

        with nc.Fori(0, 30) as i, st.step() as block:
            @block.vector
            def _(dve):
                own = Chain(dve, s_own)
                own(V.tensor_tensor(cand[:].bitcast(I32), tau[:].bitcast(I32), bit[:], ALU.bitwise_or))
                own(V.tensor_scalar(bit[:], bit[:], 1, None, ALU.logical_shift_right))
                V.tensor_scalar(s1[:], PT[:], cand[:, 0:1], None, ALU.is_ge, ALU.add, accum_out=cnt[:, 0:1]).then_inc(s_x, 1)
                dve.wait_ge(s_mm, 1)
                own(V.tensor_scalar(mask[:, 0:1], cp[:, 0:1], float(cap), cand[:, 0:1], ALU.is_ge, ALU.mult))
                own(V.tensor_tensor(tau[:], tau[:], mask[:, 0:1], ALU.max))

            @block.tensor
            def _(pe):
                pe.wait_ge(s_x, 1)
                nc.tensor.matmul(cp[:, 0:1], same[:], cnt[:, 0:1], start=True, stop=True).then_inc(s_mm, 1)

        with st.step() as block:
            @block.vector
            def _(dve):
                own = Chain(dve, s_own)
                own(V.tensor_scalar(s1[:], PT[:], tau[:, 0:1], None, ALU.is_gt, ALU.add, accum_out=cnt[:, 0:1]))
                V.tensor_scalar(s2[:], PT[:], tau[:, 0:1], None, ALU.is_equal, ALU.add, accum_out=cnt[:, 1:2]).then_inc(s_x, 1)
                dve.wait_ge(s_mm, 2)
                own(V.tensor_scalar(mask[:, 0:1], cp[:, 0:1], -1.0, float(cap), ALU.mult, ALU.add))
                own(V.tensor_copy(mask[:, 1:2], cp[:, 1:2]))
                own(V.tensor_tensor_scan(PT[:], one[:], s2[:], mask[:, 1:2], ALU.mult, ALU.add))
                own(V.tensor_scalar(PT[:], PT[:], mask[:, 0:1], None, ALU.is_le))
                own(V.tensor_tensor(s2[:], s2[:], PT[:], ALU.mult))
                own(V.tensor_tensor(s1[:], s1[:], s2[:], ALU.add))
                V.tensor_reduce(cnt[:, 0:1], s1[:], AX.X, ALU.add).then_inc(s_x, 1)
                dve.wait_ge(s_mm, 3)
                own(V.tensor_copy(mask[:, 1:2], cp[:, 1:2]))
                own(V.tensor_tensor_scan(PT[:], one[:], s1[:], mask[:, 1:2], ALU.mult, ALU.add))
                own(V.tensor_tensor(PT[:], PT[:], s1[:], ALU.mult))
                own(V.tensor_scalar(PT[:], PT[:], -1.0, None, ALU.add))

            @block.tensor
            def _(pe):
                pe.wait_ge(s_x, 1)
                nc.tensor.matmul(cp[:, 0:1], same[:], cnt[:, 0:1], start=True, stop=True).then_inc(s_mm, 1)
                nc.tensor.matmul(cp[:, 1:2], before[:], cnt[:, 1:2], start=True, stop=True).then_inc(s_mm, 1)
                pe.wait_ge(s_x, 2)
                nc.tensor.matmul(cp[:, 1:2], before[:], cnt[:, 0:1], start=True, stop=True).then_inc(s_mm, 1)

        with nc.Fori(0, TC // 4) as i, st.step() as block:
            @block.vector
            def _(dve):
                V.tensor_copy(stg[:, :, 0:HT], PT[:, bass.ds(i * (4 * HT), 4 * HT)].rearrange("p (a t) -> p a t", a=4)).then_inc(s_x, 1)
                for k in range(4):
                    dve.wait_ge(s_mm, 4)
                    V.tensor_copy(Lc[:, bass.ds(i * 4 + k, 1)],
                                  tp[0:HT, k, :].rearrange("p (a e c) -> p a e c", a=1, c=C)).then_inc(s_x, 1)
                dve.wait_ge(s_x, 5)

            @block.tensor
            def _(pe):
                pe.wait_ge(s_x, 1)
                for k in range(4):
                    nc.tensor.transpose(tp[0:HT, k, :], stg[:, k, 0:HT], c.ident[:]).then_inc(s_mm, 1)

        with st.step() as block:
            @block.vector
            def _(dve):
                own = Chain(dve, s_own)
                own(V.tensor_scalar(hi[:], L[:], 0.0, -1.0, ALU.is_ge, ALU.add))
                for g in range(1, G):
                    own(V.scalar_tensor_tensor(hi[:], L[:], float(g * HT), hi[:], ALU.is_ge, ALU.add))
                own(V.scalar_tensor_tensor(lo[:], hi[:], -float(HT), L[:], ALU.mult, ALU.add))

        with nc.Fori(0, NT // TS) as i, st.step() as block:
            @block.vector
            def _(dve):
                own = Chain(dve, s_own)
                js = bass.ds(i * TS, TS)
                ae = lambda v: Bv[:, :, :, v, :].rearrange("p a e g -> p (a e) g")
                full = [HT, TS * E, G]
                hj = hi[:, js, :].rearrange("p a e -> p (a e)").unsqueeze(2).to_broadcast(full)
                own(V.tensor_tensor(ae(0), hj, ios[:, None, :].to_broadcast(full), ALU.is_equal))
                own(V.tensor_scalar(ae(1), ae(0), qid[:, 0:1], None, ALU.mult))
                eg = Bv[:, :, :, 0, :]
                V.tensor_tensor(eg, eg, tid[:, js, None, None].to_broadcast([HT, TS, E, G]), ALU.mult).then_inc(s_x, 1)
                for k in range(TS):
                    lj = lo[:, bass.ds(i * TS + k, 1), :].rearrange("p a e -> p (a e)").unsqueeze(2).to_broadcast([HT, E, HT])
                    V.tensor_tensor(A[:, k], lj, iop[:, None, :].to_broadcast([HT, E, HT]), ALU.is_equal).then_inc(s_x, 1)
                dve.wait_ge(s_mm, 1)
                lf = lst[:].rearrange("p e v g -> p (e v g)")
                own(V.tensor_tensor(lf, lf, ip[:], ALU.add))

            @block.tensor
            def _(pe):
                for k in range(TS):
                    pe.wait_ge(s_x, k + 2)
                    for e in range(E):
                        ins = nc.tensor.matmul(ip[:, e * 2 * G:(e + 1) * 2 * G], A[:, k, e, :],
                                               Bv[:, k, e].rearrange("p v g -> p (v g)"), start=(k == 0 and e == 0),
                                               stop=(k == TS - 1 and e == E - 1))
                ins.then_inc(s_mm, 1)

        with st.step() as block:
            @block.vector
            def _(dve):
                V.scalar_tensor_tensor(idx[:], lst[:, :, 0, :], float(HT), lst[:, :, 1, :], ALU.mult, ALU.add).then_inc(s_x, 1)

            @block.sync
            def _(sp):
                sp.wait_ge(s_x, 1)
                sp.dma_start(idx_out[:, :, :], idx[:]).then_inc(s_out, 16)
                sp.wait_ge(s_out, 16)


def experts_stage(nc, c, name, E, cap, F, share, fn, xp, idx_in, Wup, bup, Wdn, bdn, acc):
    G = cap // HT
    FC = -(-F // 128)
    fw = [min(128, F - 128 * k) for k in range(FC)]
    R = D + E
    NG = G // 4
    JOBS = share * NG
    with Stage(nc, name) as st:
        idx = st.sb("idx", [HT, E, G], U32)
        ij = st.sb("ij", [HT, JOBS, 4], U32)
        xg = st.sb("xg", [HT, JOBS, 4, R])
        up = st.sb("up", [D, F])
        dn = st.sb("dn", [128, share, FC, D])
        bu = st.sb("bu", [128, FC])
        bd = st.sb("bd", [1, share, D])
        onerow = st.sb("onerow", [1, HT])
        xT = [st.sb(f"xT{i}", [D, 4 * HT]) for i in range(2)]
        a = [st.sb(f"a{i}", [128, FC, 4 * HT]) for i in range(2)]
        y = st.sb("y", [HT, JOBS, 4, D])
        tp = st.ps("tp", [D, 4, 128])
        hp = [st.ps(f"hp{i}", [128, 4 * HT]) for i in range(2)]
        yp = [st.ps(f"yp{i}", [HT, 4, D]) for i in range(2)]
        s_in = st.sem("loaded")
        s_idx = st.sem("indices")
        s_g = [st.pool_sem(f"gathered{k}") for k in range(JOBS)]
        s_tp = st.sem("transposed")
        s_xT = st.sem("xT_ready")
        s_up = st.sem("up_done")
        s_a = st.sem("act_done")
        s_dn = st.sem("down_done")
        s_y = st.sem("y_ready")
        s_sc = st.pool_sem("scattered")
        V = nc.vector
        with st.step() as block:
            @block.sync
            def _(sp):
                sp.dma_start(idx[:], idx_in[:, :, :]).then_inc(s_in, 16)
                sp.wait_ge(s_in, 16)

            @block.vector
            def _(dve):
                V.memset(onerow[:], 1.0).then_inc(s_y, 1)
                dve.wait_ge(s_y, 1)

        with nc.Fori(0, E // share) as i, st.step() as block:
            @block.sync
            def _(sp):
                sp.dma_start(up[:], Wup[i]).then_inc(s_in, 16)
                nf = F // 128
                if nf:
                    sp.dma_start(bu[:, 0:nf], bup[i][0:nf * 128].rearrange("(c p) -> p c", p=128),
                                 allow_slow_non_contiguous=True).then_inc(s_in, 16)
                if fw[-1] < 128:
                    sp.dma_start(bu[0:fw[-1], nf:nf + 1], bup[i][nf * 128:F].rearrange("(p c) -> p c", c=1)).then_inc(s_in, 16)
                for s in range(share):
                    for k in range(FC):
                        sp.dma_start(dn[0:fw[k], s, k, :], Wdn[i * share + s][k * 128:k * 128 + fw[k], :]).then_inc(s_in, 16)
                    sp.dma_start(bd[:, s, :], bdn[bass.ds(i * share + s, 1), :]).then_inc(s_in, 16)
            loads = 16 * (2 + (fw[-1] < 128) + share * (FC + 1))

            @block.gpsimd
            def _(pool):
                pool.wait_ge(s_idx, 1)
                for k in range(JOBS):
                    for t in range(4):
                        nc.gpsimd.indirect_dma_start(xg[:, k, t, :], None, xp[:, :],
                                                     bass.IndirectOffsetOnAxis(ap=ij[:, k, t:t + 1], axis=0)).then_inc(s_g[k], 16)
                for k in range(JOBS):
                    pool.wait_ge(s_y, k + 1)
                    if k % NG == 0 and k > 0:
                        pool.wait_ge(s_sc, 64 * k)
                    for t in range(4):
                        nc.gpsimd.indirect_dma_start(acc[:, :], bass.IndirectOffsetOnAxis(ap=ij[:, k, t:t + 1], axis=0),
                                                     y[:, k, t, :], None, compute_op=ALU.add).then_inc(s_sc, 16)
                pool.wait_ge(s_sc, 64 * JOBS)

            @block.vector
            def _(dve):
                V.tensor_copy(ij[:].rearrange("p (s g) t -> p s (g t)", s=share), idx[:, bass.ds(i * share, share), :]).then_inc(s_idx, 1)
                for k in range(JOBS + 1):
                    if k < JOBS:
                        dve.wait_ge(s_tp, 4 * k + 4)
                        if k >= 2:
                            dve.wait_ge(s_up, FC * (k - 1))
                        V.tensor_copy(xT[k % 2][:].rearrange("p (a t) -> p a t", a=4), tp[:, :, 0:HT]).then_inc(s_xT, 1)
                    if k >= 1:
                        m = k - 1
                        dve.wait_ge(s_dn, m + 1)
                        for t in range(4):
                            gate = xg[:, m, t, bass.ds(D + i * share + m // NG, 1)]
                            ins = V.tensor_scalar(y[:, m, t, :], yp[m % 2][:, t, :], gate, None, ALU.mult)
                        ins.then_inc(s_y, 1)

            @block.scalar
            def _(act):
                act.wait_ge(s_in, loads)
                for k in range(JOBS):
                    for f in range(FC):
                        act.wait_ge(s_up, k * FC + f + 1)
                        if k >= 2:
                            act.wait_ge(s_dn, k - 1)
                        nc.scalar.activation(a[k % 2][0:fw[f], f, :], hp[f % 2][0:fw[f], :], fn,
                                             bias=bu[0:fw[f], f:f + 1]).then_inc(s_a, 1)

            @block.tensor
            def _(pe):
                def turn(k):
                    pe.wait_ge(s_g[k], 64)
                    if k >= 1:
                        pe.wait_ge(s_xT, k)
                    for t in range(4):
                        nc.tensor.transpose(tp[:, t, 0:HT], xg[:, k, t, 0:D], c.ident[0:HT, 0:HT]).then_inc(s_tp, 1)

                turn(0)
                pe.wait_ge(s_in, loads)
                for k in range(JOBS):
                    pe.wait_ge(s_xT, k + 1)
                    for f in range(FC):
                        if k * FC + f >= 2:
                            pe.wait_ge(s_a, k * FC + f - 1)
                        nc.tensor.matmul(hp[f % 2][0:fw[f], :], up[:, f * 128:f * 128 + fw[f]], xT[k % 2][:],
                                         start=True, stop=True).then_inc(s_up, 1)
                    if k + 1 < JOBS:
                        turn(k + 1)
                    pe.wait_ge(s_a, (k + 1) * FC)
                    if k >= 2:
                        pe.wait_ge(s_y, k - 1)
                    s = k // NG
                    for t in range(4):
                        for f in range(FC):
                            nc.tensor.matmul(yp[k % 2][:, t, :], a[k % 2][0:fw[f], f, t * HT:(t + 1) * HT], dn[0:fw[f], s, f, :],
                                             start=(f == 0), stop=False)
                        ins = nc.tensor.matmul(yp[k % 2][:, t, :], onerow[:], bd[:, s, :], start=False, stop=True)
                    ins.then_inc(s_dn, 1)


def shared_stage(nc, c, xnT, sw1, sb1, sw2, sb2, h, h_out, F=512):
    FC = F // 128
    with Stage(nc, "shared") as st:
        up = st.sb("up", [D, F])
        dn = st.sb("dn", [128, FC, D])
        bu = st.sb("bu", [128, FC])
        bd = st.sb("bd", [1, D])
        onerow = st.sb("onerow", [1, HT])
        xT = st.sb("xT", [D, CT * HT])
        ht = st.sb("ht", [HT, CT, D])
        a = [st.sb(f"a{i}", [128, FC, 4 * HT]) for i in range(2)]
        hp = [st.ps(f"hp{i}", [128, 4 * HT]) for i in range(2)]
        yp = [st.ps(f"yp{i}", [HT, 4, D]) for i in range(2)]
        s_in = st.sem("loaded")
        s_x = st.sem("x_loaded")
        s_up = st.sem("up_done")
        s_a = st.sem("act_done")
        s_dn = st.sem("down_done")
        s_y = st.sem("y_ready")
        s_out = st.sem("stored")
        with st.step() as block:
            @block.sync
            def _(sp):
                sp.dma_start(up[:], sw1[:, :]).then_inc(s_in, 16)
                sp.dma_start(dn[:], sw2.rearrange("(c p) d -> p c d", p=128)).then_inc(s_in, 16)
                sp.dma_start(bu[:], sb1.rearrange("(c p) -> p c", p=128), allow_slow_non_contiguous=True).then_inc(s_in, 16)
                sp.dma_start(bd[:], sb2.rearrange("(a d) -> a d", a=1)).then_inc(s_in, 16)
                sp.wait_ge(s_in, 64)

            @block.vector
            def _(dve):
                nc.vector.memset(onerow[:], 1.0).then_inc(s_y, 1)
                dve.wait_ge(s_y, 1)
        hv, ov = tiles_of(h), tiles_of(h_out)
        with nc.Fori(0, NT // CT) as i, st.step() as block:
            @block.sync
            def _(sp):
                sp.dma_start(xT[:], xnT[:, bass.ds(i * (CT * HT), CT * HT)]).then_inc(s_x, 16)
                for k in range(NBI):
                    sp.dma_start(ht[:, 2 * k:2 * k + 2, :], hv[i * NBI + k]).then_inc(s_in, 16)
                for g in range(2):
                    sp.wait_ge(s_y, g + 1)
                    for k in range(2):
                        sp.dma_start(ov[i * NBI + 2 * g + k], ht[:, 4 * g + 2 * k:4 * g + 2 * k + 2, :]).then_inc(s_out, 16)
                sp.wait_ge(s_out, 64)

            @block.tensor
            def _(pe):
                pe.wait_ge(s_x, 16)
                for k in range(2):
                    for f in range(FC):
                        if k * FC + f >= 2:
                            pe.wait_ge(s_a, k * FC + f - 1)
                        nc.tensor.matmul(hp[f % 2][:], up[:, f * 128:(f + 1) * 128], xT[:, k * 4 * HT:(k + 1) * 4 * HT],
                                         start=True, stop=True).then_inc(s_up, 1)
                    pe.wait_ge(s_a, (k + 1) * FC)
                    for t in range(4):
                        for f in range(FC):
                            nc.tensor.matmul(yp[k][:, t, :], a[k][:, f, t * HT:(t + 1) * HT], dn[:, f, :], start=(f == 0), stop=False)
                        ins = nc.tensor.matmul(yp[k][:, t, :], onerow[:], bd[:], start=False, stop=True)
                    ins.then_inc(s_dn, 1)

            @block.scalar
            def _(act):
                for k in range(2):
                    for f in range(FC):
                        act.wait_ge(s_up, k * FC + f + 1)
                        nc.scalar.activation(a[k][:, f, :], hp[f % 2][:], ACT.Gelu_apprx_tanh, bias=bu[:, f:f + 1]).then_inc(s_a, 1)

            @block.vector
            def _(dve):
                dve.wait_ge(s_in, 64)
                for k in range(2):
                    dve.wait_ge(s_dn, k + 1)
                    t = ht[:, 4 * k:4 * k + 4, :]
                    nc.vector.tensor_tensor(t, t, yp[k][:], ALU.add).then_inc(s_y, 1)


NH = 8
HD = D // NH
DT = 0.1
US = 6


def turn_weights_stage(nc, c, name, weights, dst):
    n = len(weights)
    with Stage(nc, name) as st:
        w = st.sb("w", [D, n, D])
        wt = st.sb("wt", [D, n, D])
        tp = [st.ps(f"tp{i}", [D, 4, D]) for i in range(2)]
        s_in = st.sem("loaded")
        s_tp = st.sem("transposed")
        s_cp = st.sem("copied")
        s_out = st.sem("stored")
        with st.step() as block:
            @block.sync
            def _(sp):
                for k, x in enumerate(weights):
                    sp.dma_start(w[:, k, :], x[:, :]).then_inc(s_in, 16)
                sp.wait_ge(s_cp, n)
                sp.dma_start(dst.rearrange("n p d -> p n d"), wt[:]).then_inc(s_out, 16)
                sp.wait_ge(s_out, 16)

            @block.tensor
            def _(pe):
                pe.wait_ge(s_in, 16 * n)
                for k in range(n):
                    if k >= 2:
                        pe.wait_ge(s_cp, k - 1)
                    nc.tensor.transpose(tp[k % 2][:, 0, :], w[:, k, :], c.ident[:]).then_inc(s_tp, 1)

            @block.vector
            def _(dve):
                for k in range(n):
                    dve.wait_ge(s_tp, k + 1)
                    nc.vector.tensor_copy(wt[:, k, :], tp[k % 2][:, 0, :]).then_inc(s_cp, 1)


def liquid_stage(nc, c, xnT, wt, li_tau, li_b, liqT):
    with Stage(nc, "liquid") as st:
        S = st.sb("S", [D, B, T])
        x = [st.sb(f"x{i}", [D, 2 * T]) for i in range(2)]
        ab = st.sb("ab", [D, B, T])
        w = st.sb("w", [D, 3, D])
        cols = st.sb("cols", [D, 2])
        tau = st.sb("tau", [D, T])
        t1 = st.sb("t1", [D, T])
        a = [st.sb(f"a{i}", [D, B]) for i in range(2)]
        p = [st.sb(f"p{i}", [D, B]) for i in range(2)]
        hc = st.sb("hc", [D, B])
        pp = [st.ps(f"pp{i}", [D, 512]) for i in range(2)]
        s_in = st.sem("loaded")
        s_own = st.sem("own")
        s_mm = st.sem("multiplied")
        s_cp = st.sem("copied")
        s_act = st.sem("act")
        s_p = st.sem("decayed_state")
        s_h = st.sem("state")
        s_out = st.sem("stored")
        V = nc.vector
        with st.step() as block:
            @block.sync
            def _(sp):
                sp.dma_start(w[:, 0:2, :], wt[0:2].rearrange("n p d -> p n d")).then_inc(s_in, 16)
                sp.dma_start(cols[:, 0:1], li_tau.rearrange("(p a) -> p a", a=1)).then_inc(s_in, 16)
                sp.dma_start(cols[:, 1:2], li_b.rearrange("(p a) -> p a", a=1)).then_inc(s_in, 16)
                sp.wait_ge(s_in, 48)

            @block.vector
            def _(dve):
                own = Chain(dve, s_own)
                dve.wait_ge(s_in, 48)
                own(V.tensor_scalar(w[:, 2, :], w[:, 1, :], DT, None, ALU.mult))
                for z in (a[1], p[1], hc):
                    own(V.memset(z[:], 0.0))

        with nc.Fori(0, B // 4) as i, st.step() as block:
            @block.sync
            def _(sp):
                for k in range(2):
                    sp.dma_start(x[k][:], xnT[:, bass.ds(i * (4 * T) + k * 2 * T, 2 * T)]).then_inc(s_in, 16)

            @block.tensor
            def _(pe):
                pe.wait_ge(s_in, 32)
                for k in range(2):
                    nc.tensor.matmul(pp[k][:, 0:2 * T], w[:, 0, :], x[k][:], start=True, stop=True).then_inc(s_mm, 1)

            @block.vector
            def _(dve):
                for k in range(2):
                    dve.wait_ge(s_mm, k + 1)
                    V.tensor_copy(S[:, bass.ds(i * 4 + 2 * k, 2), :], pp[k][:, 0:2 * T].rearrange("p (b t) -> p b t", b=2)).then_inc(s_cp, 1)
                dve.wait_ge(s_cp, 2)

        with st.step() as block:
            @block.scalar
            def _(act):
                nc.scalar.activation(ab[:], S[:], ACT.Abs).then_inc(s_act, 1)
                act.wait_ge(s_p, 1)
                nc.scalar.activation(t1[:], t1[:], ACT.Exp).then_inc(s_act, 1)
                act.wait_ge(s_act, 2)
                nc.scalar.activation(t1[:], t1[:], ACT.Ln, bias=1.0).then_inc(s_act, 1)

            @block.vector
            def _(dve):
                own = Chain(dve, s_own)
                dve.wait_ge(s_act, 1)
                own(V.tensor_reduce(tau[:], ab[:].rearrange("p b t -> p t b"), AX.X, ALU.add))
                own(V.tensor_scalar(tau[:], tau[:], 0.1 / B, cols[:, 0:1], ALU.mult, ALU.add))
                own(V.tensor_scalar(t1[:], tau[:], -1.0, None, ALU.mult))
                V.tensor_tensor(t1[:], tau[:], t1[:], ALU.min).then_inc(s_p, 1)
                dve.wait_ge(s_act, 3)
                own(V.scalar_tensor_tensor(tau[:], tau[:], 0.0, t1[:], ALU.max, ALU.add))
                own(V.reciprocal(tau[:], tau[:]))
                own(V.tensor_scalar(tau[:], tau[:], -DT, 1.0, ALU.mult, ALU.add))

        col = lambda t: S[:, :, t].rearrange("p b a -> p (b a)")
        with nc.Fori(0, T // US) as i, st.step() as block:
            @block.tensor
            def _(pe):
                for k in range(US):
                    nc.tensor.matmul(pp[k % 2][:, 0:B], c.ident[:], col(bass.ds(i * US + k, 1)), start=True, stop=False)
                    if k >= 1:
                        pe.wait_ge(s_p, k)
                    nc.tensor.matmul(pp[k % 2][:, 0:B], w[:, 1, :], p[(k + 1) % 2][:], start=False, stop=False)
                    if k >= 1:
                        pe.wait_ge(s_act, k)
                    nc.tensor.matmul(pp[k % 2][:, 0:B], w[:, 2, :], a[(k + 1) % 2][:], start=False, stop=True).then_inc(s_mm, 1)

            @block.scalar
            def _(act):
                for k in range(US):
                    act.wait_ge(s_mm, k + 1)
                    if k >= 2:
                        act.wait_ge(s_h, k - 1)
                    nc.scalar.activation(a[k % 2][:], pp[k % 2][:, 0:B], ACT.Tanh, bias=cols[:, 1:2]).then_inc(s_act, 1)

            @block.vector
            def _(dve):
                for k in range(US):
                    t = bass.ds(i * US + k, 1)
                    if k >= 1:
                        dve.wait_ge(s_cp, k)
                        dve.wait_ge(s_mm, k)
                    V.tensor_scalar(p[k % 2][:], hc[:], tau[:, t], None, ALU.mult).then_inc(s_p, 1)
                    dve.wait_ge(s_p, k + 1)
                    dve.wait_ge(s_act, k + 1)
                    V.scalar_tensor_tensor(hc[:], a[k % 2][:], DT, p[k % 2][:], ALU.mult, ALU.add).then_inc(s_cp, 1)
                    dve.wait_ge(s_cp, k + 1)
                    V.tensor_copy(col(t), hc[:]).then_inc(s_h, 1)
                dve.wait_ge(s_h, US)

        with st.step() as block:
            @block.sync
            def _(sp):
                lv = liqT.rearrange("p (b t) -> p b t", b=B)
                for k in range(8):
                    sp.dma_start(lv[:, 8 * k:8 * k + 8, :], S[:, 8 * k:8 * k + 8, :]).then_inc(s_out, 16)
                sp.wait_ge(s_out, 16 * 8)


def mix_weights_stage(nc, c, xnT, W1, b1, W2, b2, fusion, wgt):
    R = D // 4
    with Stage(nc, "mixw") as st:
        x = st.sb("x", [D, B, T])
        m = st.sb("m", [D, B])
        w1 = st.sb("w1", [R, D])
        w2 = st.sb("w2", [3, R])
        w1T = st.sb("w1T", [D, R])
        w2T = st.sb("w2T", [R, 3])
        b1c = st.sb("b1c", [R, 1])
        r1 = st.sb("r1", [R, B])
        rows = st.sb("rows", [B, 2, 3])
        z = st.sb("z", [B, 2, 3])
        red = st.sb("red", [B, 2])
        p = [st.ps(f"p{i}", [128, 512]) for i in range(4)]
        s_in = st.sem("loaded")
        s_own = st.sem("own")
        s_mm = st.sem("multiplied")
        s_x = st.sem("ready")
        s_act = st.sem("act")
        s_out = st.sem("stored")
        V = nc.vector
        with st.step() as block:
            @block.sync
            def _(sp):
                sp.dma_start(w1[:], W1[:, :]).then_inc(s_in, 16)
                sp.dma_start(w2[:], W2[:, :]).then_inc(s_in, 16)
                sp.dma_start(b1c[:], b1.rearrange("(p a) -> p a", a=1)).then_inc(s_in, 16)
                sp.dma_start(rows[:, 0, :], wide(b2, B)).then_inc(s_in, 16)
                sp.dma_start(rows[:, 1, :], wide(fusion, B)).then_inc(s_in, 16)
                xv = xnT.rearrange("p (b t) -> p b t", b=B)
                for k in range(8):
                    sp.dma_start(x[:, 8 * k:8 * k + 8, :], xv[:, 8 * k:8 * k + 8, :]).then_inc(s_in, 16)
                sp.wait_ge(s_x, 6)
                sp.dma_start(wgt[:, :], z[:, 0, :]).then_inc(s_out, 16)
                sp.wait_ge(s_out, 16)

            @block.tensor
            def _(pe):
                pe.wait_ge(s_in, 16 * 13)
                nc.tensor.transpose(p[0][:, 0:R], w1[:], c.ident[0:R, 0:R]).then_inc(s_mm, 1)
                nc.tensor.transpose(p[1][0:R, 0:3], w2[:], c.ident[0:3, 0:3]).then_inc(s_mm, 1)
                pe.wait_ge(s_x, 3)
                nc.tensor.matmul(p[2][0:R, 0:B], w1T[:], m[:], start=True, stop=True).then_inc(s_mm, 1)
                pe.wait_ge(s_x, 4)
                nc.tensor.matmul(p[3][0:B, 0:3], r1[:], w2T[:], start=True, stop=True).then_inc(s_mm, 1)

            @block.vector
            def _(dve):
                own = Chain(dve, s_own)
                dve.wait_ge(s_in, 16 * 13)
                own(V.tensor_reduce(m[:], x[:], AX.X, ALU.add))
                V.tensor_scalar(m[:], m[:], 1.0 / T, None, ALU.mult).then_inc(s_x, 1)
                dve.wait_ge(s_mm, 2)
                V.tensor_copy(w1T[:], p[0][:, 0:R]).then_inc(s_x, 1)
                V.tensor_copy(w2T[:], p[1][0:R, 0:3]).then_inc(s_x, 1)
                dve.wait_ge(s_mm, 3)
                V.tensor_scalar(r1[:], p[2][0:R, 0:B], b1c[:, 0:1], 0.0, ALU.add, ALU.max).then_inc(s_x, 1)
                dve.wait_ge(s_mm, 4)
                own(V.tensor_tensor(z[:, 0, :], p[3][0:B, 0:3], rows[:, 0, :], ALU.add))
                own(V.tensor_copy(z[:, 1, :], rows[:, 1, :]))
                own(V.tensor_reduce(red[:], z[:], AX.X, ALU.max))
                V.tensor_tensor(z[:], z[:], red[:].unsqueeze(2).to_broadcast([B, 2, 3]), ALU.subtract).then_inc(s_x, 1)
                dve.wait_ge(s_act, 1)
                own(V.tensor_reduce(red[:], z[:], AX.X, ALU.add))
                own(V.reciprocal(red[:], red[:]))
                own(V.tensor_tensor(z[:], z[:], red[:].unsqueeze(2).to_broadcast([B, 2, 3]), ALU.mult))
                V.tensor_tensor(z[:, 0, :], z[:, 0, :], z[:, 1, :], ALU.mult).then_inc(s_x, 1)

            @block.scalar
            def _(act):
                act.wait_ge(s_x, 5)
                nc.scalar.activation(z[:], z[:], ACT.Exp).then_inc(s_act, 1)


def head_masks(pool, nc, own, headmask, blockmask=None):
    P = nc.gpsimd
    for m, wd in ((headmask, 1),) + (((blockmask, HD),) if blockmask is not None else ()):
        v = m[:].rearrange("p (h d) -> p h d", h=NH)
        own(P.memset(m[:], 1.0))
        own(P.affine_select(out=v, in_=v, compare_op=ALU.is_ge, fill=0.0, base=0, pattern=[[-HD, NH], [0, wd]], channel_multiplier=1))
        own(P.affine_select(out=v, in_=v, compare_op=ALU.is_ge, fill=0.0, base=HD - 1, pattern=[[HD, NH], [0, wd]], channel_multiplier=-1))


def retention_stage(nc, c, xnT, liqT, wt, vecs, theta, wgt, h, h_out):
    with Stage(nc, "ret") as st:
        w = st.sb("w", [D, 9, D])
        WOUT, RQ, RK, RV, RO, LQ, LK, LV, LO = range(9)
        gnw, gnb, rbo, lbq, lbk, lbv, lbo, lnw, lnb = vecs
        wv = st.sb("wv", [HT, 4, D])
        br = st.sb("br", [1, 4, D])
        bq = st.sb("bq", [D, 1])
        th = st.sb("th", [HT, NH])
        ones = st.sb("ones", [HT, HT])
        diff = st.sb("diff", [HT, 2, T])
        dm = st.sb("dm", [HT, 2, T])
        ng = st.sb("ng", [HT, 2, T])
        hm = st.sb("hm", [D, NH])
        bm = st.sb("bm", [D, D])
        eps = st.sb("eps", [HT, 1])
        x = st.sb("x", [D, T])
        lq = st.sb("lq", [D, T])
        hb = st.sb("hb", [HT, 2, D])
        mw = st.sb("mw", [HT, 3])
        QM = st.sb("QM", [D, NH, T])
        KT = st.sb("KT", [D, T])
        Vt = st.sb("Vt", [HT, 2, D])
        q2 = st.sb("q2", [D, T])
        e2 = st.sb("e2", [D, T])
        k2 = st.sb("k2", [HT, 2, D])
        f2 = st.sb("f2", [HT, 2, D])
        v2 = st.sb("v2", [HT, 2, D])
        kv = st.sb("kv", [D, D])
        ks = st.sb("ks", [D, NH])
        lin = st.sb("lin", [HT, 2, D])
        den = st.sb("den", [HT, 2, NH])
        sc = [st.sb(f"sc{i}", [HT, NH, HT * (i + 1)]) for i in range(2)]
        mx = st.sb("mx", [HT, 2, NH])
        rs = st.sb("rs", [HT, 2, NH])
        ri = st.sb("ri", [HT, 2, NH])
        PT = st.sb("PT", [HT, NH, 2, HT])
        ret = st.sb("ret", [HT, 2, D])
        sq = st.sb("sq", [HT, 2, D])
        gm = st.sb("gm", [HT, 2, NH])
        oT = st.sb("oT", [D, 4, HT])
        fu = st.sb("fu", [HT, 2, D])
        stt = st.sb("stt", [HT, 2, 6])
        mv = st.sb("mv", [HT, 2, 2])
        sd = st.sb("sd", [HT, 2])
        scp = st.ps("scp", [HT, 4, 512])
        gp = [st.ps(f"gp{i}", [128, 512]) for i in range(2)]
        tp = [st.ps(f"tp{i}", [HT, 4, 128]) for i in range(2)]
        s_w = st.sem("weights")
        s_own = st.sem("own")
        s_po = st.sem("pool_own")
        s_in = st.sem("loaded")
        s_hb = st.sem("h_loaded")
        s_g = st.sem("product_done")
        s_e = st.sem("product_read")
        s_sc = st.sem("scores_done")
        s_mx = st.sem("max_ready")
        s_ex = st.sem("exp_done")
        s_el = st.sem("elu_args")
        s_el2 = st.sem("elu_exp")
        s_q2 = st.sem("elu_done")
        s_tp = st.sem("p_transposed")
        s_pt = st.sem("p_copied")
        s_rt = st.sem("branches_ready")
        s_vr = st.sem("variances")
        s_sd = st.sem("roots")
        s_out = st.sem("stored")
        V = nc.vector
        tmp_ = lambda k: QM[0:HT, 2 * (k % 2):2 * (k % 2) + 2, :]

        with st.step() as block:
            @block.sync
            def _(sp):
                sp.dma_start(w[:], wt[2:11].rearrange("n p d -> p n d")).then_inc(s_w, 16)
                for k, v in enumerate((gnw, gnb, lnw, lnb)):
                    sp.dma_start(wv[:, k, :], wide(v, HT)).then_inc(s_w, 16)
                for k, v in enumerate((rbo, lbk, lbv, lbo)):
                    sp.dma_start(br[:, k, :], v.rearrange("(a d) -> a d", a=1)).then_inc(s_w, 16)
                sp.dma_start(bq[:], lbq.rearrange("(p a) -> p a", a=1)).then_inc(s_w, 16)
                sp.dma_start(th[:], wide(theta, HT)).then_inc(s_w, 16)
                sp.wait_ge(s_w, 16 * 11)

            @block.gpsimd
            def _(pool):
                own = Chain(pool, s_po)
                P = nc.gpsimd
                own(P.iota(diff[:], pattern=[[HT, 2], [-1, T]], base=0, channel_multiplier=1, allow_small_or_imprecise_dtypes=True))
                P.memset(ones[:], 1.0).then_inc(s_in, 1)
                head_masks(pool, nc, own, hm, bm)
                own(P.memset(ng[:], 0.0))
                own(P.affine_select(out=ng[:], in_=ng[:], compare_op=ALU.is_ge, fill=-1e30, base=0,
                                    pattern=[[HT, 2], [-1, T]], channel_multiplier=1))
                pool.wait_ge(s_ex, 1)
                own(P.affine_select(out=dm[:], in_=dm[:], compare_op=ALU.is_ge, fill=0.0, base=0,
                                    pattern=[[HT, 2], [-1, T]], channel_multiplier=1))
                pool.wait_ge(s_in, 1)

            @block.vector
            def _(dve):
                own = Chain(dve, s_own)
                own(V.memset(eps[:], EPS))
                dve.wait_ge(s_w, 16 * 11)
                own(V.tensor_scalar(th[:], th[:], -1.0, None, ALU.mult))
                dve.wait_ge(s_po, 1)
                V.tensor_scalar(diff[:], diff[:], 0.0, None, ALU.max).then_inc(s_mx, 1)
                for k in range(NH):
                    dve.wait_ge(s_e, k + 1)
                    if k == 0:
                        ins = V.tensor_copy(dm[:], tmp_(0))
                    else:
                        ins = V.tensor_tensor(dm[:], dm[:], tmp_(k), ALU.add)
                    own(ins)
                    V.engine_nop().then_inc(s_g, 1)
                V.tensor_scalar(dm[:], dm[:], 1.0 / NH / HD ** 0.5, None, ALU.mult).then_inc(s_ex, 1)

            @block.scalar
            def _(act):
                act.wait_ge(s_mx, 1)
                for k in range(NH):
                    if k >= 2:
                        act.wait_ge(s_g, k - 1)
                    nc.scalar.activation(tmp_(k), diff[:], ACT.Exp, scale=th[:, k:k + 1]).then_inc(s_e, 1)

        hv, ov = tiles_of(h), tiles_of(h_out)
        with nc.Fori(0, B) as b, st.step() as block:
            @block.sync
            def _(sp):
                sp.dma_start(x[:], xnT[:, bass.ds(b * T, T)]).then_inc(s_in, 16)
                sp.dma_start(lq[:], liqT[:, bass.ds(b * T, T)]).then_inc(s_hb, 16)
                sp.dma_start(hb[:], hv[b]).then_inc(s_hb, 16)
                sp.dma_start(mw[:], bass.AP(wgt.tensor, 0, [[3, B], [0, HT], [1, 3]])[b]).then_inc(s_hb, 16)
                sp.wait_ge(s_rt, 2)
                sp.dma_start(ov[b], hb[:]).then_inc(s_out, 16)
                sp.wait_ge(s_out, 16)

            @block.tensor
            def _(pe):
                n = [0]

                def job(fn):
                    k = n[0]
                    if k >= 2:
                        pe.wait_ge(s_e, k - 1)
                    fn(gp[k % 2]).then_inc(s_g, 1)
                    n[0] += 1

                def mm(o, l, r, first=True, last=True):
                    return nc.tensor.matmul(o, l, r, start=first, stop=last)

                def tokens(wi, bias):
                    def fn(p):
                        for k in range(2):
                            o = p[0:HT, k * D:(k + 1) * D]
                            ins = mm(o, x[:, k * HT:(k + 1) * HT], w[:, wi, :], True, bias is None)
                            if bias is not None:
                                ins = mm(o, ones[0:1, :], br[:, bias, :], False, True)
                        return ins
                    return fn

                def scores(f):
                    if f:
                        pe.wait_ge(s_mx, 1)
                    for hd in range(NH):
                        ins = mm(scp[:, hd // 2, (hd % 2) * T:(hd % 2) * T + HT * (f + 1)],
                                 QM[:, hd, f * HT:(f + 1) * HT], KT[:, 0:HT * (f + 1)])
                    ins.then_inc(s_sc, 1)

                def turn(f):
                    n0 = 0 if f == 0 else 2
                    for m in range(NH * (f + 1) // 4):
                        if n0 + m >= 2:
                            pe.wait_ge(s_pt, n0 + m - 1)
                        for r in range(4):
                            hd, sh = divmod(4 * m + r, f + 1)
                            pe.wait_ge(s_ex, f * NH + hd + 1)
                            nc.tensor.transpose(tp[m % 2][:, r, 0:HT], sc[f][:, hd, sh * HT:(sh + 1) * HT],
                                                c.ident[0:HT, 0:HT]).then_inc(s_tp, 1)

                def pv(f):
                    def fn(p):
                        pe.wait_ge(s_pt, 2 if f == 0 else 6)
                        for hd in range(NH):
                            for sh in range(f + 1):
                                ins = mm(p[0:HT, hd * HD:(hd + 1) * HD], PT[:, hd, sh, :], Vt[:, sh, hd * HD:(hd + 1) * HD],
                                         sh == 0, sh == f)
                        return ins
                    return fn

                pe.wait_ge(s_in, 16)
                job(lambda p: mm(p[:, 0:T], w[:, RQ, :], x[:]))
                job(lambda p: mm(p[:, 0:T], w[:, RK, :], x[:]))
                job(tokens(RV, None))
                pe.wait_ge(s_e, 2)
                scores(0)
                job(lambda p: mm(p[:, 0:T], w[:, LQ, :], x[:]))
                job(tokens(LK, 1))
                job(tokens(LV, 2))
                scores(1)
                turn(0)
                pe.wait_ge(s_e, 3)
                job(pv(0))
                pe.wait_ge(s_q2, 2)
                pe.wait_ge(s_e, 6)

                def kvs(p):
                    for k in range(2):
                        mm(p[:, 0:D], k2[:, k, :], v2[:, k, :], k == 0, k == 1)
                    for k in range(2):
                        ins = mm(p[:, D:D + 1], k2[:, k, :], ones[:, 0:1], k == 0, k == 1)
                    return ins
                job(kvs)
                pe.wait_ge(s_e, 8)

                def numden(p):
                    for k in range(2):
                        mm(p[0:HT, k * D:(k + 1) * D], q2[:, k * HT:(k + 1) * HT], kv[:])
                        ins = mm(p[0:HT, 256 + k * NH:256 + (k + 1) * NH], q2[:, k * HT:(k + 1) * HT], ks[:])
                    return ins
                job(numden)
                turn(1)
                job(pv(1))
                pe.wait_ge(s_rt, 1)

                def turn_out(p):
                    for k in range(2):
                        nc.tensor.transpose(p[:, k * 128:k * 128 + HT], ret[:, k, :], c.ident[0:HT, 0:HT])
                    for k in range(2):
                        ins = nc.tensor.transpose(p[:, (2 + k) * 128:(2 + k) * 128 + HT], lin[:, k, :], c.ident[0:HT, 0:HT])
                    return ins
                job(turn_out)
                pe.wait_ge(s_e, 11)
                pe.wait_ge(s_hb, 48)

                def outs(p):
                    for k in range(2):
                        mm(p[0:HT, k * D:(k + 1) * D], lq[:, k * HT:(k + 1) * HT], w[:, WOUT, :])
                    for k in range(2):
                        o = p[0:HT, (2 + k) * D:(3 + k) * D]
                        mm(o, oT[:, k, :], w[:, RO, :], True, False)
                        ins = mm(o, ones[0:1, :], br[:, 0, :], False, True)
                    return ins
                job(outs)

                def outl(p):
                    for k in range(2):
                        o = p[0:HT, k * D:(k + 1) * D]
                        mm(o, oT[:, 2 + k, :], w[:, LO, :], True, False)
                        ins = mm(o, ones[0:1, :], br[:, 3, :], False, True)
                    return ins
                job(outl)

            @block.vector
            def _(dve):
                own = Chain(dve, s_own)

                def read(k, ins):
                    ins.then_inc(s_e, 1)
                    dve.wait_ge(s_e, k)

                def soft(f):
                    dve.wait_ge(s_sc, f + 1)
                    wd = HT * (f + 1)
                    sv = sc[f][:].rearrange("p (a c) s -> p a c s", c=2)
                    pv = scp[:, :, 0:2 * T].rearrange("p a (c s) -> p a c s", c=2)[:, :, :, 0:wd]
                    own(V.tensor_tensor(sv, pv, dm[:, f, None, None, 0:wd].to_broadcast([HT, 4, 2, wd]), ALU.mult))
                    own(V.tensor_tensor(sc[f][:], sc[f][:], ng[:, f, None, 0:wd].to_broadcast([HT, NH, wd]), ALU.add))
                    own(V.tensor_reduce(mx[:, f, :], sc[f][:], AX.X, ALU.max))
                    V.tensor_scalar(mx[:, f, :], mx[:, f, :], -1.0, None, ALU.mult).then_inc(s_mx, 1)

                def heads(f, k, src):
                    p = gp[(k - 1) % 2]
                    dve.wait_ge(s_g, k)
                    own(V.reciprocal(ri[:, f, :], rs[:, f, :]))
                    read(k, V.tensor_tensor(ret[:, f, :].rearrange("p (h d) -> p h d", h=NH), p[0:HT, 0:D].rearrange("p (h d) -> p h d", h=NH),
                                            ri[:, f, :].unsqueeze(2).to_broadcast([HT, NH, HD]), ALU.mult))

                dve.wait_ge(s_g, 1)
                read(1, V.tensor_tensor(QM[:], gp[0][:, None, 0:T].to_broadcast([D, NH, T]),
                                        hm[:].unsqueeze(2).to_broadcast([D, NH, T]), ALU.mult))
                dve.wait_ge(s_g, 2)
                read(2, V.tensor_copy(KT[:], gp[1][:, 0:T]))
                dve.wait_ge(s_g, 3)
                read(3, V.tensor_copy(Vt[:].rearrange("p a d -> p (a d)"), gp[0][0:HT, 0:2 * D]))
                soft(0)
                dve.wait_ge(s_g, 4)
                read(4, V.tensor_scalar(q2[:], gp[1][:, 0:T], bq[:, 0:1], None, ALU.add))
                V.tensor_scalar(e2[:], q2[:], 0.0, None, ALU.min).then_inc(s_el, 1)
                dve.wait_ge(s_g, 5)
                read(5, V.tensor_copy(k2[:].rearrange("p a d -> p (a d)"), gp[0][0:HT, 0:2 * D]))
                V.tensor_scalar(f2[:], k2[:], 0.0, None, ALU.min).then_inc(s_el, 1)
                dve.wait_ge(s_g, 6)
                read(6, V.tensor_copy(v2[:].rearrange("p a d -> p (a d)"), gp[1][0:HT, 0:2 * D]))
                dve.wait_ge(s_el2, 2)
                V.scalar_tensor_tensor(q2[:], q2[:], 0.0, e2[:], ALU.max, ALU.add).then_inc(s_q2, 1)
                V.scalar_tensor_tensor(k2[:], k2[:], 0.0, f2[:], ALU.max, ALU.add).then_inc(s_q2, 1)
                soft(1)
                heads(0, 7, 0)
                dve.wait_ge(s_g, 8)
                own(V.tensor_scalar(ks[:], hm[:], gp[1][:, D:D + 1], None, ALU.mult))
                read(8, V.tensor_tensor(kv[:], bm[:], gp[1][:, 0:D], ALU.mult))
                dve.wait_ge(s_g, 9)
                own(V.tensor_scalar(den[:].rearrange("p a h -> p (a h)"), gp[0][0:HT, 256:256 + 2 * NH], 1e-8, None, ALU.add))
                own(V.reciprocal(den[:], den[:]))
                read(9, V.tensor_tensor(lin[:].rearrange("p a (h d) -> p (a h) d", h=NH),
                                        gp[0][0:HT, 0:2 * D].rearrange("p (a d) -> p a d", d=HD),
                                        den[:].rearrange("p a h -> p (a h)").unsqueeze(2).to_broadcast([HT, 2 * NH, HD]), ALU.mult))
                heads(1, 10, 1)
                rh = ret[:].rearrange("p a (h d) -> p (a h) d", h=NH)
                sh = sq[:].rearrange("p a (h d) -> p (a h) d", h=NH)
                gh = gm[:].rearrange("p a h -> p (a h)")
                gb = gh.unsqueeze(2).to_broadcast([HT, 2 * NH, HD])
                own(V.tensor_reduce(gh, rh, AX.X, ALU.add))
                own(V.tensor_scalar(gh, gh, 1.0 / HD, None, ALU.mult))
                own(V.tensor_tensor(rh, rh, gb, ALU.subtract))
                own(V.tensor_tensor(sh, rh, rh, ALU.mult))
                V.tensor_reduce(gh, sh, AX.X, ALU.add).then_inc(s_vr, 1)
                dve.wait_ge(s_sd, 1)
                own(V.reciprocal(gh, gh))
                own(V.tensor_tensor(rh, rh, gb, ALU.mult))
                vb = lambda k: wv[:, k, None, :].to_broadcast([HT, 2, D])
                own(V.tensor_tensor(ret[:], ret[:], vb(0), ALU.mult))
                V.tensor_tensor(ret[:], ret[:], vb(1), ALU.add).then_inc(s_rt, 1)
                dve.wait_ge(s_g, 11)
                read(11, V.tensor_copy(oT[:], gp[0][:, 0:512].rearrange("p (a t) -> p a t", a=4)[:, :, 0:HT]))
                dve.wait_ge(s_hb, 48)
                dve.wait_ge(s_g, 12)
                f = lambda t: t[:].rearrange("p a d -> p (a d)")
                own(V.tensor_scalar(f(fu), gp[1][0:HT, 0:256], mw[:, 0:1], None, ALU.mult))
                read(12, V.scalar_tensor_tensor(f(fu), gp[1][0:HT, 256:512], mw[:, 1:2], f(fu), ALU.mult, ALU.add))
                dve.wait_ge(s_g, 13)
                read(13, V.scalar_tensor_tensor(f(fu), gp[0][0:HT, 0:256], mw[:, 2:3], f(fu), ALU.mult, ALU.add))
                for k in range(2):
                    own(V.bn_stats(stt[:, k, :], fu[:, k, :]))
                    own(V.bn_aggr(mv[:, k, :], stt[:, k, :]))
                V.engine_nop().then_inc(s_vr, 1)
                dve.wait_ge(s_sd, 2)
                own(V.reciprocal(sd[:], sd[:]))
                for k in range(2):
                    own(V.tensor_scalar(fu[:, k, :], fu[:, k, :], mv[:, k, 0:1], sd[:, k:k + 1], ALU.subtract, ALU.mult))
                own(V.tensor_tensor(fu[:], fu[:], vb(2), ALU.mult))
                own(V.tensor_tensor(fu[:], fu[:], vb(3), ALU.add))
                V.tensor_tensor(hb[:], hb[:], fu[:], ALU.add).then_inc(s_rt, 1)

            @block.scalar
            def _(act):
                def exps(f):
                    act.wait_ge(s_mx, f + 1)
                    for hd in range(NH):
                        nc.scalar.activation(sc[f][:, hd, :], sc[f][:, hd, :], ACT.Exp, bias=mx[:, f, hd:hd + 1],
                                             accum_out=rs[:, f, hd:hd + 1]).then_inc(s_ex, 1)

                def copies(f):
                    n0 = 0 if f == 0 else 2
                    if f:
                        act.wait_ge(s_g, 7)
                    for m in range(NH * (f + 1) // 4):
                        act.wait_ge(s_tp, 4 * (n0 + m + 1))
                        if f == 0:
                            dst = PT[:, 4 * m:4 * m + 4, 0, :]
                        else:
                            dst = PT[:, 2 * m:2 * m + 2, :, :].rearrange("p a s t -> p (a s) t")
                        nc.scalar.activation(dst, tp[m % 2][:, :, 0:HT], ACT.Copy).then_inc(s_pt, 1)

                exps(0)
                act.wait_ge(s_el, 2)
                nc.scalar.activation(e2[:], e2[:], ACT.Exp).then_inc(s_el2, 1)
                nc.scalar.activation(f2[:], f2[:], ACT.Exp).then_inc(s_el2, 1)
                copies(0)
                exps(1)
                copies(1)
                act.wait_ge(s_vr, 1)
                nc.scalar.activation(gm[:], gm[:], ACT.Sqrt, bias=eps[:, 0:1], scale=1.0 / HD).then_inc(s_sd, 1)
                act.wait_ge(s_vr, 2)
                nc.scalar.activation(sd[:], mv[:, :, 1], ACT.Sqrt, bias=eps[:, 0:1]).then_inc(s_sd, 1)


FH = 8
FD = 64
SL = B
PROJ = FH * (5 * FD + 2)
KW = FH * FD


def slow_weights_stage(nc, c, W, dst, Wout, dst_out):
    NR = 5 * KW // 128
    with Stage(nc, "slow") as st:
        w = st.sb("w", [128, NR + 1, D])
        wt = st.sb("wt", [D, NR + 1, 128])
        wo = st.sb("wo", [D, 4, 128])
        wot = st.sb("wot", [128, 4, D])
        tp = [st.ps(f"tp{i}", [D, 4, 128]) for i in range(2)]
        s_in = st.sem("loaded")
        s_tp = st.sem("transposed")
        s_cp = st.sem("copied")
        s_out = st.sem("stored")
        HR = 5 * FD + 2
        src_kind = [0, 1, 3, 2, 4]
        with st.step() as block:
            @block.sync
            def _(sp):
                for n in range(NR):
                    kind, hp = divmod(n, 4)
                    for a in range(2):
                        r = (2 * hp + a) * HR + src_kind[kind] * FD
                        sp.dma_start(w[a * FD:(a + 1) * FD, n, :], W[r:r + FD, :]).then_inc(s_in, 16)
                for hd in range(FH):
                    r = hd * HR + 5 * FD
                    sp.dma_start(w[2 * hd:2 * hd + 2, NR, :], W[r:r + 2, :]).then_inc(s_in, 16)
                sp.dma_start(wo[:], Wout.rearrange("o (c k) -> o c k", c=4)).then_inc(s_in, 16)
                sp.wait_ge(s_cp, NR + 5)
                sp.dma_start(dst[:, 0:5 * KW], wt[:, 0:NR, :].rearrange("p n k -> p (n k)")).then_inc(s_out, 16)
                sp.dma_start(dst[:, 5 * KW:PROJ], wt[:, NR, 0:2 * FH]).then_inc(s_out, 16)
                sp.dma_start(dst_out[:, :, :], wot[:]).then_inc(s_out, 16)
                sp.wait_ge(s_out, 48)

            @block.tensor
            def _(pe):
                pe.wait_ge(s_in, 16 * (2 * NR + FH + 1))
                for n in range(NR + 5):
                    if n >= 2:
                        pe.wait_ge(s_cp, n - 1)
                    if n < NR:
                        ins = nc.tensor.transpose(tp[n % 2][:, 0, :], w[:, n, :], c.ident[:])
                    elif n == NR:
                        ins = nc.tensor.transpose(tp[n % 2][:, 0, 0:2 * FH], w[0:2 * FH, n, :], c.ident[0:2 * FH, 0:2 * FH])
                    else:
                        ins = nc.tensor.transpose(tp[n % 2][:, 0, :], wo[:, n - NR - 1, :], c.ident[:])
                    ins.then_inc(s_tp, 1)

            @block.vector
            def _(dve):
                for n in range(NR + 5):
                    dve.wait_ge(s_tp, n + 1)
                    if n < NR:
                        ins = nc.vector.tensor_copy(wt[:, n, :], tp[n % 2][:, 0, :])
                    elif n == NR:
                        ins = nc.vector.tensor_copy(wt[:, n, 0:2 * FH], tp[n % 2][:, 0, 0:2 * FH])
                    else:
                        ins = nc.vector.tensor_copy(wot[:, n - NR - 1, :], tp[n % 2][:, 0, :])
                    ins.then_inc(s_cp, 1)


def delta_stage(nc, c, xT, wslow, kr, ur, zz):
    with Stage(nc, "delta") as st:
        X = st.sb("X", [D, SL, T])
        W = st.sb("W", [D, PROJ])
        xc = st.sb("xc", [D, 2, SL])
        QK = st.sb("QK", [128, 5, KW])
        sb_ = st.sb("sb", [128, FH, 2])
        mx = st.sb("mx", [128, 3 * FH])
        sm = st.sb("sm", [128, 3 * FH])
        KT = st.sb("KT", [128, 12, 128])
        maskL = st.sb("maskL", [128, 128])
        maskU = st.sb("maskU", [128, 128])
        maskZ = st.sb("maskZ", [128, 128])
        lvl = [[st.sb(f"{what}{k}{g}{p}", shape) for what, shape in
                (("nuB", [128, 4, 128]), ("nlB", [128, 4, 128]), ("nuC", [128, 4, FD]), ("nlU", [128, 4, 2, FD]))]
               for p in range(2) for k in range(2) for g in range(2)]
        first = lambda k, g: lvl[2 * k + g]
        later = lambda k, l: lvl[4 + 2 * k + l % 2]
        P = [st.sb(f"P{k}", [128, 4, FD]) for k in range(2)]
        az = [st.sb(f"az{g}", [128, 4, 128]) for g in range(2)]
        Uf = st.sb("Uf", [128, 4, 2, FD])
        Z = st.sb("Z", [128, 4, 2, FD])
        gp = [st.ps(f"gp{i}", [128, 512]) for i in range(2)]
        pR = [[st.ps(f"pR{k}{p}", [128, 4, 2, FD]) for p in range(2)] for k in range(2)]
        pS = [st.ps(f"pS{k}", [128, 4, FD]) for k in range(2)]
        s_w = st.sem("weights")
        s_own = st.sem("own")
        s_x = st.sem("x_ready")
        s_g = st.sem("product_done")
        s_e = st.sem("product_copied")
        s_m = st.sem("product_masked")
        s_be = st.sem("beta_ready")
        s_mx = st.sem("max_ready")
        s_sh = st.sem("shifted")
        s_ex = st.sem("exp_done")
        s_sm = st.sem("scale_ready")
        s_k = st.sem("keys_ready")
        s_v = st.sem("values_ready")
        s_R = [st.sem(f"applied{k}") for k in range(2)]
        s_S = [st.sem(f"squared{k}") for k in range(2)]
        s_dv = [st.sem(f"applied_read{k}") for k in range(2)]
        s_ac = [st.sem(f"squared_read{k}") for k in range(2)]
        s_pk = st.sem("packed")
        s_pa = st.sem("transpose_packed")
        s_z = st.sem("z_read")
        s_out = st.sem("stored")
        s_out2 = st.sem("keys_stored")
        V = nc.vector
        SQ = 4
        LV = SQ + 3
        dv = [0, 4, 8, 12, 13, 14, 15, 16]
        ac = [0, 3, 6, 9, 11, 11, 11, 11]
        slots = [(g, l, k) for g in range(2) for l in range(LV) for k in range(2)]
        HALF = [slice(0, 64), slice(64, 128)]
        PROJ_AT = {0: 0, 1: 1, 2: 2, 3: 3, 4: 4, 5: 5}
        TURN_AT = {16: 0, 17: 1, 18: 2}
        GRAM_AT = {19: 0, 20: 1, 21: 2, 22: 3, 23: 4, 24: 5}
        PROJ_READ = {s + 1: j for s, j in PROJ_AT.items()}
        TURN_READ = {s + 1: j for s, j in TURN_AT.items()}
        MASK_AT = {s + 1: j for s, j in GRAM_AT.items() if j < 5}
        MASK_AT[len(slots) - 1] = 5
        MAX_AT, EXP_AT, SUM_AT = 5, 9, 12
        PACK_AT = {s + 2: j for s, j in GRAM_AT.items() if j % 3 < 2}
        VAL_AT = {7: (0, 0), 8: (1, 0), 16: (0, 1), 17: (1, 1)}

        def step_of(new, old, done):
            with st.step() as block:
                solve, prep = old is not None, new is not None

                @block.tensor
                def _(pe):
                    def mm(o, l, r):
                        return nc.tensor.matmul(o, l, r, start=True, stop=True)

                    def free(n):
                        if n >= 11:
                            pe.wait_ge(s_m, [2, 4, 5, 7, 9, 10][n - 11])
                        elif n >= 2:
                            pe.wait_ge(s_e, n - 1)

                    xv = xc[:].rearrange("p a s -> p (a s)")
                    kt = lambda kind, hd: KT[FD * (hd % 2):FD * (hd % 2) + FD, 4 * kind + hd // 2, :]
                    for n, (g, l, k) in enumerate(slots):
                        if solve:
                            nuB, nlB, nuC, nlU = first(k, g) if l == 0 else later(k, min(l, SQ))
                            if g or l:
                                more = 1 <= l < SQ
                                pe.wait_ge(s_dv[k], 16 * g + dv[l] - 2 * more)
                                pe.wait_ge(s_ac[k], 11 * g + ac[l] - more)
                            if g and l == 0 and k == 0:
                                pe.wait_ge(s_z, 1)
                            for a in range(4):
                                if l < SQ - 1:
                                    ins = mm(pR[k][l % 2][:, a], nuB[:, a, :], nlU[:, a])
                                elif l <= SQ:
                                    ins = mm(pR[k][l % 2][:, a, 1, :], nuB[:, a, :], nlU[:, a, 1, :])
                                else:
                                    ins = mm(pR[k][l % 2][:, a, 1, :], nuB[:, a, :], P[k][:, a, :])
                            ins.then_inc(s_R[k], 1)
                            if l < SQ:
                                if l:
                                    pe.wait_ge(s_dv[k], 16 * g + dv[l])
                                    pe.wait_ge(s_ac[k], 11 * g + ac[l])
                                for a in range(4):
                                    ins = mm(pS[k][:, a, :], nlB[:, a, :], nuC[:, a, :])
                                ins.then_inc(s_S[k], 1)
                            if l == LV - 1 and k == 1:
                                pe.wait_ge(s_dv[0], 16 * (g + 1))
                                for a in range(4):
                                    ins = mm(pR[0][LV % 2][:, a, 1, :], az[g][:, a, :], P[0][:, a, :])
                                ins.then_inc(s_R[0], 1)
                        if not prep:
                            continue
                        if n in PROJ_AT:
                            j = PROJ_AT[n]
                            free(j)
                            if j == 0:
                                pe.wait_ge(s_x, 1)
                                mm(gp[0][:, 0:2 * FH], xv, W[:, 5 * KW:PROJ]).then_inc(s_g, 1)
                            else:
                                mm(gp[j % 2][:], xv, W[:, (j - 1) * KW:j * KW]).then_inc(s_g, 1)
                        if n in TURN_AT:
                            j = TURN_AT[n]
                            free(6 + j)
                            if j == 0:
                                pe.wait_ge(s_k, 1)
                            for m in range(4):
                                ins = nc.tensor.transpose(gp[j % 2][:, m * 128:(m + 1) * 128],
                                                          QK[:, j, m * 128:(m + 1) * 128], c.ident[:])
                            ins.then_inc(s_g, 1)
                        if n in GRAM_AT:
                            j = GRAM_AT[n]
                            free(9 + j)
                            if j == 0:
                                pe.wait_ge(s_e, 9)
                            g, kind = divmod(j, 3)
                            for a in range(4):
                                hd = 2 * a + g
                                ins = mm(gp[(9 + j) % 2][:, a * 128:(a + 1) * 128], kt((1, 2, 1)[kind], hd), kt((1, 2, 0)[kind], hd))
                            ins.then_inc(s_g, 1)

                @block.scalar
                def _(act):
                    for n, (g, l, k) in enumerate(slots):
                        if solve and l < SQ:
                            nuB, _, nuC, _ = later(k, l + 1)
                            act.wait_ge(s_S[k], SQ * g + l + 1)
                            for h in range(2):
                                nc.scalar.activation(nuB[HALF[h], :, HALF[h]], pS[k][HALF[h]], ACT.Copy).then_inc(s_ac[k], 1)
                            if l < SQ - 1:
                                nc.scalar.activation(nuC[:], pS[k][:], ACT.Copy).then_inc(s_ac[k], 1)
                        if not prep:
                            continue
                        if n in PROJ_READ:
                            j = PROJ_READ[n]
                            act.wait_ge(s_g, j + 1)
                            if j == 0:
                                nc.scalar.activation(sb_[:].rearrange("p h a -> p (h a)"), gp[0][:, 0:2 * FH],
                                                     ACT.Sigmoid).then_inc(s_e, 1)
                            else:
                                nc.scalar.activation(QK[:, j - 1, :], gp[j % 2][:], ACT.Copy).then_inc(s_e, 1)
                            if j == 5:
                                nc.scalar.activation(sb_[:], sb_[:], ACT.Sqrt).then_inc(s_be, 1)
                        if n == EXP_AT:
                            act.wait_ge(s_sh, 1)
                            nc.scalar.activation(QK[:, 0:3, :], QK[:, 0:3, :], ACT.Exp).then_inc(s_ex, 1)
                        if n in PACK_AT:
                            gg, kind = divmod(PACK_AT[n], 3)
                            act.wait_ge(s_m, 5 * gg + 2 * kind + 1)
                            nuB, _, nuC, _ = first(kind, gg)
                            for h in range(2):
                                nc.scalar.activation(nuC[HALF[h]], nuB[HALF[h], :, HALF[h]], ACT.Copy).then_inc(s_pa, 1)
                        if n in TURN_READ:
                            j = TURN_READ[n]
                            act.wait_ge(s_g, 7 + j)
                            nc.scalar.activation(KT[:, 4 * j:4 * j + 4, :], gp[j % 2][:].rearrange("p (a s) -> p a s", a=4),
                                                 ACT.Copy).then_inc(s_e, 1)

                    if prep:
                        act.wait_ge(s_pa, 8)

                qk = QK[:, 0:3, :].rearrange("p k (h d) -> p (k h) d", d=FD)
                wide_of = lambda t: t[:].unsqueeze(2).to_broadcast([128, 3 * FH, FD])

                @block.gpsimd
                def _(pool):
                    if not prep:
                        return
                    pool.wait_ge(s_mx, 1)
                    nc.gpsimd.tensor_tensor(qk, qk, wide_of(mx), ALU.subtract).then_inc(s_sh, 1)
                    pool.wait_ge(s_sm, 1)
                    nc.gpsimd.tensor_tensor(qk, qk, wide_of(sm), ALU.mult).then_inc(s_k, 1)
                    for n, (g, k) in enumerate(((0, 0), (0, 1), (1, 0), (1, 1))):
                        pool.wait_ge(s_m, 2 * (n + 1) + g)
                        nuB, nlB, nuC, nlU = first(k, g)
                        for h in range(2):
                            nc.gpsimd.tensor_copy(nlU[HALF[h], :, 0, :], nlB[HALF[h], :, HALF[h]]).then_inc(s_pk, 1)
                    pool.wait_ge(s_pk, 8)

                @block.vector
                def _(dve):
                    own = Chain(dve, s_own)
                    if prep:
                        V.tensor_copy(xc[:].rearrange("p a s -> p s a"), X[:, :, bass.ds(2 * new, 2)]).then_inc(s_x, 1)
                    for n, (g, l, k) in enumerate(slots):
                        if solve:
                            now = first(k, g) if l == 0 else later(k, min(l, SQ))
                            u = now[3][:, :, 1, :]
                            dve.wait_ge(s_R[k], (LV + 1 - k) * g + l + 1)
                            if l < SQ:
                                _, nlB, _, nlU = later(k, l + 1)
                                V.tensor_tensor(nlU[:, :, 1, :], u, pR[k][l % 2][:, :, 1, :],
                                                ALU.subtract if l == 0 else ALU.add).then_inc(s_dv[k], 1)
                                if l < SQ - 1:
                                    V.tensor_copy(nlU[:, :, 0, :], pR[k][l % 2][:, :, 0, :]).then_inc(s_dv[k], 1)
                                    for h in range(2):
                                        V.tensor_copy(nlB[HALF[h], :, HALF[h]], pR[k][l % 2][HALF[h], :, 0, :]).then_inc(s_dv[k], 1)
                            else:
                                if k and l == LV - 1 and g == 0 and done is not None:
                                    dve.wait_ge(s_out, 32)
                                o = Uf[:, :, g, :] if k and l == LV - 1 else P[k][:]
                                V.tensor_tensor(o, u, pR[k][l % 2][:, :, 1, :], ALU.add).then_inc(s_dv[k], 1)
                            if l == LV - 1 and k == 1:
                                dve.wait_ge(s_R[0], (LV + 1) * (g + 1))
                                V.tensor_copy(Z[:, :, g, :], pR[0][LV % 2][:, :, 1, :]).then_inc(s_z, 1)
                        if not prep:
                            continue
                        if n == MAX_AT:
                            dve.wait_ge(s_e, 4)
                            V.tensor_reduce(mx[:], qk, AX.X, ALU.max).then_inc(s_mx, 1)
                        if n in VAL_AT:
                            vk, vg = VAL_AT[n]
                            dve.wait_ge(s_e, 6)
                            dve.wait_ge(s_be, 1)
                            vv = QK[:, 3 + vk, :].rearrange("p (a g d) -> p g a d", a=4, g=2)[:, vg]
                            be = sb_[:, :, vk].rearrange("p (a g) -> p g a", g=2)[:, vg].unsqueeze(2)
                            V.tensor_tensor(first(vk, vg)[3][:, :, 1, :], vv, be.to_broadcast([128, 4, FD]),
                                            ALU.mult).then_inc(s_v, 1)
                        if n == SUM_AT:
                            dve.wait_ge(s_ex, 1)
                            own(V.tensor_reduce(sm[:], qk, AX.X, ALU.add))
                            own(V.reciprocal(sm[:], sm[:]))
                            for kk in range(2):
                                r = slice((1 + kk) * FH, (2 + kk) * FH)
                                V.tensor_tensor(sm[:, r], sm[:, r], sb_[:, :, kk], ALU.mult).then_inc(s_own, 1)
                            own.n += 2
                            dve.wait_ge(s_own, own.n)
                            V.tensor_copy(sm[:, 0:1], sm[:, 0:1]).then_inc(s_sm, 1)
                        if n in MASK_AT:
                            j = MASK_AT[n]
                            gg, kind = divmod(j, 3)
                            dve.wait_ge(s_g, 10 + j)
                            G = gp[(9 + j) % 2][:].rearrange("p (a s) -> p a s", a=4)
                            bc = lambda m: m[:, None, :].to_broadcast([128, 4, 128])
                            if kind < 2:
                                V.tensor_tensor(first(kind, gg)[0][:], G, bc(maskU), ALU.mult).then_inc(s_m, 1)
                                V.tensor_tensor(first(kind, gg)[1][:], G, bc(maskL), ALU.mult).then_inc(s_m, 1)
                            else:
                                V.tensor_tensor(az[gg][:], G, bc(maskZ), ALU.mult).then_inc(s_m, 1)

                @block.sync
                def _(sp):
                    rows = lambda t, j: t.rearrange("(n a) s d -> n (a s) d", a=2)[j]
                    flat = lambda t: t[:].rearrange("p a g d -> p (a g d)")
                    if done is not None:
                        sp.dma_start(rows(ur, done), flat(Uf)).then_inc(s_out, 16)
                        sp.dma_start(rows(zz, done), flat(Z)).then_inc(s_out, 16)
                    if prep:
                        sp.wait_ge(s_k, 1)
                        sp.dma_start(rows(kr, new), QK[:, 2, :]).then_inc(s_out2, 16)
                        sp.wait_ge(s_out2, 16)
                    if done is not None:
                        sp.wait_ge(s_out, 32)

        with st.step() as block:
            @block.sync
            def _(sp):
                xv = xT.rearrange("p (b t) -> p b t", b=B)
                for k in range(8):
                    sp.dma_start(X[:, 8 * k:8 * k + 8, :], xv[:, 8 * k:8 * k + 8, :]).then_inc(s_w, 16)
                sp.dma_start(W[:], wslow[:, :]).then_inc(s_w, 16)
                sp.wait_ge(s_w, 16 * 9)

            @block.vector
            def _(dve):
                for n in range(4, 8):
                    for t in lvl[n][0:2]:
                        V.memset(t[:], 0.0).then_inc(s_dv[0], 1)
                dve.wait_ge(s_dv[0], 8)

            @block.gpsimd
            def _(pool):
                own = Chain(pool, s_own)
                own(nc.gpsimd.memset(maskZ[:], 1.0))
                own(nc.gpsimd.memset(maskZ[0:64, 64:128], 0.0))
                own(nc.gpsimd.memset(maskZ[64:128, 0:64], 0.0))
                own(nc.gpsimd.affine_select(out=maskU[:], in_=maskZ[:], compare_op=ALU.is_gt, fill=0.0, base=0,
                                            pattern=[[1, 128]], channel_multiplier=-1))
                own(nc.gpsimd.affine_select(out=maskL[:], in_=maskZ[:], compare_op=ALU.is_gt, fill=0.0, base=0,
                                            pattern=[[-1, 128]], channel_multiplier=1))
                own(nc.gpsimd.affine_select(out=maskZ[:], in_=maskZ[:], compare_op=ALU.is_ge, fill=0.0, base=0,
                                            pattern=[[1, 128]], channel_multiplier=-1))

        NP = T // 2
        step_of(0, None, None)
        step_of(1, 0, None)
        with nc.Fori(0, NP - 2) as i:
            step_of(i + 2, i + 1, i)
        step_of(None, NP - 1, NP - 2)
        step_of(None, None, NP - 1)


def recur_stage(nc, c, kr, ur, zz, hs):
    SC = 16
    NL = SL // SC
    PC = 256 // FD
    shares = []
    for t in range(SL):
        n = t + 1
        m = n if n < 2 * PC else min(n, PC * round(0.7 * n / PC))
        shares.append((n, m, m if m <= PC else PC * ((m // PC + 1) // 2)))
    pooled = [n > m for n, m, _ in shares]
    p_upto = [sum(pooled[:t + 1]) for t in range(SL)]
    v_upto = [sum(2 if m > k else 1 for n, m, k in shares[:t + 1]) for t in range(SL)]
    with Stage(nc, "recur") as st:
        K = [st.sb(f"K{a}", [HT, SL, FD]) for a in range(2)]
        U = [st.sb(f"U{a}", [HT, SL, FD]) for a in range(2)]
        Hh = [st.sb(f"H{a}", [HT, SL, FD]) for a in range(2)]
        pr = [st.sb(f"pr{a}", [HT, SL * FD]) for a in range(2)]
        acc = [st.ps(f"acc{a}", [HT, PC * FD]) for a in range(2)]
        e = [st.sb(f"e{a}", [HT, FD]) for a in range(2)]
        w = [st.sb(f"w{a}", [HT, SL]) for a in range(2)]
        sm = [st.sb(f"sm{a}", [HT, FD]) for a in range(2)]
        mx = [st.sb(f"mx{a}", [HT, 1]) for a in range(2)]
        rs = [st.sb(f"rs{a}", [HT, 1]) for a in range(2)]
        s_in = [st.sem(f"loaded{k}") for k in range(NL)]
        s_own = [st.sem(f"own{a}") for a in range(2)]
        s_kp = [st.sem(f"pool_keys{a}") for a in range(2)]
        s_dot = [st.sem(f"dots{a}") for a in range(2)]
        s_v = [st.sem(f"values{a}") for a in range(2)]
        s_vp = [st.sem(f"pool_values{a}") for a in range(2)]
        s_sum = [st.sem(f"summed{a}") for a in range(2)]
        s_mx = [st.sem(f"max{a}") for a in range(2)]
        s_ex = [st.sem(f"exp{a}") for a in range(2)]
        s_out = st.sem("stored")
        V, P = nc.vector, nc.gpsimd
        view = lambda t: t.rearrange("(c p) s (h d) -> c h p s d", c=2, h=FH)
        rows = lambda a, lo, hi: pr[a][:, lo * FD:hi * FD].rearrange("p (s d) -> p s d", d=FD)

        def keys(eng, a, lo, hi):
            return eng.tensor_tensor(rows(a, lo, hi), K[a][:, lo:hi, :],
                                     e[a][:, None, :].to_broadcast([HT, hi - lo, FD]), ALU.mult)

        def values(eng, a, lo, hi):
            return eng.tensor_tensor(rows(a, lo, hi), U[a][:, lo:hi, :],
                                     w[a][:, lo:hi].unsqueeze(2).to_broadcast([HT, hi - lo, FD]), ALU.mult)

        with nc.Fori(0, FH) as i, st.step() as block:
            @block.sync
            def _(sp):
                for k in range(NL):
                    r = slice(k * SC, (k + 1) * SC)
                    for a in range(2):
                        for src, dst in ((kr, K), (ur, U), (zz, Hh)):
                            sp.dma_start(dst[a][:, r, :], view(src)[a, i][:, r, :]).then_inc(s_in[k], 16)
                for k in range(NL):
                    r = slice(k * SC, (k + 1) * SC)
                    for a in range(2):
                        sp.wait_ge(s_mx[a], (k + 1) * SC)
                        sp.dma_start(hs.rearrange("s (c p) (h d) -> c h p s d", c=2, h=FH)[a, i][:, r, :],
                                     Hh[a][:, r, :]).then_inc(s_out, 16)
                sp.wait_ge(s_out, 32 * NL)

            @block.scalar
            def _(act):
                for t in range(1, SL):
                    for a in range(2):
                        act.wait_ge(s_mx[a], t)
                        nc.scalar.activation(e[a][:], Hh[a][:, t - 1, :], ACT.Exp, bias=mx[a][:, 0:1],
                                             accum_out=rs[a][:, 0:1]).then_inc(s_ex[a], 1)

            @block.gpsimd
            def _(pool):
                for t in range(SL):
                    n, m, _ = shares[t]
                    if not pooled[t]:
                        continue
                    if t % SC == 0 or not pooled[t - 1]:
                        pool.wait_ge(s_in[t // SC], 96)
                    for a in range(2):
                        pool.wait_ge(s_ex[a], t)
                        keys(P, a, m, n).then_inc(s_kp[a], 1)
                        pool.wait_ge(s_dot[a], t + 1)
                        values(P, a, m, n).then_inc(s_vp[a], 1)

            @block.tensor
            def _(pe):
                for t in range(SL):
                    n, m, k = shares[t]
                    for a in range(2):
                        for lo, hi in ((0, k), (k, m), (m, n)):
                            if lo == hi:
                                continue
                            if hi == n and pooled[t]:
                                pe.wait_ge(s_vp[a], p_upto[t])
                            else:
                                pe.wait_ge(s_v[a], v_upto[t] - (1 if hi < m else 0))
                            for s in range(lo, hi, PC):
                                q = min(s + PC, hi)
                                ins = nc.tensor.matmul(acc[a][:, 0:(q - s) * FD], c.ident[0:HT, 0:HT],
                                                       pr[a][:, s * FD:q * FD], start=(s == 0), stop=(q == n))
                        ins.then_inc(s_sum[a], 1)

            @block.vector
            def _(dve):
                own = [Chain(dve, s_own[a]) for a in range(2)]

                def dots(a, t):
                    n, m, _ = shares[t]
                    if t:
                        dve.wait_ge(s_ex[a], t)
                    keys(V, a, 0, m).then_inc(s_own[a], 1)
                    V.reciprocal(rs[a][:], rs[a][:]).then_inc(s_own[a], 1)
                    own[a].n += 2
                    dve.wait_ge(s_own[a], own[a].n)
                    if pooled[t]:
                        dve.wait_ge(s_kp[a], p_upto[t])
                    V.tensor_reduce(w[a][:, 0:n], rows(a, 0, n), AX.X, ALU.add).then_inc(s_dot[a], 1)

                def turn(a, t, b, r):
                    n, m, k = shares[t] if a is not None else (0, 0, 0)
                    if r >= 0:
                        q = min(r + 1, PC)
                        dve.wait_ge(s_sum[b], r + 1)
                        V.tensor_reduce(sm[b][:], acc[b][:, 0:q * FD].rearrange("p (s d) -> p d s", d=FD),
                                        AX.X, ALU.add).then_inc(s_own[b], 1)
                        own[b].n += 1
                    if a is not None:
                        dve.wait_ge(s_dot[a], t + 1)
                        values(V, a, 0, k).then_inc(s_v[a], 1)
                    if r >= 0:
                        dve.wait_ge(s_own[b], own[b].n)
                        own[b](V.scalar_tensor_tensor(Hh[b][:, r, :], sm[b][:], rs[b][:, 0:1], Hh[b][:, r, :], ALU.mult, ALU.add))
                        V.tensor_reduce(mx[b][:], Hh[b][:, r, :], AX.X, ALU.max, negate=True).then_inc(s_mx[b], 1)
                    if m > k:
                        values(V, a, k, m).then_inc(s_v[a], 1)

                for a in range(2):
                    own[a](V.memset(e[a][:], 1.0))
                    own[a](V.memset(rs[a][:], float(FD)))
                for t in range(SL):
                    if t % SC == 0:
                        dve.wait_ge(s_in[t // SC], 96)
                    dots(0, t)
                    turn(0, t, 1, t - 1)
                    dots(1, t)
                    turn(1, t, 0, t)
                turn(None, SL, 1, SL - 1)


def delta_out_stage(nc, c, hs, wout, xn, h, h_out):
    NQ = 4
    with Stage(nc, "dout") as st:
        wo = st.sb("wo", [128, 4, D])
        t = [st.sb(f"t{q}", [HT, 2, KW]) for q in range(NQ)]
        tT = [st.sb(f"tT{q}", [128, 2, 4, HT]) for q in range(2)]
        hb = [st.sb(f"hb{q}", [HT, 2, D]) for q in range(NQ)]
        xb = [st.sb(f"xb{q}", [HT, 2, D]) for q in range(NQ)]
        tp = [st.ps(f"tp{i}", [128, 4, 128]) for i in range(4)]
        yp = [st.ps(f"yp{i}", [HT, 2, D]) for i in range(2)]
        s_w = st.sem("weights")
        s_in = [st.sem(f"loaded{q}") for q in range(NQ)]
        s_h = [st.sem(f"h_loaded{q}") for q in range(NQ)]
        s_tp = st.sem("transposed")
        s_cp = st.sem("copied")
        s_mm = st.sem("multiplied")
        s_hx = st.sem("input_added")
        s_y = st.sem("y_ready")
        s_out = st.sem("stored")
        with st.step() as block:
            @block.sync
            def _(sp):
                sp.dma_start(wo[:], wout[:, :, :]).then_inc(s_w, 16)
                sp.wait_ge(s_w, 16)
        with nc.Fori(0, B // NQ) as b, st.step() as block:
            @block.sync
            def _(sp):
                for q in range(NQ):
                    sp.dma_start(t[q][:], hs.rearrange("s (c p) d -> s p c d", c=2)[b * NQ + q]).then_inc(s_in[q], 16)
                    sp.dma_start(hb[q][:], tiles_of(h)[b * NQ + q]).then_inc(s_h[q], 16)
                    sp.dma_start(xb[q][:], tiles_of(xn)[b * NQ + q]).then_inc(s_h[q], 16)
                for q in range(NQ):
                    sp.wait_ge(s_y, q + 1)
                    sp.dma_start(tiles_of(h_out)[b * NQ + q], hb[q][:]).then_inc(s_out, 16)
                sp.wait_ge(s_out, 16 * NQ)

            @block.tensor
            def _(pe):
                def turn(q):
                    pe.wait_ge(s_in[q], 16)
                    for k in range(2):
                        if q >= 2:
                            pe.wait_ge(s_cp, 2 * (q - 2) + k + 1)
                        for m in range(4):
                            ins = nc.tensor.transpose(tp[2 * (q % 2) + k][:, m, 0:HT], t[q][:, k, m * 128:(m + 1) * 128],
                                                      c.ident[0:HT, 0:HT])
                        ins.then_inc(s_tp, 1)

                turn(0)
                for q in range(NQ):
                    if q + 1 < NQ:
                        turn(q + 1)
                    if q >= 2:
                        pe.wait_ge(s_y, q - 1)
                    for k in range(2):
                        pe.wait_ge(s_cp, 2 * q + k + 1)
                        for m in range(4):
                            ins = nc.tensor.matmul(yp[q % 2][:, k, :], tT[q % 2][:, k, m, :], wo[:, m, :], start=(m == 0), stop=(m == 3))
                    ins.then_inc(s_mm, 1)

            @block.scalar
            def _(act):
                for q in range(NQ):
                    if q >= 2:
                        act.wait_ge(s_mm, q - 1)
                    for k in range(2):
                        act.wait_ge(s_tp, 2 * q + k + 1)
                        nc.scalar.activation(tT[q % 2][:, k], tp[2 * (q % 2) + k][:, :, 0:HT], ACT.Copy).then_inc(s_cp, 1)

            @block.vector
            def _(dve):
                def inputs(q):
                    dve.wait_ge(s_h[q], 32)
                    nc.vector.tensor_tensor(hb[q][:], hb[q][:], xb[q][:], ALU.add).then_inc(s_hx, 1)

                inputs(0)
                for q in range(NQ):
                    if q + 1 < NQ:
                        inputs(q + 1)
                    dve.wait_ge(s_hx, q + 1)
                    dve.wait_ge(s_mm, q + 1)
                    nc.vector.tensor_tensor(hb[q][:], hb[q][:], yp[q % 2][:], ALU.add).then_inc(s_y, 1)


CE = 8
CK = 2 * T // CE
CF = 256
CS = 64
RG = B * CE // 128


def choice_stage(nc, c, xn, xnT, Wg, W1, b1, W2, b2, h, h_out):
    with Stage(nc, "choice") as st:
        L = st.sb("L", [HT, 2, B, CE])
        PO = st.sb("PO", [HT, 2, B, CE])
        wg = st.sb("wg", [D, CE])
        xt = st.sb("xt", [D, CT * HT])
        red = st.sb("red", [HT, 2, NT])
        PT = st.sb("PT", [128, RG, T])
        t1 = st.sb("t1", [128, RG, T])
        t2 = st.sb("t2", [128, RG, T])
        one = st.sb("one", [128, T])
        tau = st.sb("tau", [128, RG])
        cand = st.sb("cand", [128, RG])
        bit = st.sb("bit", [128, RG], I32)
        cnt = st.sb("cnt", [128, RG])
        w1 = st.sb("w1", [D, CE, CF])
        w2 = st.sb("w2", [128, CE, 2, D])
        bu = st.sb("bu", [128, CE, 2])
        bd = st.sb("bd", [128, CE // 2, D])
        ios = st.sb("ios", [HT, CS])
        x = st.sb("x", [HT, 2, 2, D])
        hb = st.sb("hb", [HT, 2, 2, D])
        P = [st.sb(f"P{i}", [HT, 2, CE, CS]) for i in range(2)]
        PG = [st.sb(f"PG{i}", [HT, 2, CE, CS]) for i in range(2)]
        PGT = [st.sb(f"PGT{i}", [128, 2, CE // 2, HT]) for i in range(2)]
        xg = st.sb("xg", [D, CE, 2, CS])
        a = st.sb("a", [128, CE, 2, 2, CS])
        Y = [st.sb(f"Y{i}", [128, CE // 2, D]) for i in range(2)]
        gp = [st.ps(f"gp{i}", [128, 512]) for i in range(2)]
        tp = [st.ps(f"tp{i}", [128, 4, 128]) for i in range(2)]
        up = [st.ps(f"up{i}", [128, 2, 2, CS]) for i in range(2)]
        s_in = st.sem("loaded")
        s_own = st.sem("own")
        s_po = st.sem("pool_own")
        s_mm = st.sem("multiplied")
        s_act = st.sem("act")
        s_x = st.sem("ready")
        s_P = st.sem("onehot_ready")
        s_g = st.sem("product_done")
        s_e = st.sem("product_read")
        s_tp = st.sem("transposed")
        s_pt = st.sem("scatter_ready")
        s_up = st.sem("up_done")
        s_a = st.sem("act_done")
        s_h = st.sem("h_loaded")
        s_out = st.sem("stored")
        V = nc.vector
        with st.step() as block:
            @block.sync
            def _(sp):
                sp.dma_start(wg[:], Wg[:, :]).then_inc(s_in, 16)
                sp.dma_start(w1[:], W1.rearrange("e d f -> d e f")).then_inc(s_in, 16)
                for k in range(2):
                    sp.dma_start(w2[:, :, k, :], W2[:, k * 128:(k + 1) * 128, :].rearrange("e f d -> f e d")).then_inc(s_in, 16)
                    sp.dma_start(bu[:, :, k], b1[:, k * 128:(k + 1) * 128].rearrange("e f -> f e"),
                                 allow_slow_non_contiguous=True).then_inc(s_in, 16)
                    sp.dma_start(bd[k * CS:(k + 1) * CS, :, :], bass.AP(b2.tensor, k * D, [[0, CS], [2 * D, CE // 2], [1, D]])).then_inc(s_in, 16)
                sp.wait_ge(s_in, 16 * 8)

            @block.vector
            def _(dve):
                own = Chain(dve, s_own)
                own(V.memset(tau[:], 0.0))
                own(V.memset(one[:], 1.0))
                own(V.memset(bit[:], 1 << 29))

            @block.gpsimd
            def _(pool):
                nc.gpsimd.iota(ios[:], pattern=[[1, CS]], base=0, channel_multiplier=0,
                               allow_small_or_imprecise_dtypes=True).then_inc(s_po, 1)
                pool.wait_ge(s_po, 1)

        with nc.Fori(0, NT // CT) as i, st.step() as block:
            @block.sync
            def _(sp):
                sp.dma_start(xt[:], xnT[:, bass.ds(i * (CT * HT), CT * HT)]).then_inc(s_in, 16)

            @block.tensor
            def _(pe):
                pe.wait_ge(s_in, 16)
                for k in range(CT):
                    nc.tensor.matmul(gp[0][0:HT, k * CE:(k + 1) * CE], xt[:, k * HT:(k + 1) * HT], wg[:], start=True,
                                     stop=True).then_inc(s_mm, 1)

            @block.vector
            def _(dve):
                dve.wait_ge(s_mm, CT)
                V.tensor_copy(L[:, :, bass.ds(i * NBI, NBI), :], gp[0][0:HT, 0:CT * CE].rearrange("p (b c e) -> p c b e", c=2, e=CE)).then_inc(s_x, 1)
                dve.wait_ge(s_x, 1)

        with st.step() as block:
            @block.vector
            def _(dve):
                own = Chain(dve, s_own)
                Lf = L[:].rearrange("p c b e -> p (c b) e")
                rb = lambda k: red[:, k, :].unsqueeze(2).to_broadcast([HT, NT, CE])
                own(V.tensor_reduce(red[:, 0, :], Lf, AX.X, ALU.max))
                V.tensor_tensor(Lf, Lf, rb(0), ALU.subtract).then_inc(s_x, 1)
                dve.wait_ge(s_act, 1)
                own(V.tensor_reduce(red[:, 1, :], Lf, AX.X, ALU.add))
                own(V.reciprocal(red[:, 1, :], red[:, 1, :]))
                V.tensor_tensor(Lf, Lf, rb(1), ALU.mult).then_inc(s_x, 1)
                for k in range(2):
                    dve.wait_ge(s_mm, 4 * k + 4)
                    V.tensor_copy(PT[:, 2 * k:2 * k + 2, :].rearrange("p r (c t) -> p r c t", c=2),
                                  tp[k][:].rearrange("p (r c) t -> p r c t", r=2)[:, :, :, 0:HT]).then_inc(s_x, 1)
                dve.wait_ge(s_x, 4)

            @block.scalar
            def _(act):
                act.wait_ge(s_x, 1)
                nc.scalar.activation(L[:], L[:], ACT.Exp).then_inc(s_act, 1)

            @block.tensor
            def _(pe):
                pe.wait_ge(s_x, 2)
                for r in range(RG):
                    for k in range(2):
                        m = 2 * r + k
                        nc.tensor.transpose(tp[m // 4][:, m % 4, 0:HT], L[:, k, 16 * r:16 * r + 16, :].rearrange("p b e -> p (b e)"), c.ident[0:HT, 0:HT]).then_inc(s_mm, 1)

        full = [128, RG, T]
        with nc.Fori(0, 30) as i, st.step() as block:
            @block.vector
            def _(dve):
                own = Chain(dve, s_own)
                own(V.tensor_tensor(cand[:].bitcast(I32), tau[:].bitcast(I32), bit[:], ALU.bitwise_or))
                own(V.tensor_scalar(bit[:], bit[:], 1, None, ALU.logical_shift_right))
                own(V.tensor_tensor(t1[:], PT[:], cand[:].unsqueeze(2).to_broadcast(full), ALU.is_ge))
                own(V.tensor_reduce(cnt[:], t1[:], AX.X, ALU.add))
                own(V.scalar_tensor_tensor(cand[:], cnt[:], float(CK), cand[:], ALU.is_ge, ALU.mult))
                own(V.tensor_tensor(tau[:], tau[:], cand[:], ALU.max))

        with st.step() as block:
            @block.vector
            def _(dve):
                own = Chain(dve, s_own)
                tb = tau[:].unsqueeze(2).to_broadcast(full)
                own(V.tensor_tensor(t1[:], PT[:], tb, ALU.is_gt))
                own(V.tensor_tensor(t2[:], PT[:], tb, ALU.is_equal))
                own(V.tensor_reduce(cnt[:], t1[:], AX.X, ALU.add))
                own(V.tensor_scalar(cnt[:], cnt[:], -1.0, float(CK), ALU.mult, ALU.add))
                for r in range(RG):
                    own(V.tensor_tensor_scan(PT[:, r, :], one[:], t2[:, r, :], 0.0, ALU.mult, ALU.add))
                own(V.tensor_tensor(PT[:], PT[:], cnt[:].unsqueeze(2).to_broadcast(full), ALU.is_le))
                own(V.tensor_tensor(t2[:], t2[:], PT[:], ALU.mult))
                own(V.tensor_tensor(t1[:], t1[:], t2[:], ALU.add))
                for r in range(RG):
                    own(V.tensor_tensor_scan(PT[:, r, :], one[:], t1[:, r, :], 0.0, ALU.mult, ALU.add))
                own(V.tensor_tensor(PT[:], PT[:], t1[:], ALU.mult))
                V.tensor_scalar(PT[:], PT[:], -1.0, None, ALU.add).then_inc(s_x, 1)
                for k in range(2):
                    dve.wait_ge(s_mm, 4 * k + 4)
                    for m in range(4):
                        r, cc = divmod(4 * k + m, 2)
                        V.tensor_copy(PO[:, cc, 16 * r:16 * r + 16, :], tp[k][0:HT, m, :].rearrange("p (b e) -> p b e", e=CE)).then_inc(s_x, 1)
                dve.wait_ge(s_x, 9)

            @block.tensor
            def _(pe):
                pe.wait_ge(s_x, 1)
                for m in range(8):
                    r, cc = divmod(m, 2)
                    nc.tensor.transpose(tp[m // 4][0:HT, m % 4, :], PT[:, r, cc * HT:(cc + 1) * HT], c.ident[:]).then_inc(s_mm, 1)

        xv, hv, ov = tiles_of(xn), tiles_of(h), tiles_of(h_out)
        with nc.Fori(0, B // 2) as i, st.step() as block:
            @block.sync
            def _(sp):
                for k in range(2):
                    sp.dma_start(x[:, k], xv[2 * i + k]).then_inc(s_in, 16)
                for k in range(2):
                    sp.dma_start(hb[:, k], hv[2 * i + k]).then_inc(s_h, 16)
                for k in range(2):
                    sp.wait_ge(s_x, k + 1)
                    sp.dma_start(ov[2 * i + k], hb[:, k]).then_inc(s_out, 16)
                sp.wait_ge(s_out, 32)

            @block.gpsimd
            def _(pool):
                pool.wait_ge(s_P, 1)
                for k in range(2):
                    pool.wait_ge(s_P, k + 1)
                    for cc in range(2):
                        nc.gpsimd.tensor_tensor(PG[k][:, cc], P[k][:, cc],
                                                L[:, cc, bass.ds(2 * i + k, 1), :].rearrange("p b e -> p (b e)").unsqueeze(2).to_broadcast([HT, CE, CS]),
                                                ALU.mult).then_inc(s_po, 1)

            @block.tensor
            def _(pe):
                pe.wait_ge(s_in, 32)
                for k in range(2):
                    pe.wait_ge(s_P, k + 1)
                    for cc in range(2):
                        ins = nc.tensor.matmul(gp[k][:], x[:, k, cc, :], P[k][:, cc].rearrange("p e s -> p (e s)"),
                                               start=(cc == 0), stop=(cc == 1))
                    ins.then_inc(s_g, 1)
                for k in range(2):
                    for cc in range(2):
                        if k:
                            pe.wait_ge(s_pt, cc + 1)
                        for m in range(4):
                            pe.wait_ge(s_po, 2 * k + cc + 1)
                            ins = nc.tensor.transpose(tp[cc][:, m, 0:HT], PG[k][:, cc, 2 * m:2 * m + 2, :].rearrange("p e s -> p (e s)"),
                                                      c.ident[0:HT, 0:HT])
                        ins.then_inc(s_tp, 1)
                pe.wait_ge(s_e, 2)
                for e in range(CE):
                    if e >= 2:
                        pe.wait_ge(s_a, 2 * (e - 1))
                    for f in range(2):
                        ins = nc.tensor.matmul(up[e % 2][:, f].rearrange("p b s -> p (b s)"), w1[:, e, f * 128:(f + 1) * 128],
                                               xg[:, e].rearrange("p b s -> p (b s)"), start=True, stop=True)
                    ins.then_inc(s_up, 1)
                pe.wait_ge(s_a, 2 * CE)
                for k in range(2):
                    for e in range(CE):
                        o = gp[k][CS * (e % 2):CS * (e % 2) + CS, (e // 2) * D:(e // 2 + 1) * D]
                        for f in range(2):
                            ins = nc.tensor.matmul(o, a[:, e, f, k, :], w2[:, e, f, :], start=(f == 0), stop=(f == 1))
                    ins.then_inc(s_g, 1)
                for k in range(2):
                    pe.wait_ge(s_e, 3 + k)
                    pe.wait_ge(s_pt, 2 * k + 2)
                    for cc in range(2):
                        for m in range(CE // 2):
                            ins = nc.tensor.matmul(up[k][0:HT].rearrange("p f b s -> p (f b s)")[:, cc * D:(cc + 1) * D],
                                                   PGT[k][:, cc, m, :], Y[k][:, m, :], start=(m == 0), stop=(m == CE // 2 - 1))
                    ins.then_inc(s_mm, 1)

            @block.vector
            def _(dve):
                for k in range(2):
                    for cc in range(2):
                        ins = V.tensor_tensor(P[k][:, cc], PO[:, cc, bass.ds(2 * i + k, 1)].rearrange("p b e -> p (b e)").unsqueeze(2).to_broadcast([HT, CE, CS]),
                                              ios[:, None, :].to_broadcast([HT, CE, CS]), ALU.is_equal)
                    ins.then_inc(s_P, 1)
                for k in range(2):
                    dve.wait_ge(s_g, k + 1)
                    V.tensor_copy(xg[:, :, k, :], gp[k][:].rearrange("p (e s) -> p e s", e=CE)).then_inc(s_e, 1)
                for k in range(2):
                    dve.wait_ge(s_g, 3 + k)
                    V.tensor_tensor(Y[k][:].rearrange("p m d -> p (m d)"), gp[k][:], bd[:].rearrange("p m d -> p (m d)"), ALU.add).then_inc(s_e, 1)
                dve.wait_ge(s_h, 32)
                for k in range(2):
                    dve.wait_ge(s_mm, k + 1)
                    hf = hb[:, k].rearrange("p c d -> p (c d)")
                    V.tensor_tensor(hf, hf, up[k][0:HT].rearrange("p f b s -> p (f b s)"), ALU.add).then_inc(s_x, 1)

            @block.scalar
            def _(act):
                for k in range(2):
                    for cc in range(2):
                        act.wait_ge(s_tp, 2 * k + cc + 1)
                        nc.scalar.activation(PGT[k][:, cc], tp[cc][:, :, 0:HT], ACT.Copy).then_inc(s_pt, 1)
                for e in range(CE):
                    act.wait_ge(s_up, e + 1)
                    for f in range(2):
                        nc.scalar.activation(a[:, e, f].rearrange("p b s -> p (b s)"), up[e % 2][:, f].rearrange("p b s -> p (b s)"),
                                             ACT.Gelu, bias=bu[:, e, f:f + 1]).then_inc(s_a, 1)


RP = 2 * T - 1
WB = T + HT - 1


def position_stage(nc, c, pos, Wp, bp, pT):
    with Stage(nc, "pos") as st:
        e = st.sb("e", [HT, 4, D])
        eT = st.sb("eT", [D, 4, HT])
        w = st.sb("w", [D, D])
        b = st.sb("b", [D, 1])
        o = st.sb("o", [D, 4 * HT])
        tp = st.ps("tp", [D, 4, 128])
        op = st.ps("op", [D, 4 * HT])
        s_in = st.sem("loaded")
        s_pe = st.sem("pe")
        s_x = st.sem("ready")
        s_out = st.sem("stored")
        with st.step() as block:
            @block.sync
            def _(sp):
                sp.dma_start(e[:], pos[0, 0:4 * HT, :].rearrange("(a p) d -> p a d", a=4)).then_inc(s_in, 16)
                sp.dma_start(w[:], Wp[:, :]).then_inc(s_in, 16)
                sp.dma_start(b[:], bp.rearrange("(p a) -> p a", a=1)).then_inc(s_in, 16)
                sp.wait_ge(s_x, 2)
                sp.dma_start(pT[:, :], o[:]).then_inc(s_out, 16)
                sp.wait_ge(s_out, 16)

            @block.tensor
            def _(pe):
                pe.wait_ge(s_in, 48)
                for k in range(4):
                    ins = nc.tensor.transpose(tp[:, k, 0:HT], e[:, k, :], c.ident[0:HT, 0:HT])
                ins.then_inc(s_pe, 1)
                pe.wait_ge(s_x, 1)
                nc.tensor.matmul(op[:], w[:], eT[:].rearrange("p a t -> p (a t)"), start=True, stop=True).then_inc(s_pe, 1)

            @block.vector
            def _(dve):
                dve.wait_ge(s_pe, 1)
                nc.vector.tensor_copy(eT[:], tp[:, :, 0:HT]).then_inc(s_x, 1)
                dve.wait_ge(s_pe, 2)
                nc.vector.tensor_scalar(o[:], op[:], b[:, 0:1], None, ALU.add).then_inc(s_x, 1)


def relative_stage(nc, c, xnT, pT, Wq, bq, Wk, bk, Wv, bv, Wo, bo, pu, pv_, scr, h, h_out):
    SCALE = HD ** -0.5
    with Stage(nc, "rel") as st:
        w = st.sb("w", [D, 4, D])
        cols = st.sb("cols", [D, 5])
        br = st.sb("br", [1, 2, D])
        hm = st.sb("hm", [D, NH])
        ones = st.sb("ones", [1, HT])
        pt = st.sb("pt", [D, RP + 1])
        x = st.sb("x", [D, 2, T])
        hb = st.sb("hb", [HT, 2, 2, D])
        QU = [st.sb(f"QU{k}", [D, NH, T]) for k in range(2)]
        QV = st.sb("QV", [D, NH, T])
        KT = [st.sb(f"KT{k}", [D, T]) for k in range(2)]
        Vt = [st.sb(f"V{k}", [HT, 2, D]) for k in range(2)]
        BD = [st.sb(f"BD{f}", [HT, NH, WB]) for f in range(2)]
        sc = [[st.sb(f"sc{k}{f}", [HT, NH, T]) for f in range(2)] for k in range(2)]
        PT = st.sb("PT", [HT, NH, 2, HT])
        mx = st.sb("mx", [HT, 2, 2, NH])
        rs = st.sb("rs", [HT, 2, 2, NH])
        ri = st.sb("ri", [HT, 2, 2, NH])
        o = [st.sb(f"o{k}", [HT, 2, D]) for k in range(2)]
        oT = [st.sb(f"oT{k}", [D, 2, HT]) for k in range(2)]
        scp = st.ps("scp", [HT, 4, 512])
        gp = [st.ps(f"gp{i}", [128, 512]) for i in range(2)]
        ap = [st.ps(f"ap{i}", [128, 4, 128]) for i in range(2)]
        s_w = st.sem("weights")
        s_own = st.sem("own")
        s_po = st.sem("pool_own")
        s_in = st.sem("loaded")
        s_hb = st.sem("h_loaded")
        s_g = st.sem("product_done")
        s_e = st.sem("product_read")
        s_ag = st.sem("act_product_done")
        s_ae = st.sem("act_product_read")
        s_qv = st.sem("qv_ready")
        s_bw = [st.sem(f"positions_stored{f}") for f in range(2)]
        s_bd = [st.sem(f"positions_back{m}") for m in range(4)]
        s_sc = st.sem("scores_done")
        s_sr = st.sem("scores_read")
        s_mx = st.sem("max_ready")
        s_ex = st.sem("exp_done")
        s_y = st.sem("h_ready")
        s_out = st.sem("stored")
        V = nc.vector
        with st.step() as block:
            @block.sync
            def _(sp):
                for k, m in enumerate((Wq, Wk, Wv, Wo)):
                    sp.dma_start(w[:, k, :], m[:, :]).then_inc(s_w, 16)
                for k, v in enumerate((bq, bk)):
                    sp.dma_start(cols[:, k:k + 1], v.rearrange("(p a) -> p a", a=1)).then_inc(s_w, 16)
                for k, v in enumerate((pu, pv_)):
                    sp.dma_start(cols[:, 2 + k:3 + k], bass.AP(v.tensor, 0, [[1, D], [1, 1]])).then_inc(s_w, 16)
                for k, v in enumerate((bv, bo)):
                    sp.dma_start(br[:, k, :], v.rearrange("(a d) -> a d", a=1)).then_inc(s_w, 16)
                sp.dma_start(pt[:], pT[:, :]).then_inc(s_w, 16)
                sp.wait_ge(s_w, 16 * 11)

            @block.gpsimd
            def _(pool):
                own = Chain(pool, s_po)
                head_masks(pool, nc, own, hm)

            @block.vector
            def _(dve):
                own = Chain(dve, s_own)
                own(V.memset(ones[:], 1.0))
                dve.wait_ge(s_w, 16 * 11)
                own(V.tensor_tensor(cols[:, 2:3], cols[:, 2:3], cols[:, 0:1], ALU.add))
                own(V.tensor_tensor(cols[:, 3:4], cols[:, 3:4], cols[:, 0:1], ALU.add))

        NB = 2 * NH
        NTR = 2 * NH // 4 * 2
        hv, ov = tiles_of(h), tiles_of(h_out)
        with nc.Fori(0, B // 2) as i, st.step() as block:
            @block.sync
            def _(sp):
                sp.dma_start(x[:].rearrange("p a t -> p (a t)"), xnT[:, bass.ds(i * (2 * T), 2 * T)]).then_inc(s_in, 16)
                for k in range(2):
                    for f in range(2):
                        m = 2 * k + f
                        sp.wait_ge(s_ae, NH * (m + 1))
                        sp.dma_start(scr[m], BD[f][:]).then_inc(s_bw[f], 16)
                        sp.wait_ge(s_bw[f], 16 * (k + 1))
                        sp.dma_start(sc[k][f][:], bass.AP(scr.tensor, m * HT * NH * WB + HT - 1, [[NH * WB - 1, HT], [WB, NH], [1, T]])).then_inc(s_bd[m], 16)
                for k in range(2):
                    sp.dma_start(hb[:, k], hv[2 * i + k]).then_inc(s_hb, 16)
                for k in range(2):
                    sp.wait_ge(s_y, k + 1)
                    sp.dma_start(ov[2 * i + k], hb[:, k]).then_inc(s_out, 16)
                sp.wait_ge(s_out, 32)

            @block.tensor
            def _(pe):
                n = [0, 0]

                def mm(o_, l, r, first=True, last=True):
                    return nc.tensor.matmul(o_, l, r, start=first, stop=last)

                def job(fn):
                    m = n[0]
                    if m >= 2:
                        pe.wait_ge(s_e, m - 1)
                    fn(gp[m % 2]).then_inc(s_g, 1)
                    n[0] += 1

                def ajob(fn):
                    m = n[1]
                    if m >= 2:
                        pe.wait_ge(s_ae, m - 1)
                    fn(ap[m % 2]).then_inc(s_ag, 1)
                    n[1] += 1

                pe.wait_ge(s_in, 16)
                for k in range(2):
                    xk = x[:, k, :]
                    job(lambda p: mm(p[:, 0:T], w[:, 0, :], xk))
                    job(lambda p: mm(p[:, 0:T], w[:, 1, :], xk))

                    def values(p):
                        for cc in range(2):
                            mm(p[0:HT, cc * D:(cc + 1) * D], x[:, k, cc * HT:(cc + 1) * HT], w[:, 2, :], True, False)
                            ins = mm(p[0:HT, cc * D:(cc + 1) * D], ones[:], br[:, 0, :], False, True)
                        return ins
                    job(values)
                    pe.wait_ge(s_qv, 2 * k + 2)
                    for f in range(2):
                        for hd in range(NH):
                            ajob(lambda p: mm(p[0:HT].rearrange("p a t -> p (a t)")[:, 0:WB], QV[:, hd, f * HT:(f + 1) * HT],
                                              pt[:, (1 - f) * HT:(1 - f) * HT + WB]))
                def finish(k):
                    def turn_out(p):
                        pe.wait_ge(s_e, n[0])
                        for cc in range(2):
                            ins = nc.tensor.transpose(p[:, cc * 128:cc * 128 + HT], o[k][:, cc, :], c.ident[0:HT, 0:HT])
                        return ins
                    job(turn_out)

                    def outs(p):
                        pe.wait_ge(s_e, n[0])
                        for cc in range(2):
                            mm(p[0:HT, cc * D:(cc + 1) * D], oT[k][:, cc, :], w[:, 3, :], True, False)
                            ins = mm(p[0:HT, cc * D:(cc + 1) * D], ones[:], br[:, 1, :], False, True)
                        return ins
                    job(outs)

                def scores(m):
                    k, f = divmod(m, 2)
                    if m:
                        pe.wait_ge(s_sr, m)
                    for hd in range(NH):
                        ins = mm(scp[:, hd // 2, (hd % 2) * T:(hd % 2 + 1) * T], QU[k][:, hd, f * HT:(f + 1) * HT], KT[k][:])
                    ins.then_inc(s_sc, 1)

                pe.wait_ge(s_e, 6)
                scores(0)
                for k in range(2):
                    for f in range(2):
                        m = 2 * k + f
                        if m < 3:
                            scores(m + 1)
                        if m == 2:
                            finish(0)
                        for g in range(4):
                            def turn(p):
                                for r in range(4):
                                    hd, sh = divmod(4 * g + r, 2)
                                    pe.wait_ge(s_ex, m * NH + hd + 1)
                                    ins = nc.tensor.transpose(p[0:HT, r, 0:HT], sc[k][f][:, hd, sh * HT:(sh + 1) * HT], c.ident[0:HT, 0:HT])
                                return ins
                            ajob(turn)

                        def pv(p):
                            pe.wait_ge(s_ae, 2 * NB + 4 * (m + 1))
                            for hd in range(NH):
                                for sh in range(2):
                                    ins = mm(p[0:HT, hd * HD:(hd + 1) * HD], PT[:, hd, sh, :], Vt[k][:, sh, hd * HD:(hd + 1) * HD],
                                             sh == 0, sh == 1)
                            return ins
                        job(pv)
                finish(1)

            @block.vector
            def _(dve):
                own = Chain(dve, s_own)
                n = [0]

                def read(fn):
                    n[0] += 1
                    dve.wait_ge(s_g, n[0])
                    fn(gp[(n[0] - 1) % 2]).then_inc(s_e, 1)

                full = [D, NH, T]
                for k in range(2):
                    def queries(p):
                        mask = hm[:].unsqueeze(2).to_broadcast(full)
                        src = p[:, None, 0:T].to_broadcast(full)
                        if k:
                            dve.wait_ge(s_ag, NB)
                        V.scalar_tensor_tensor(QV[:], src, cols[:, 3:4], mask, ALU.add, ALU.mult).then_inc(s_qv, 1)
                        return V.scalar_tensor_tensor(QU[k][:], src, cols[:, 2:3], mask, ALU.add, ALU.mult)
                    read(queries)
                    V.engine_nop().then_inc(s_qv, 1)
                    read(lambda p: V.tensor_scalar(KT[k][:], p[:, 0:T], cols[:, 1:2], None, ALU.add))
                    read(lambda p: V.tensor_copy(Vt[k][:].rearrange("p a d -> p (a d)"), p[0:HT, 0:2 * D]))
                def heads(k, f):
                    def fn(p):
                        own(V.reciprocal(ri[:, k, f, :], rs[:, k, f, :]))
                        return V.tensor_tensor(o[k][:, f, :].rearrange("p (h d) -> p h d", h=NH),
                                               p[0:HT, 0:D].rearrange("p (h d) -> p h d", h=NH),
                                               ri[:, k, f, :].unsqueeze(2).to_broadcast([HT, NH, HD]), ALU.mult)
                    read(fn)

                def finish(k):
                    read(lambda p: V.tensor_copy(oT[k][:], p[:, 0:256].rearrange("p (a t) -> p a t", a=2)[:, :, 0:HT]))
                    dve.wait_ge(s_hb, 32)
                    hf = hb[:, k].rearrange("p c d -> p (c d)")
                    read(lambda p: V.tensor_tensor(hf, hf, p[0:HT, 0:256], ALU.add))
                    V.engine_nop().then_inc(s_y, 1)

                for k in range(2):
                    for f in range(2):
                        m = 2 * k + f
                        dve.wait_ge(s_sc, m + 1)
                        dve.wait_ge(s_bd[m], 16)
                        sv = sc[k][f][:].rearrange("p (a b) s -> p a (b s)", b=2)
                        V.tensor_tensor(sv, sv, scp[:, :, 0:2 * T], ALU.add).then_inc(s_sr, 1)
                        dve.wait_ge(s_sr, m + 1)
                        own(V.tensor_reduce(mx[:, k, f, :], sc[k][f][:], AX.X, ALU.max))
                        V.tensor_scalar(mx[:, k, f, :], mx[:, k, f, :], -SCALE, None, ALU.mult).then_inc(s_mx, 1)
                        if m:
                            heads(*divmod(m - 1, 2))
                        if m == 2:
                            finish(0)
                heads(1, 1)
                finish(1)

            @block.scalar
            def _(act):
                n = [0]

                def read(fn):
                    n[0] += 1
                    act.wait_ge(s_ag, n[0])
                    fn(ap[(n[0] - 1) % 2]).then_inc(s_ae, 1)

                for k in range(2):
                    for f in range(2):
                        if k:
                            act.wait_ge(s_bw[f], 16)
                        for hd in range(NH):
                            read(lambda p: nc.scalar.activation(BD[f][:, hd, :], p[0:HT].rearrange("p a t -> p (a t)")[:, 0:WB], ACT.Copy))
                for k in range(2):
                    for f in range(2):
                        m = 2 * k + f
                        act.wait_ge(s_mx, m + 1)
                        for hd in range(NH):
                            nc.scalar.activation(sc[k][f][:, hd, :], sc[k][f][:, hd, :], ACT.Exp, bias=mx[:, k, f, hd:hd + 1], scale=SCALE,
                                                 accum_out=rs[:, k, f, hd:hd + 1]).then_inc(s_ex, 1)
                        if m:
                            act.wait_ge(s_g, 6 + m + (2 if k and f else 0))
                        for g in range(4):
                            read(lambda p: nc.scalar.activation(PT[:, 2 * g:2 * g + 2].rearrange("p a s t -> p (a s) t"), p[0:HT, :, 0:HT], ACT.Copy))


def last_stage(nc, c, xnT, Wg, bg, We, be, h, out):
    E = 16
    with Stage(nc, "last") as st:
        xa = st.sb("xa", [D, B, T])
        m = st.sb("m", [D, B])
        wg = st.sb("wg", [D, E])
        bgb = st.sb("bgb", [B, E])
        z = st.sb("z", [B, E])
        red = st.sb("red", [B, 4])
        ie = st.sb("ie", [B, E])
        pid = st.sb("pid", [128, 1])
        wide2 = st.sb("wide2", [B, 2, 128])
        gate = st.sb("gate", [128, B])
        rows = st.sb("rows", [128, 2, B], U32)
        cur = st.sb("cur", [128, 2, 4], U32)
        hb = st.sb("hb", [HT, 4, 2, D])
        x = st.sb("x", [D, 4, T])
        ws = st.sb("ws", [D, 4, D])
        bs = st.sb("bs", [D, 4, D])
        y = st.sb("y", [HT, 4, 2, D])
        p = [st.ps(f"p{i}", [128, 512]) for i in range(4)]
        s_in = st.sem("loaded")
        s_own = st.sem("own")
        s_po = st.sem("pool_own")
        s_mm = st.sem("multiplied")
        s_x = st.sem("ready")
        s_act = st.sem("act")
        s_g = [st.pool_sem(f"gathered{k}") for k in range(4)]
        s_h = st.sem("h_loaded")
        s_out = st.sem("stored")
        V = nc.vector
        with st.step() as block:
            @block.sync
            def _(sp):
                sp.dma_start(wg[:], Wg[:, :]).then_inc(s_in, 16)
                sp.dma_start(bgb[:], wide(bg, B)).then_inc(s_in, 16)
                xv = xnT.rearrange("p (b t) -> p b t", b=B)
                for k in range(8):
                    sp.dma_start(xa[:, 8 * k:8 * k + 8, :], xv[:, 8 * k:8 * k + 8, :]).then_inc(s_in, 16)
                sp.wait_ge(s_in, 160)

            @block.gpsimd
            def _(pool):
                P = nc.gpsimd
                own = Chain(pool, s_po)
                own(P.iota(ie[:], pattern=[[1, E]], base=0, channel_multiplier=0, allow_small_or_imprecise_dtypes=True))
                own(P.iota(pid[:], pattern=[[0, 1]], base=0, channel_multiplier=1, allow_small_or_imprecise_dtypes=True))

            @block.tensor
            def _(pe):
                pe.wait_ge(s_x, 1)
                nc.tensor.matmul(p[0][0:B, 0:E], m[:], wg[:], start=True, stop=True).then_inc(s_mm, 1)
                pe.wait_ge(s_x, 3)
                for k in range(2):
                    ins = nc.tensor.matmul(p[1][:, k * B:(k + 1) * B], wide2[:, k, :], c.ident[0:B, 0:B], start=True, stop=True)
                ins.then_inc(s_mm, 1)

            @block.scalar
            def _(act):
                act.wait_ge(s_x, 2)
                nc.scalar.activation(z[:], z[:], ACT.Exp).then_inc(s_act, 1)

            @block.vector
            def _(dve):
                own = Chain(dve, s_own)
                dve.wait_ge(s_in, 160)
                own(V.tensor_reduce(m[:], xa[:], AX.X, ALU.add))
                V.tensor_scalar(m[:], m[:], 1.0 / T, None, ALU.mult).then_inc(s_x, 1)
                dve.wait_ge(s_mm, 1)
                own(V.tensor_tensor(z[:], p[0][0:B, 0:E], bgb[:], ALU.add))
                own(V.tensor_reduce(red[:, 0:1], z[:], AX.X, ALU.max))
                V.tensor_scalar(z[:], z[:], red[:, 0:1], None, ALU.subtract).then_inc(s_x, 1)
                dve.wait_ge(s_act, 1)
                dve.wait_ge(s_po, 2)
                own(V.tensor_reduce(red[:, 1:2], z[:], AX.X, ALU.add))
                own(V.reciprocal(red[:, 1:2], red[:, 1:2]))
                own(V.tensor_scalar(z[:], z[:], red[:, 1:2], None, ALU.mult))
                own(V.tensor_reduce(red[:, 2:3], z[:], AX.X, ALU.max))
                own(V.tensor_scalar(z[:], z[:], red[:, 2:3], float(-E), ALU.is_equal, ALU.mult))
                own(V.tensor_tensor(z[:], z[:], ie[:], ALU.add))
                own(V.tensor_reduce(red[:, 3:4], z[:], AX.X, ALU.min))
                own(V.tensor_scalar(red[:, 3:4], red[:, 3:4], float(E), None, ALU.add))
                own(V.tensor_copy(wide2[:, 0, :], red[:, 2:3].to_broadcast([B, 128])))
                V.tensor_copy(wide2[:, 1, :], red[:, 3:4].to_broadcast([B, 128])).then_inc(s_x, 1)
                dve.wait_ge(s_mm, 2)
                own(V.tensor_copy(gate[:], p[1][:, 0:B]))
                own(V.tensor_scalar(rows[:, 0, :], p[1][:, B:2 * B], float(D), pid[:, 0:1], ALU.mult, ALU.add))
                own(V.tensor_copy(rows[:, 1, :], p[1][:, B:2 * B]))

        wrows = We.rearrange("e d o -> (e d) o")
        with nc.Fori(0, B // 4) as i, st.step() as block:
            @block.vector
            def _(dve):
                V.tensor_copy(cur[:], rows[:, :, bass.ds(4 * i, 4)]).then_inc(s_x, 1)
                dve.wait_ge(s_h, 64)
                for k in range(4):
                    dve.wait_ge(s_mm, k + 1)
                    yk = y[:, k]
                    V.tensor_tensor(yk, p[k][0:HT, 0:256].rearrange("p (a d) -> p a d", a=2),
                                    bs[0:HT, k, None, :].to_broadcast([HT, 2, D]), ALU.add).then_inc(s_act, 1)
                    dve.wait_ge(s_act, k + 1)
                    V.scalar_tensor_tensor(hb[:, k], yk, gate[0:HT, bass.ds(4 * i + k, 1)], hb[:, k], ALU.mult, ALU.add).then_inc(s_x, 1)

            @block.gpsimd
            def _(pool):
                pool.wait_ge(s_x, 1)
                for k in range(4):
                    nc.gpsimd.indirect_dma_start(ws[:, k, :], None, wrows, bass.IndirectOffsetOnAxis(ap=cur[:, 0, k:k + 1], axis=0)).then_inc(s_g[k], 16)
                    nc.gpsimd.indirect_dma_start(bs[:, k, :], None, be[:, :], bass.IndirectOffsetOnAxis(ap=cur[:, 1, k:k + 1], axis=0)).then_inc(s_g[k], 16)

            @block.sync
            def _(sp):
                sp.dma_start(x[:].rearrange("p a t -> p (a t)"), xnT[:, bass.ds(i * (4 * T), 4 * T)]).then_inc(s_in, 16)
                for k in range(4):
                    sp.dma_start(hb[:, k], tiles_of(h)[4 * i + k]).then_inc(s_h, 16)
                for k in range(4):
                    sp.wait_ge(s_x, k + 2)
                    sp.dma_start(out.rearrange("b (c p) d -> b p c d", c=2)[4 * i + k], hb[:, k]).then_inc(s_out, 16)
                sp.wait_ge(s_out, 64)

            @block.tensor
            def _(pe):
                pe.wait_ge(s_in, 16)
                for k in range(4):
                    pe.wait_ge(s_g[k], 32)
                    for a in range(2):
                        ins = nc.tensor.matmul(p[k][0:HT, a * D:(a + 1) * D], x[:, k, a * HT:(a + 1) * HT], ws[:, k, :], start=True, stop=True)
                    ins.then_inc(s_mm, 1)


def build_audio_tower(nc, a, out):
    scratch = lambda name, *shape, dt=F32: nc.dram_tensor(name, list(shape), dt).ap()
    hA, hB = scratch("hA", N, D), scratch("hB", N, D)
    xn = scratch("xn", N, D)
    xnT, xn2T = scratch("xnT", D, N), scratch("xn2T", D, N)
    kpad = scratch("kpad", D, KP)
    wt1 = scratch("wt1", 11, D, D)
    liqT, wgt = scratch("liqT", D, N), scratch("wgt", B, 3)
    wslow, wout = scratch("wslow", D, PROJ), scratch("wout", D, 4, D)
    kr, ur, zz = (scratch(n, T, SL, KW) for n in ("kr", "ur", "zz"))
    hs = scratch("hs", SL, T, KW)
    pT, scr = scratch("pT", D, RP + 1), scratch("scr", 4, HT, NH, WB)
    of = lambda layer: (lambda *names: [a[f"{layer}_{n}"] for n in names])

    with Stage(nc, "const") as st:
        class c:
            ident = st.sb("ident", [128, 128])
        consts_stage(nc, st, c.ident)

        tok_stage(nc, c, a["x"], *of("L0_tok")("W", "b", "gamma", "beta"), hA)

        ln_stage(nc, c, "ln0", hA, xn, None)
        s4_kernel_stage(nc, c, *of("L0_attn")("Lambda_re", "Lambda_im", "P", "B", "C", "D", "log_step"),
                        a["s4_cos"], a["s4_sin"], a["s4_dft_re"], a["s4_dft_im"], kpad)
        s4_conv_stage(nc, c, xn, kpad, hA, hB)

        ln_stage(nc, c, "ln1", hB, xn, xnT)
        g = of("L0_ffn")
        E, cap = 32, N // 32
        xp, idx = scratch("xp0", N, D + E), scratch("idx0", HT, E, cap // HT, dt=U32)
        route_stage(nc, c, "route0", E, cap, xn, xnT, *g("W_router", "b_router"), xp, idx)
        experts_stage(nc, c, "experts0", E, cap, a["L0_ffn_W_up"].shape[2], 4, ACT.Silu, xp, idx,
                      *g("W_up", "b_up", "W_down", "b_down"), hB)

        ln_stage(nc, c, "ln2", hB, None, xnT)
        g = of("L1_attn")
        turn_weights_stage(nc, c, "turn1", g("li_Win", "li_Wrec", "li_Wout", "re_Wq", "re_Wk", "re_Wv", "re_Wo",
                                             "la_Wq", "la_Wk", "la_Wv", "la_Wo"), wt1)
        liquid_stage(nc, c, xnT, wt1, *g("li_tau", "li_b"), liqT)
        mix_weights_stage(nc, c, xnT, *g("rt_W1", "rt_b1", "rt_W2", "rt_b2", "fusion_w"), wgt)
        retention_stage(nc, c, xnT, liqT, wt1, g("re_gnw", "re_gnb", "re_bo", "la_bq", "la_bk", "la_bv", "la_bo",
                                                 "ln_w", "ln_b"), a["L1_attn_re_theta"], wgt, hB, hA)

        ln_stage(nc, c, "ln3", hA, xn, xnT)
        g = of("L1_ffn")
        E, cap = 16, N // 16
        xp, idx = scratch("xp1", N, D + E), scratch("idx1", HT, E, cap // HT, dt=U32)
        route_stage(nc, c, "route1", E, cap, xn, xnT, a["L1_ffn_gate_w"], None, xp, idx)
        shared_stage(nc, c, xnT, *g("sw1", "sb1", "sw2", "sb2"), hA, hB)
        experts_stage(nc, c, "experts1", E, cap, a["L1_ffn_w1"].shape[2], 1, ACT.Gelu_apprx_tanh, xp, idx,
                      *g("w1", "b1", "w2", "b2"), hB)

        ln_stage(nc, c, "ln4", hB, xn, None)
        ln_stage(nc, c, "ln5", xn, None, xn2T, *of("L2_attn")("ln_gamma", "ln_beta"))
        slow_weights_stage(nc, c, a["L2_attn_W_slow"], wslow, a["L2_attn_W_out"], wout)
        delta_stage(nc, c, xn2T, wslow, kr, ur, zz)
        recur_stage(nc, c, kr, ur, zz, hs)
        delta_out_stage(nc, c, hs, wout, xn, hB, hA)

        ln_stage(nc, c, "ln6", hA, xn, xnT)
        choice_stage(nc, c, xn, xnT, *of("L2_ffn")("Wg", "W1", "b1", "W2", "b2"), hA, hB)

        ln_stage(nc, c, "ln7", hB, None, xnT)
        g = of("L3_attn")
        position_stage(nc, c, *g("pos_emb", "Wp", "bp"), pT)
        relative_stage(nc, c, xnT, pT, *g("Wq", "bq", "Wk", "bk", "Wv", "bv", "Wo", "bo", "pos_bias_u", "pos_bias_v"),
                       scr, hB, hA)

        ln_stage(nc, c, "ln8", hA, None, xnT)
        last_stage(nc, c, xnT, *of("L3_ffn")("Wg", "bg", "We", "be"), hA, out)


def kernel(**inputs):
    import numpy as _np
    import concourse.bacc as _bacc
    from concourse import mybir as _mybir
    from concourse.bass_utils import run_bass_kernel_spmd as _run

    nc = _bacc.Bacc("TRN2", target_bir_lowering=False, num_devices=1)
    arrays, args = {}, {}
    for name, value in {**inputs, **s4_constants()}.items():
        v = _np.ascontiguousarray(value)
        arrays[f"in_{name}_dram"] = v
        args[name] = nc.dram_tensor(f"in_{name}_dram", v.shape, _mybir.dt.from_np(v.dtype), kind="ExternalInput").ap()
    out = nc.dram_tensor("out_0_dram", (B, T, D), _mybir.dt.float32, kind="ExternalOutput").ap()
    build_audio_tower(nc, args, out)
    r = _run(nc, [arrays], core_ids=[0])
    return r.results[0]["out_0_dram"]
```
